# Optimizing a Trainium2 kernel written in Bass

```python
import numpy as np
import jax
import jax.numpy as jnp

def _softmax(x, axis=-1):
    return jax.nn.softmax(x, axis=axis)

def _gelu(x):
    return jax.nn.gelu(x, approximate=True)

def _silu(x):
    return jax.nn.silu(x)

def _sigmoid(x):
    return jax.nn.sigmoid(x)

def _layernorm(x, axis=-1, eps=1e-05):
    m = jnp.mean(x, axis=axis, keepdims=True)
    v = jnp.var(x, axis=axis, keepdims=True)
    return (x - m) / jnp.sqrt(v + eps)

def _scatter_add(tgt, idx, src, axis=0):
    return tgt.at[idx].add(src)

def _segment_sum(src, seg, n):
    return jax.ops.segment_sum(src, seg, n)
kernel_name = 'mk_flamingo_gated_d2_seqx_r4_694884'

def setup_inputs(seed: int=0):
    np.random.seed(seed)
    _w = jnp.asarray

    def _rec_inputs():
        import jax
        import jax.numpy as jnp
        _rk = jax.random.key(seed)
        x = -0.0002928 + 1 * jax.random.normal(jax.random.fold_in(_rk, 1), (16, 100, 256), jnp.float32)
        _lenS = 100 - jax.random.randint(jax.random.fold_in(_rk, 7), (16,), 0, max(1, 100 // 4) + 1, jnp.int32)
        _lenS2 = 361 - jax.random.randint(jax.random.fold_in(_rk, 8), (16,), 0, max(1, 361 // 4) + 1, jnp.int32)
        _ctx_1024P = jax.random.normal(jax.random.fold_in(_rk, 11), (16, 16, 256), jnp.float32)
        _ctx_1024c = jax.random.dirichlet(jax.random.fold_in(_rk, 511), 0.3 * jnp.ones((16,), jnp.float32), (16, 361))
        _ctx_1024t = jnp.einsum('bsk,bkd->bsd', _ctx_1024c, _ctx_1024P)
        _ctx_1024t = _ctx_1024t * jax.lax.rsqrt(jnp.mean(jnp.square(_ctx_1024t)) + 1e-12) * 0.953939
        ctx_1024 = -1.39393e-06 + 0.999914 * (_ctx_1024t + 0.3 * jax.random.normal(jax.random.fold_in(_rk, 611), (16, 361, 256), jnp.float32))
        _validS = jnp.arange(100)[None, :] < _lenS[:, None]
        _validS2 = jnp.arange(361)[None, :] < _lenS2[:, None]
        _causal = jnp.tril(jnp.ones((100, 100), dtype=bool))
        mask_Bx1x1xS2_ik0 = jnp.where(jnp.broadcast_to(_validS2[:, None, None, :], (16, 1, 1, 361)), 0, 1).astype(jnp.int32)
        mask_BxSxS2_bf0 = jnp.logical_not(jnp.ones((16, 100, 361), dtype=bool))
        _g = jax.random.normal(jax.random.fold_in(_rk, 9001), (2, 2), jnp.float32)
        _g = jnp.sign(_g) * jnp.maximum(jnp.abs(_g), 1.0) + (_g == 0) * 1.0
        g_xattn = _g[0]
        g_ffn = _g[1]
        return (x, ctx_1024, mask_Bx1x1xS2_ik0, mask_BxSxS2_bf0, g_xattn, g_ffn)
    x, ctx_1024, mask_Bx1x1xS2_ik0, mask_BxSxS2_bf0, g_xattn, g_ffn = _rec_inputs()

    def _L0_xattn_setup():
        import jax, jax.numpy as jnp
        import numpy as np
        B, S, D, H = (2, 512, 256, 16)
        DK = D // H
        key = jax.random.key(seed)
        ks = jax.random.split(key, 12)
        s = 1.0 / np.sqrt(D)
        return {'query': jax.random.normal(ks[0], (B, S, D), dtype=jnp.float32), 'key': jax.random.normal(ks[1], (B, S, D), dtype=jnp.float32), 'value': jax.random.normal(ks[2], (B, S, D), dtype=jnp.float32), 'mask': jax.random.randint(ks[3], (B, 1, 1, S), 0, 2, dtype=jnp.int32), 'wq': jax.random.normal(ks[4], (D, D), dtype=jnp.float32) * s, 'bq': jnp.zeros((D,), dtype=jnp.float32), 'wk': jax.random.normal(ks[5], (D, D), dtype=jnp.float32) * s, 'bk': jnp.zeros((D,), dtype=jnp.float32), 'wv': jax.random.normal(ks[6], (D, D), dtype=jnp.float32) * s, 'bv': jnp.zeros((D,), dtype=jnp.float32), 'wo': jax.random.normal(ks[7], (D, D), dtype=jnp.float32) * s, 'bo': jnp.zeros((D,), dtype=jnp.float32)}
    _L0_xattn_all = _L0_xattn_setup()
    _L0_xattn_in = {k: v for k, v in _L0_xattn_all.items() if k in ('wq', 'bq', 'wk', 'bk', 'wv', 'bv', 'wo', 'bo')}
    del _L0_xattn_all

    def _L0_ffn_setup():
        import jax, jax.numpy as jnp
        import numpy as np
        import math
        N_EXP = 8
        TOP_K = 2
        CAPACITY_FACTOR = 1.25

        def _capacity(num_tokens):
            cap = math.floor(TOP_K * CAPACITY_FACTOR * num_tokens / N_EXP)
            cap += cap % 2
            return int(cap)
        key = jax.random.key(seed)
        k1, k2, k3, k4 = jax.random.split(key, 4)
        B, C, d = (4, 256, 256)
        x = jax.random.normal(k1, (B, C, d), dtype=jnp.float32)
        w_g = jax.random.normal(k2, (d, N_EXP), dtype=jnp.float32) * 0.02
        c_fc = jax.random.normal(k3, (N_EXP, d, 4 * d), dtype=jnp.float32) * 0.02
        c_proj = jax.random.normal(k4, (N_EXP, 4 * d, d), dtype=jnp.float32) * 0.02
        return {'x': x, 'w_g': w_g, 'c_fc': c_fc, 'c_proj': c_proj}
    _L0_ffn_all = _L0_ffn_setup()
    _L0_ffn_in = {k: v for k, v in _L0_ffn_all.items() if k in ('w_g', 'c_fc', 'c_proj')}
    del _L0_ffn_all

    def _L1_xattn_setup():
        import jax, jax.numpy as jnp
        import numpy as np
        H, D, KD, VD = (16, 256, 64, 64)
        B, L = (8, 128)
        EPS = 0.001
        key = jax.random.key(seed)
        ks = jax.random.split(key, 10)
        q = jax.random.normal(ks[0], (B, L, D), dtype=jnp.float32)
        k = jax.random.normal(ks[1], (B, L, D), dtype=jnp.float32)
        v = jax.random.normal(ks[2], (B, L, D), dtype=jnp.float32)
        attention_mask = jnp.zeros((B, L, L), dtype=bool)

        def xav(k_, shape, fan_in, fan_out):
            std = float(np.sqrt(2.0 / (fan_in + fan_out)))
            return jax.random.normal(k_, shape, dtype=jnp.float32) * std
        w_qs = xav(ks[3], (H, D, KD), D, KD)
        w_ks = xav(ks[4], (H, D, KD), D, KD)
        w_vs = xav(ks[5], (H, D, VD), D, VD)
        W_o = xav(ks[6], (D, H * VD), H * VD, D)
        b_o = jnp.zeros((D,), dtype=jnp.float32)
        gamma = jnp.ones((D,), dtype=jnp.float32)
        beta = jnp.zeros((D,), dtype=jnp.float32)
        return {'q': q, 'k': k, 'v': v, 'attention_mask': attention_mask, 'w_qs': w_qs, 'w_ks': w_ks, 'w_vs': w_vs, 'W_o': W_o, 'b_o': b_o, 'gamma': gamma, 'beta': beta}
    _L1_xattn_all = _L1_xattn_setup()
    _L1_xattn_in = {k: v for k, v in _L1_xattn_all.items() if k in ('w_qs', 'w_ks', 'w_vs', 'W_o', 'b_o', 'gamma', 'beta')}
    del _L1_xattn_all

    def _L1_ffn_setup():
        import jax, jax.numpy as jnp
        import numpy as np
        NUM_EXPERTS = 8
        TOP_K = 2
        B, S, H, D = (4, 512, 256, 512)
        key = jax.random.key(seed)
        ks = jax.random.split(key, 8)
        return {'x': jax.random.normal(ks[0], (B, S, H), jnp.float32), 'router_w': jax.random.normal(ks[1], (H, NUM_EXPERTS), jnp.float32) * 0.02, 'router_b': jnp.zeros((NUM_EXPERTS,), jnp.float32), 'routing_weights': jax.random.normal(ks[2], (H, NUM_EXPERTS), jnp.float32) * 0.02, 'W1': jax.random.normal(ks[3], (NUM_EXPERTS, H, D), jnp.float32) * 0.02, 'b1': jnp.zeros((NUM_EXPERTS, D), jnp.float32), 'W2': jax.random.normal(ks[4], (NUM_EXPERTS, D, H), jnp.float32) * 0.02, 'b2': jnp.zeros((NUM_EXPERTS, H), jnp.float32)}
    _L1_ffn_all = _L1_ffn_setup()
    _L1_ffn_in = {k: v for k, v in _L1_ffn_all.items() if k in ('router_w', 'router_b', 'routing_weights', 'W1', 'b1', 'W2', 'b2')}
    del _L1_ffn_all
    return {'x': x, 'ctx_1024': ctx_1024, 'mask_Bx1x1xS2_ik0': mask_Bx1x1xS2_ik0, 'mask_BxSxS2_bf0': mask_BxSxS2_bf0, 'g_xattn': g_xattn, 'g_ffn': g_ffn, 'L0_xattn_wq': _L0_xattn_in['wq'], 'L0_xattn_bq': _L0_xattn_in['bq'], 'L0_xattn_wk': _L0_xattn_in['wk'], 'L0_xattn_bk': _L0_xattn_in['bk'], 'L0_xattn_wv': _L0_xattn_in['wv'], 'L0_xattn_bv': _L0_xattn_in['bv'], 'L0_xattn_wo': _L0_xattn_in['wo'], 'L0_xattn_bo': _L0_xattn_in['bo'], 'L0_ffn_w_g': _L0_ffn_in['w_g'], 'L0_ffn_c_fc': _L0_ffn_in['c_fc'], 'L0_ffn_c_proj': _L0_ffn_in['c_proj'], 'L1_xattn_w_qs': _L1_xattn_in['w_qs'], 'L1_xattn_w_ks': _L1_xattn_in['w_ks'], 'L1_xattn_w_vs': _L1_xattn_in['w_vs'], 'L1_xattn_W_o': _L1_xattn_in['W_o'], 'L1_xattn_b_o': _L1_xattn_in['b_o'], 'L1_xattn_gamma': _L1_xattn_in['gamma'], 'L1_xattn_beta': _L1_xattn_in['beta'], 'L1_ffn_router_w': _L1_ffn_in['router_w'], 'L1_ffn_router_b': _L1_ffn_in['router_b'], 'L1_ffn_routing_weights': _L1_ffn_in['routing_weights'], 'L1_ffn_W1': _L1_ffn_in['W1'], 'L1_ffn_b1': _L1_ffn_in['b1'], 'L1_ffn_W2': _L1_ffn_in['W2'], 'L1_ffn_b2': _L1_ffn_in['b2']}

def reference(x, ctx_1024, mask_Bx1x1xS2_ik0, mask_BxSxS2_bf0, g_xattn, g_ffn, L0_xattn_wq, L0_xattn_bq, L0_xattn_wk, L0_xattn_bk, L0_xattn_wv, L0_xattn_bv, L0_xattn_wo, L0_xattn_bo, L0_ffn_w_g, L0_ffn_c_fc, L0_ffn_c_proj, L1_xattn_w_qs, L1_xattn_w_ks, L1_xattn_w_vs, L1_xattn_W_o, L1_xattn_b_o, L1_xattn_gamma, L1_xattn_beta, L1_ffn_router_w, L1_ffn_router_b, L1_ffn_routing_weights, L1_ffn_W1, L1_ffn_b1, L1_ffn_W2, L1_ffn_b2):
    import jax
    import jax.numpy as jnp

    def _L0_xattn_ref(query, key, value, mask, wq, bq, wk, bk, wv, bv, wo, bo):
        import jax, jax.numpy as jnp
        import numpy as np
        B, S, D, H = (2, 512, 256, 16)
        DK = D // H
        b, s, d = query.shape

        def proj(x, w, bias):
            return (x @ w.T + bias).reshape(b, -1, H, DK).transpose(0, 2, 1, 3)
        q = proj(query, wq, bq)
        k = proj(key, wk, bk)
        v = proj(value, wv, bv)
        scores = jnp.einsum('bhqd,bhkd->bhqk', q, k) / jnp.sqrt(jnp.float32(DK))
        scores = jnp.where(mask == 0, jnp.float32(-1000000000.0), scores)
        attn = jax.nn.softmax(scores, axis=-1)
        x = jnp.einsum('bhqk,bhkd->bhqd', attn, v)
        x = x.transpose(0, 2, 1, 3).reshape(b, s, d)
        return x @ wo.T + bo

    def _L0_ffn_ref(x, w_g, c_fc, c_proj):
        import jax, jax.numpy as jnp
        import numpy as np
        import math
        N_EXP = 8
        TOP_K = 2
        CAPACITY_FACTOR = 1.25

        def _capacity(num_tokens):
            cap = math.floor(TOP_K * CAPACITY_FACTOR * num_tokens / N_EXP)
            cap += cap % 2
            return int(cap)
        B, C, d = x.shape
        T = B * C
        cap = _capacity(T)
        xt = x.reshape(T, d)
        logits = xt @ w_g
        top_v, top_i = jax.lax.top_k(logits, TOP_K)
        full = jnp.full_like(logits, -jnp.inf)
        full = full.at[jnp.arange(T)[:, None], top_i].set(top_v)
        probs = jax.nn.softmax(full, axis=-1)
        exp_mask = jax.nn.one_hot(top_i, N_EXP, dtype=jnp.int32)
        exp_mask = jnp.transpose(exp_mask, (1, 0, 2))
        exp_rank = jnp.cumsum(exp_mask.reshape(TOP_K * T, N_EXP), axis=0) - 1
        exp_rank = exp_rank.reshape(TOP_K, T, N_EXP)
        exp_mask = exp_mask * (exp_rank < cap).astype(jnp.int32)
        exp_rank = jnp.sum(exp_mask * exp_rank, axis=-1)
        exp_weights = exp_mask.astype(x.dtype) * probs[None]
        rank_oh = jax.nn.one_hot(exp_rank, cap, dtype=x.dtype)
        cb_weight = jnp.einsum('kte,ktc->tec', exp_weights, rank_oh)
        sec_mask = (cb_weight != 0).astype(x.dtype)
        exp_batches = jnp.einsum('tec,td->ecd', sec_mask, xt)
        h = jax.nn.gelu(jnp.einsum('ecd,edf->ecf', exp_batches, c_fc), approximate=False)
        exp_out = jnp.einsum('ecf,efd->ecd', h, c_proj)
        out = cb_weight.reshape(T, N_EXP * cap) @ exp_out.reshape(N_EXP * cap, d)
        return out.reshape(B, C, d)

    def _L1_xattn_ref(q, k, v, attention_mask, w_qs, w_ks, w_vs, W_o, b_o, gamma, beta):
        import jax, jax.numpy as jnp
        import numpy as np
        H, D, KD, VD = (16, 256, 64, 64)
        B, L = (8, 128)
        EPS = 0.001
        b, qlen, d = q.shape
        h, _, vd = w_vs.shape
        scale = jnp.asarray(np.sqrt(d), q.dtype)
        Q = jnp.einsum('bqd,hdk->hbqk', q, w_qs)
        K = jnp.einsum('bsd,hdk->hbsk', k, w_ks)
        V = jnp.einsum('bsd,hdv->hbsv', v, w_vs)
        scores = jnp.einsum('hbqk,hbsk->hbqs', Q, K) / scale
        scores = jnp.where(attention_mask[None, :, :, :], -jnp.inf, scores)
        attn = jax.nn.softmax(scores, axis=-1)
        out = jnp.einsum('hbqs,hbsv->hbqv', attn, V)
        cat = out.transpose(1, 2, 0, 3).reshape(b, qlen, h * vd)
        lin = cat @ W_o.T + b_o
        z = lin + q
        mu = jnp.mean(z, axis=-1, keepdims=True)
        sigma = jnp.std(z, axis=-1, keepdims=True, ddof=1)
        return (z - mu) / (sigma + EPS) * gamma + beta

    def _L1_ffn_ref(x, router_w, router_b, routing_weights, W1, b1, W2, b2):
        import jax, jax.numpy as jnp
        import numpy as np
        NUM_EXPERTS = 8
        TOP_K = 2
        B, S, H, D = (4, 512, 256, 512)
        b, s, h = x.shape
        xr = x.reshape(-1, h)
        _router_logits = xr @ router_w + router_b
        logits = xr @ routing_weights
        probs = jax.nn.softmax(logits, axis=-1)
        top_vals, top_idx = jax.lax.top_k(probs, TOP_K)
        gates = jnp.sum(jax.nn.one_hot(top_idx, NUM_EXPERTS, dtype=x.dtype) * top_vals[..., None], axis=1)
        hmid = jnp.einsum('th,ehd->etd', xr, W1) + b1[:, None, :]
        hmid = jax.nn.gelu(hmid)
        y = jnp.einsum('etd,edo->eto', hmid, W2) + b2[:, None, :]
        out = jnp.einsum('te,eto->to', gates, y)
        return out.reshape(b, s, -1)
    x = x + jnp.tanh(g_xattn[0]) * _L0_xattn_ref(_layernorm(x, axis=-1), ctx_1024, ctx_1024, mask_Bx1x1xS2_ik0, L0_xattn_wq, L0_xattn_bq, L0_xattn_wk, L0_xattn_bk, L0_xattn_wv, L0_xattn_bv, L0_xattn_wo, L0_xattn_bo)
    x = x + jnp.tanh(g_ffn[0]) * _L0_ffn_ref(_layernorm(x, axis=-1), L0_ffn_w_g, L0_ffn_c_fc, L0_ffn_c_proj)
    x = x + jnp.tanh(g_xattn[1]) * _L1_xattn_ref(_layernorm(x, axis=-1), ctx_1024, ctx_1024, mask_BxSxS2_bf0, L1_xattn_w_qs, L1_xattn_w_ks, L1_xattn_w_vs, L1_xattn_W_o, L1_xattn_b_o, L1_xattn_gamma, L1_xattn_beta)
    x = x + jnp.tanh(g_ffn[1]) * _L1_ffn_ref(_layernorm(x, axis=-1), L1_ffn_router_w, L1_ffn_router_b, L1_ffn_routing_weights, L1_ffn_W1, L1_ffn_b1, L1_ffn_W2, L1_ffn_b2)
    return x

_drawn_inputs = setup_inputs


def setup_inputs(seed=0):
    import zlib

    import numpy as np

    out = dict(_drawn_inputs(seed))
    spreads = {'g_ffn': (-1.0, 0.6),
     'L0_xattn_bq': (0.0, 0.612),
     'L0_xattn_bk': (0.0, 0.8),
     'L0_xattn_bv': (0.0, 0.1),
     'L0_xattn_bo': (0.0, 0.1),
     'L1_xattn_b_o': (0.0, 0.1),
     'L1_xattn_gamma': (1.0, 0.2),
     'L1_xattn_beta': (0.0, 0.1),
     'L1_ffn_router_b': (0.0, 0.1),
     'L1_ffn_b1': (0.0, 0.8),
     'L1_ffn_b2': (0.0, 0.285)}
    factors = {'L1_ffn_W1': 2.668}
    for name, (base, spread) in spreads.items():
        noise = np.random.default_rng([zlib.crc32(name.encode()), seed]).standard_normal(out[name].shape)
        drawn = base * np.exp(spread * noise) if base else spread * noise
        out[name] = jnp.asarray(drawn.astype(out[name].dtype))
    for name, factor in factors.items():
        out[name] = (out[name] * factor).astype(out[name].dtype)
    return out
```

```python
from contextlib import ExitStack

import concourse.bass as bass
from concourse import mybir

F32 = mybir.dt.float32
I32 = mybir.dt.int32
U32 = mybir.dt.uint32
U8 = mybir.dt.uint8
ALU = mybir.AluOpType
ACT = mybir.ActivationFunctionType
AX = mybir.AxisListType

P = 128
B, S, L, D = 16, 100, 361, 256
H = 16
E = 8
DK = D // P
PAIRS = B // 2
KTS = [(k, min(P, L - k)) for k in range(0, L, P)]
KT_N = len(KTS)
SLOTS = 512
CAP = 2 * 5 * B * S // (4 * E)
CAP += CAP % 2
TILES = 32
ROWS = TILES * P
DROP0 = ROWS
F0, F1 = 1024, 512
LN_EPS, Z_EPS = 1e-5, 1e-3
BIG = 3.0e38


class Counted:

    def __init__(self, nc, name, per, pre=0):
        self.sem, self.per, self.pre = nc.alloc_semaphore(name), per, pre

    def credit(self, eng):
        eng.sem_inc(self.sem, self.per)

    def before(self, k):
        return self.per + k

    def at(self, i, k):
        return self.per + self.pre + i * self.per + k


class Chain:

    def __init__(self, nc, name):
        self.sem, self.n = nc.alloc_semaphore(name), 0

    def mark(self, ins):
        self.n += 1
        ins.then_inc(self.sem, 1)
        return self.n

    def link(self, eng, ins):
        eng.wait_ge(self.sem, self.mark(ins))


class LoopChain:

    def __init__(self, nc, name, per):
        self.sem, self.per, self.n = nc.alloc_semaphore(name), per, 0

    def begin(self, i):
        self.i, self.n = i, 0

    def mark(self, ins):
        self.n += 1
        ins.then_inc(self.sem, 1)
        return self.i * self.per + self.n

    def link(self, eng, ins):
        eng.wait_ge(self.sem, self.mark(ins))

    def end(self):
        assert self.n == self.per, (self.n, self.per)


class Apart:

    def __init__(self, nc, name):
        self.sems = {eng.engine: nc.alloc_semaphore(f"{name}passed_{k}") for k, eng in
                     (("dve", nc.vector), ("pool", nc.gpsimd), ("sp", nc.sync))}

    def __call__(self, eng):
        eng.sem_inc(self.sems[eng.engine], 1)


class Layer:

    def __init__(self, n, dh, score_scale):
        self.n, self.dh, self.scale = n, dh, score_scale
        self.first = n == 0
        self.width = H * dh
        self.nt = self.width // P
        self.per_tile = P // dh
        self.v_cols = min(self.width, 512)
        self.v_parts = self.width // self.v_cols
        self.pv_rows = 32 if self.first else dh
        self.per_out = P // self.pv_rows
        self.out_tiles = H // self.per_out
        self.groups = self.out_tiles * S // 400


LT, LP = 3, 4
HEADS = 2 * H
N_SLOTS = HEADS + LP + 4
N_SB, N_PB, N_PT = 4, 4, 2


def schedule(layer, last):
    at = [[] for _ in range(N_SLOTS)]
    kv = [("K", t, 0) for t in range(layer.nt)]
    kv += [("V", t, p) for t in range(KT_N) for p in range(layer.v_parts)]
    first = [("Q", 0, t, 0) for t in range(layer.nt)]
    for n, (kind, t, p) in enumerate(kv):
        at[1 + n * (H - 2) // len(kv)].append((kind, 1, t, p))
    if not last:
        begin, end = H + LP + 1, HEADS + LP + 1
        for n, (kind, t, p) in enumerate(kv):
            at[begin + n * (end - begin) // len(kv)].append((kind, 0, t, p))
    for b in range(2):
        at[H * b + H - 1 + LP + 2].append(("W", b, 0, 0))
    units = first + [u for slot in at for u in slot]
    assert last or len(units) % 2 == 0
    owner, count = [], {"A": 0, "D": 0}
    for kind, b, t, p in units:
        if kind == "Q":
            eng = "AD"[t % 2]
        elif kind == "K":
            eng = "D" if layer.first or t % 2 else "A"
        elif kind == "V":
            eng = "AD"[(t + p) % 2] if layer.n else "A"
        else:
            eng = "D"
        count[eng] += 1
        owner.append((eng, count[eng]))
    index, slots = 0, []
    for slot in [first] + at:
        slots.append([(index + n, u) for n, u in enumerate(slot)])
        index += len(slot)
    return slots[0], slots[1:], owner, count, units


def attention(nc, layer, T, D_):
    n = layer.n
    nm = f"a{n}_"
    ctx = ExitStack()

    def sb(name, shape, dt=F32):
        return ctx.enter_context(nc.sbuf_tensor(nm + name, shape, dt))

    cx = [sb(f"context{s}", [P, DK, L]) for s in range(2)]
    kt = [sb(f"keys{s}", [P, layer.nt, L]) for s in range(2)]
    vt = [sb(f"values{s}", [P, KT_N, layer.width]) for s in range(2)]
    qm = sb("queries", [P, H, 2 * S])
    raw = [sb(f"mask_raw{s}", [P, L], I32 if n == 0 else U8) for s in range(2)]
    bias = [sb(f"mask_bias{s}", [P, L]) for s in range(2)]
    keep = [sb(f"mask_keep{s}", [P, L]) for s in range(2)] if n == 0 else None
    masked = sb("masked", [P, N_SB, L])
    low = sb("low", [P, N_SB])
    prob = sb("prob", [P, N_PB, L])
    total = sb("total", [P, N_PB])
    inv = sb("inv", [P, N_PB])
    pt = sb("prob_t", [P, N_PT, KT_N * S])
    ot = [sb(f"out_t{s}", [P, layer.out_tiles, S]) for s in range(2)]
    lin = sb("lin", [P, 2, D])
    ps_s = [ctx.enter_context(nc.psum_tensor(f"{nm}ps_s{k}", [P, 512], F32)) for k in range(2)]
    ps_t = [ctx.enter_context(nc.psum_tensor(f"{nm}ps_t{k}", [P, 512], F32)) for k in range(2)]
    ps_o = [ctx.enter_context(nc.psum_tensor(f"{nm}ps_o{k}", [P, 512], F32)) for k in range(2)]
    ps_p = [ctx.enter_context(nc.psum_tensor(f"{nm}ps_p{k}", [P, 512], F32)) for k in range(2)]

    full, lastly = schedule(layer, False), schedule(layer, True)
    n_units = len(full[4])
    pre_units = [("K", 0, t, 0) for t in range(layer.nt)]
    pre_units += [("V", 0, t, p) for t in range(KT_N) for p in range(layer.v_parts)]
    pre_owner, pre_count = [], {"A": 0, "D": 0}
    for kind, b, t, p in pre_units:
        eng = "D" if kind == "K" and n == 0 else "A"
        pre_count[eng] += 1
        pre_owner.append((eng, pre_count[eng]))

    groups = 2 * layer.groups
    scored = Counted(nc, nm + "scored", HEADS)
    maxed = Counted(nc, nm + "maxed", HEADS)
    exped = Counted(nc, nm + "exped", HEADS)
    inverted = Counted(nc, nm + "inverted", HEADS)
    normed = Counted(nc, nm + "normed", HEADS)
    turned = Counted(nc, nm + "turned", HEADS)
    pt_ready = Counted(nc, nm + "pt_ready", HEADS)
    valued = Counted(nc, nm + "valued", HEADS)
    out_ready = Counted(nc, nm + "out_ready", groups)
    unit_done = Counted(nc, nm + "unit_done", n_units, len(pre_units))
    taken = {"A": Counted(nc, nm + "taken_act", full[3]["A"], pre_count["A"]),
             "D": Counted(nc, nm + "taken_dve", full[3]["D"], pre_count["D"])}
    loaded = [nc.alloc_semaphore(f"{nm}loaded{s}") for s in range(2)]
    kept = [nc.alloc_semaphore(f"{nm}kept{s}") for s in range(2)]
    biased = [nc.alloc_semaphore(f"{nm}biased{s}") for s in range(2)]
    zeroed = nc.alloc_semaphore(nm + "zeroed")
    dve_own = LoopChain(nc, nm + "dve_own", 2)
    apart = Apart(nc, nm)
    LOADS = 2 * 16

    def body(sched):
        return sched[0], sched[1], sched[2]

    with nc.Block() as block:

        @block.sync
        def _(sp):
            def load(batch, s):
                apart(sp)
                if n == 0:
                    mask = D_["mask0"][bass.ds(batch, 1), :].to_broadcast((P, L))
                    dst = raw[s][:, :]
                else:
                    mask = D_["mask1"][:, bass.ds(batch * L, L)]
                    dst = raw[s][0:S, :]
                sp.dma_start(cx[s][:, :, :], D_["ctx"][:, :, bass.ds(batch * L, L)]).then_inc(loaded[s], 16)
                sp.dma_start(dst, mask).then_inc(loaded[s], 16)

            load(0, 0)
            load(1, 1)
            with sp.Fori(0, PAIRS - 1) as i:
                sp.wait_ge(unit_done.sem, unit_done.at(i, 0))
                apart(sp)
                sp.wait_ge(biased[0], i + 1)
                load(2 * i + 2, 0)
                last_kv1 = max(k for slot in full[1] for k, u in slot if u[0] in "KV" and u[1] == 1)
                sp.wait_ge(unit_done.sem, unit_done.at(i, last_kv1 + 1))
                apart(sp)
                sp.wait_ge(biased[1], i + 1)
                load(2 * i + 3, 1)

        @block.gpsimd
        def _(pool):
            if n == 1:
                nc.gpsimd.memset(qm[:, :, :], 0.0).then_inc(zeroed, 1)

            masked_value = -1.0e9 / layer.scale

            def convert(s, nth, before):
                pool.wait_ge(loaded[s], LOADS * nth)
                if before is not None:
                    pool.wait_ge(maxed.sem, before)
                apart(pool)
                if n == 0:
                    nc.gpsimd.tensor_scalar(bias[s][:, :], raw[s][:, :], 0.0, masked_value, ALU.is_equal,
                                            ALU.mult).then_inc(biased[s], 1)
                    pool.wait_ge(biased[s], nth)
                    apart(pool)
                    nc.gpsimd.tensor_scalar(keep[s][:, :], bias[s][:, :], 0.0, None, ALU.is_equal).then_inc(kept[s], 1)
                else:
                    nc.gpsimd.tensor_scalar(bias[s][0:S, :], raw[s][0:S, :], -BIG, 10.0, ALU.mult,
                                            ALU.mult).then_inc(biased[s], 1)

            convert(0, 1, None)
            convert(1, 1, None)
            with pool.Fori(0, PAIRS - 1) as i:
                convert(0, i + 2, maxed.at(i, H))
                convert(1, i + 2, maxed.at(i, HEADS))

        @block.tensor
        def _(pe):
            def project(u, unit, owner, i, pre):
                kind, s, t, p = unit
                bank = ps_p[u % 2]
                if pre:
                    if u >= 2:
                        eng, k = pre_owner[u - 2]
                        pe.wait_ge(taken[eng].sem, taken[eng].before(k))
                elif u >= 2:
                    eng, k = owner[u - 2]
                    pe.wait_ge(taken[eng].sem, taken[eng].at(i, k))
                else:
                    eng, k = full[2][n_units + u - 2]
                    pe.wait_ge(taken[eng].sem, taken[eng].at(i, k - taken[eng].per))
                if kind in "KV":
                    pe.wait_ge(loaded[s], LOADS if pre else (i + 2 - s) * LOADS)
                if kind == "Q":
                    for k in range(DK):
                        ins = nc.tensor.matmul(bank[:, 0:2 * S], T[f"wq{n}"][:, k, t * P:(t + 1) * P],
                                               T["xn_t"][:, k, bass.ds(i * 2 * S, 2 * S)],
                                               start=k == 0, stop=k == DK - 1)
                elif kind == "K":
                    for k in range(DK):
                        ins = nc.tensor.matmul(bank[:, 0:L], T[f"wk{n}"][:, k, t * P:(t + 1) * P],
                                               cx[s][:, k, :], start=k == 0, stop=k == DK - 1)
                elif kind == "V":
                    k0, kn = KTS[t]
                    w = layer.v_cols
                    for k in range(DK):
                        ins = nc.tensor.matmul(bank[0:kn, 0:w], cx[s][:, k, k0:k0 + kn],
                                               T[f"wv{n}"][:, k, p * w:(p + 1) * w],
                                               start=k == 0, stop=k == DK - 1)
                else:
                    pe.wait_ge(out_ready.sem, out_ready.at(i, layer.groups * (s + 1)))
                    for k in range(layer.out_tiles):
                        ins = nc.tensor.matmul(bank[0:S, 0:D], ot[s][:, k, :], T[f"wo{n}"][:, k, :],
                                               start=k == 0, stop=k == layer.out_tiles - 1)
                ins.then_inc(unit_done.sem, 1)

            def heads(i, sched):
                first, slots, owner = body(sched)
                for u, unit in first:
                    project(u, unit, owner, i, False)
                of_slot = {s: [x for slot in slots for x in slot if x[1][1] == s and x[1][0] in "KV"] for s in (0, 1)}
                for g in range(N_SLOTS):
                    if g < HEADS:
                        b, h = g // H, g % H
                        if g == 0:
                            for eng in "AD":
                                q = max([owner[u][1] for u, x in first if owner[u][0] == eng])
                                pe.wait_ge(taken[eng].sem, taken[eng].at(i, q))
                        if g == H:
                            for eng in "AD":
                                k1 = [owner[u][1] for u, x in of_slot[1] if owner[u][0] == eng]
                                if k1:
                                    pe.wait_ge(taken[eng].sem, taken[eng].at(i, max(k1)))
                        pe.wait_ge(maxed.sem, maxed.at(i, g - 1))
                        nc.tensor.matmul(ps_s[g % 2][0:S, 0:L], qm[:, h, b * S:(b + 1) * S],
                                         kt[b][:, h // layer.per_tile, :], start=True, stop=True).then_inc(scored.sem, 1)
                    for u, unit in slots[g]:
                        project(u, unit, owner, i, False)
                    t = g - LT
                    if 0 <= t < HEADS:
                        pe.wait_ge(normed.sem, normed.at(i, t + 1))
                        pe.wait_ge(pt_ready.sem, pt_ready.at(i, t - 1))
                        for c, (k0, kn) in enumerate(KTS):
                            ins = nc.tensor.transpose(ps_t[t % 2][0:kn, c * S:(c + 1) * S],
                                                      prob[0:S, t % N_PB, k0:k0 + kn], T["ident"][0:S, 0:S])
                        ins.then_inc(turned.sem, 1)
                    v = g - LP
                    if 0 <= v < HEADS:
                        b, h = v // H, v % H
                        per_group = H // layer.groups
                        group = v // per_group
                        pe.wait_ge(pt_ready.sem, pt_ready.at(i, v + 1))
                        if v % per_group == 0:
                            pe.wait_ge(out_ready.sem, out_ready.at(i, group - 1))
                        w = layer.pv_rows
                        row = h % layer.per_out * w
                        col = (h // layer.per_out * S) % 400
                        v0 = (h // 2 * 32) if n == 0 else h * w
                        for c, (k0, kn) in enumerate(KTS):
                            ins = nc.tensor.matmul(ps_o[group % 2][row:row + w, col:col + S],
                                                   vt[b][0:kn, c, v0:v0 + w], pt[0:kn, v % N_PT, c * S:(c + 1) * S],
                                                   start=c == 0, stop=c == KT_N - 1)
                        ins.then_inc(valued.sem, 1)

            for k in (scored, turned, valued, unit_done):
                k.credit(pe)
            pe.wait_ge(T["weights_in"], T["weights_in_value"][n])
            for u, unit in enumerate(pre_units):
                project(u, unit, pre_owner, 0, True)
            for eng in "AD":
                if pre_count[eng]:
                    pe.wait_ge(taken[eng].sem, taken[eng].before(pre_count[eng]))
            with pe.Fori(0, PAIRS - 1) as i:
                heads(i, full)
            heads(PAIRS - 1, lastly)

        def take(eng, nce, me, u, unit, i, pre):
            kind, s, t, p = unit
            bank = ps_p[u % 2]
            eng.wait_ge(unit_done.sem, unit_done.before(u + 1) if pre else unit_done.at(i, u + 1))
            act = me == "A"
            if kind == "Q":
                eng.wait_ge(scored.sem, scored.at(i, 0))
                if n == 0:
                    for j in range(layer.per_tile):
                        h = t * layer.per_tile + j
                        args = (qm[:, h, :], bank[:, 0:2 * S])
                        if act:
                            ins = nc.scalar.activation(*args, ACT.Identity, scale=T["head_rows"][:, j:j + 1],
                                                       bias=T["bq_head"][:, h:h + 1])
                        else:
                            ins = nc.vector.tensor_scalar(*args, T["head_rows"][:, j:j + 1],
                                                          T["bq_head"][:, h:h + 1], ALU.mult, ALU.add)
                else:
                    if not pre:
                        eng.wait_ge(zeroed, 1)
                    for j in range(2):
                        r = slice(64 * j, 64 * j + 64)
                        args = (qm[r, 2 * t + j, :], bank[r, 0:2 * S])
                        ins = nc.scalar.copy(*args) if act else nc.vector.tensor_copy(*args)
            elif kind == "K":
                if not pre:
                    eng.wait_ge(scored.sem, scored.at(i, 0 if s == 1 else H))
                if n == 0:
                    eng.wait_ge(kept[s], 1 if pre else i + 2 - s)
                    ins = nc.vector.scalar_tensor_tensor(kt[s][:, t, :], bank[:, 0:L], T["bk_col"][:, t:t + 1],
                                                         keep[s][:, :], ALU.add, ALU.mult)
                else:
                    args = (kt[s][:, t, :], bank[:, 0:L])
                    ins = nc.scalar.copy(*args) if act else nc.vector.tensor_copy(*args)
            elif kind == "V":
                if not pre:
                    eng.wait_ge(valued.sem, valued.at(i, 0 if s == 1 else H))
                kn, w = KTS[t][1], layer.v_cols
                args = (vt[s][0:kn, t, p * w:(p + 1) * w], bank[0:kn, 0:w])
                ins = nc.scalar.copy(*args) if act else nc.vector.tensor_copy(*args)
            else:
                x = T["x"][0:S, bass.ds((2 * i + s) * D, D)]
                dve_own.link(eng, nc.vector.tensor_tensor(lin[0:S, s, :], bank[0:S, 0:D], T[f"bo{n}"][0:S, :], ALU.add))
                if n == 0:
                    ins = nc.vector.scalar_tensor_tensor(x, lin[0:S, s, :], T["gate"][0:S, 0:1], x, ALU.mult, ALU.add)
                else:
                    xn = T["xn"][0:S, bass.ds((2 * i + s) * D, D)]
                    ins = nc.vector.tensor_tensor(T["z"][0:S, bass.ds((2 * i + s) * D, D)], lin[0:S, s, :], xn, ALU.add)
            ins.then_inc(taken[me].sem, 1)

        def take_before(eng, nce, me):
            for u, unit in enumerate(pre_units):
                if pre_owner[u][0] == me:
                    take(eng, nce, me, u, unit, 0, True)

        @block.scalar
        def _(act):
            def heads(i, sched):
                first, slots, owner = body(sched)
                for u, unit in first:
                    if owner[u][0] == "A":
                        take(act, nc.scalar, "A", u, unit, i, False)
                for g in range(N_SLOTS):
                    if g < HEADS:
                        act.wait_ge(maxed.sem, maxed.at(i, g + 1))
                        act.wait_ge(turned.sem, turned.at(i, g + 1 - N_PB))
                        nc.scalar.activation(prob[0:S, g % N_PB, :], masked[0:S, g % N_SB, :], ACT.Exp,
                                             bias=low[0:S, g % N_SB:g % N_SB + 1], scale=-1.0,
                                             accum_out=total[0:S, g % N_PB:g % N_PB + 1]).then_inc(exped.sem, 1)
                    t = g - LT
                    if 0 <= t < HEADS:
                        act.wait_ge(turned.sem, turned.at(i, t + 1))
                        act.wait_ge(valued.sem, valued.at(i, t + 1 - N_PT))
                        kl = KTS[-1][1]
                        nc.scalar.copy(pt[0:P, t % N_PT, 0:(KT_N - 1) * S], ps_t[t % 2][0:P, 0:(KT_N - 1) * S])
                        nc.scalar.copy(pt[0:kl, t % N_PT, (KT_N - 1) * S:KT_N * S],
                                       ps_t[t % 2][0:kl, (KT_N - 1) * S:KT_N * S]).then_inc(pt_ready.sem, 1)
                    for u, unit in slots[g]:
                        if owner[u][0] == "A":
                            take(act, nc.scalar, "A", u, unit, i, False)

            for k in (exped, pt_ready, taken["A"]):
                k.credit(act)
            take_before(act, nc.scalar, "A")
            with act.Fori(0, PAIRS - 1) as i:
                heads(i, full)
            heads(PAIRS - 1, lastly)

        @block.vector
        def _(dve):
            def heads(i, sched):
                first, slots, owner = body(sched)
                dve_own.begin(i)
                for u, unit in first:
                    if owner[u][0] == "D":
                        take(dve, nc.vector, "D", u, unit, i, False)
                for g in range(N_SLOTS):
                    if g < HEADS:
                        s = g // H
                        if g % H == 0:
                            dve.wait_ge(biased[s], i + 1)
                        dve.wait_ge(scored.sem, scored.at(i, g + 1))
                        dve.wait_ge(exped.sem, exped.at(i, g + 1 - N_SB))
                        apart(dve)
                        nc.vector.tensor_tensor_reduce(out=masked[0:S, g % N_SB, :], in0=ps_s[g % 2][0:S, 0:L],
                                                       in1=bias[s][0:S, :], scale=-layer.scale, scalar=BIG,
                                                       op0=ALU.add, op1=ALU.min,
                                                       accum_out=low[0:S, g % N_SB:g % N_SB + 1]).then_inc(maxed.sem, 1)
                    for u, unit in slots[g]:
                        if owner[u][0] == "D":
                            take(dve, nc.vector, "D", u, unit, i, False)
                    r = g - 1
                    if 0 <= r < HEADS:
                        k = r % N_PB
                        dve.wait_ge(exped.sem, exped.at(i, r + 1))
                        nc.vector.reciprocal(inv[0:S, k:k + 1], total[0:S, k:k + 1]).then_inc(inverted.sem, 1)
                        dve.wait_ge(inverted.sem, inverted.at(i, r + 1))
                        nc.vector.tensor_scalar(prob[0:S, k, :], prob[0:S, k, :], inv[0:S, k:k + 1], None,
                                                ALU.mult).then_inc(normed.sem, 1)
                    v = g - LP - 1
                    per_group = H // layer.groups
                    if 0 <= v < HEADS and v % per_group == per_group - 1:
                        group = v // per_group
                        b, half = v // H, group % layer.groups
                        dve.wait_ge(valued.sem, valued.at(i, v + 1))
                        w_unit = [u for slot in full[1] for u, x in slot if x[0] == "W" and x[1] == b][0]
                        dve.wait_ge(unit_done.sem, unit_done.at(i, w_unit + 1 - n_units))
                        dst = ot[b][:, half * 4:half * 4 + 4, :]
                        src = ps_o[group % 2][:, 0:4 * S].rearrange("p (t s) -> p t s", t=4)
                        if n == 0:
                            bv = T["bv_out"][:, :].unsqueeze(2).to_broadcast((P, 4, S))
                            ins = nc.vector.tensor_tensor(dst, src, bv, ALU.add)
                        else:
                            ins = nc.vector.tensor_copy(dst, src)
                        ins.then_inc(out_ready.sem, 1)
                dve_own.end()

            for k in (maxed, inverted, normed, out_ready, taken["D"]):
                k.credit(dve)
            take_before(dve, nc.vector, "D")
            with dve.Fori(0, PAIRS - 1) as i:
                heads(i, full)
            heads(PAIRS - 1, lastly)

    ctx.close()


def normalise(nc, T, nm, z_first):
    with ExitStack() as ctx:
        stats = ctx.enter_context(nc.sbuf_tensor(nm + "stats", [P, B, 6], F32))
        mv = ctx.enter_context(nc.sbuf_tensor(nm + "mv", [P, B, 2], F32))
        dev = ctx.enter_context(nc.sbuf_tensor(nm + "dev", [P, 2, B], F32))
        rs = ctx.enter_context(nc.sbuf_tensor(nm + "rs", [P, B], F32))
        banks = [ctx.enter_context(nc.psum_tensor(f"{nm}bank{k}", [P, 512], F32)) for k in range(8)]
        own = Chain(nc, nm + "own")
        var_ready = nc.alloc_semaphore(nm + "var_ready")
        root_ready = nc.alloc_semaphore(nm + "root_ready")
        xn_ready = nc.alloc_semaphore(nm + "xn_ready")
        turned = nc.alloc_semaphore(nm + "turned")
        x3 = T["x"][0:S, :].rearrange("p (b d) -> p b d", b=B)

        with nc.Block() as block:

            @block.vector
            def _(dve):
                dve.wait_ge(T["x_in"], 16)

                def moments(src, scale, eps, nth):
                    for b in range(B):
                        last = own.mark(nc.vector.bn_stats(stats[0:S, b, :], src[0:S, b * D:(b + 1) * D]))
                    dve.wait_ge(own.sem, last)
                    for b in range(B):
                        last = own.mark(nc.vector.bn_aggr(mv[0:S, b, :], stats[0:S, b, :]))
                    dve.wait_ge(own.sem, last)
                    nc.vector.tensor_scalar(dev[0:S, 0, :], mv[0:S, :, 1], scale, eps, ALU.mult,
                                            ALU.add).then_inc(var_ready, 1)
                    dve.wait_ge(root_ready, nth)

                if z_first:
                    moments(T["z"], D / (D - 1.0), 0.0, 1)
                    own.link(dve, nc.vector.tensor_scalar(rs[0:S, :], dev[0:S, 1, :], Z_EPS, None, ALU.add))
                    own.link(dve, nc.vector.reciprocal(rs[0:S, :], rs[0:S, :]))
                    for b in range(B):
                        zb = T["z"][0:S, b * D:(b + 1) * D]
                        last = own.mark(nc.vector.tensor_scalar(zb, zb, mv[0:S, b, 0:1], rs[0:S, b:b + 1],
                                                                ALU.subtract, ALU.mult))
                    dve.wait_ge(own.sem, last)
                    z3 = T["z"][0:S, :].rearrange("p (b d) -> p b d", b=B)
                    wide = (S, B, D)
                    own.link(dve, nc.vector.tensor_tensor(z3, z3, T["gamma"][0:S, :].unsqueeze(1).to_broadcast(wide), ALU.mult))
                    own.link(dve, nc.vector.tensor_tensor(z3, z3, T["beta"][0:S, :].unsqueeze(1).to_broadcast(wide), ALU.add))
                    own.link(dve, nc.vector.scalar_tensor_tensor(T["x"][0:S, :], T["z"][0:S, :], T["gate"][0:S, 2:3],
                                                                 T["x"][0:S, :], ALU.mult, ALU.add))
                moments(T["x"], 1.0, LN_EPS, 1 + z_first)
                own.link(dve, nc.vector.reciprocal(rs[0:S, :], dev[0:S, 1, :]))
                for b in range(B):
                    nc.vector.tensor_scalar(T["xn"][0:S, b * D:(b + 1) * D], T["x"][0:S, b * D:(b + 1) * D],
                                            mv[0:S, b, 0:1], rs[0:S, b:b + 1], ALU.subtract, ALU.mult).then_inc(xn_ready, 1)
                for q in range(1, 8, 2):
                    dve.wait_ge(turned, q + 1)
                    nc.vector.tensor_copy(T["xn_t"][:, q % DK, q // DK * 4 * S:(q // DK + 1) * 4 * S], banks[q][:, 0:4 * S])

            @block.scalar
            def _(act):
                for nth in range(1 + z_first):
                    act.wait_ge(var_ready, nth + 1)
                    nc.scalar.activation(dev[0:S, 1, :], dev[0:S, 0, :], ACT.Sqrt).then_inc(root_ready, 1)
                for q in range(0, 8, 2):
                    act.wait_ge(turned, q + 1)
                    nc.scalar.copy(T["xn_t"][:, q % DK, q // DK * 4 * S:(q // DK + 1) * 4 * S], banks[q][:, 0:4 * S])

            @block.tensor
            def _(pe):
                pe.wait_ge(T["ident_ready"], 1)
                for q in range(8):
                    for j in range(4):
                        b = q // DK * 4 + j
                        pe.wait_ge(xn_ready, b + 1)
                        c = b * D + q % DK * P
                        ins = nc.tensor.transpose(banks[q][:, j * S:(j + 1) * S], T["xn"][0:S, c:c + P],
                                                  T["ident"][0:S, 0:S])
                    ins.then_inc(turned, 1)


def feed_forward(nc, n, T, D_, out):
    nm = f"f{n}_"
    ctx = ExitStack()

    def sb(name, shape, dt=F32):
        return ctx.enter_context(nc.sbuf_tensor(nm + name, shape, dt))

    logits, top, ex = sb("logits", [P, B, E]), sb("top", [P, B, E]), sb("ex", [P, B, E])
    idx, chosen = sb("idx", [P, B, E], U32), sb("chosen", [P, 2, B])
    weight = sb("weight", [P, 2, B])
    norm = sb("norm", [P, B])
    hot = sb("hot", [P, 2, B, E])
    tot = sb("tot", [P, 2, B, E])
    run = [sb(f"run{k}", [P, 2, B, E]) for k in range(2)]
    rank = sb("rank", [P, 2, B, E])
    picked = sb("picked", [P, 2, B])
    slot, row, valid = sb("slot", [P, 2, B]), sb("row", [P, 2, B]), sb("valid", [P, 2, B])
    scat, gath = sb("scat", [P, 2, B], U32), sb("gath", [P, 2, B], U32)
    drop_row = sb("drop_row", [P, 2, B])
    need, need_i, ends = sb("need", [P, E]), sb("need_i", [P, E], I32), [sb(f"ends{k}", [P, E]) for k in range(2)]
    step = sb("step", [P, TILES])
    before = sb("before", [P, TILES, E])
    owner_f, owner_i = sb("owner_f", [P, TILES]), sb("owner_i", [P, TILES], I32)
    got = [[sb(f"got{k}_{s}", [P, D]) for s in range(2)] for k in range(2)]
    ps = [ctx.enter_context(nc.psum_tensor(f"{nm}ps{k}", [P, 512], F32)) for k in range(8)]

    logits_done, hot_ready, ranked = (nc.alloc_semaphore(nm + k) for k in ("logits_done", "hot_ready", "ranked"))
    diff_ready, ex_ready = nc.alloc_semaphore(nm + "diff_ready"), nc.alloc_semaphore(nm + "ex_ready")
    rows_ready, dispatched = nc.alloc_semaphore(nm + "rows_ready"), nc.alloc_semaphore(nm + "dispatched")
    iotas = nc.alloc_semaphore(nm + "iotas")
    stored = nc.alloc_semaphore(nm + "stored")
    gathered = [nc.alloc_semaphore(f"{nm}gathered{s}") for s in range(2)]
    added = nc.alloc_semaphore(nm + "added")
    out_done = nc.alloc_semaphore(nm + "out_done")
    own = Chain(nc, nm + "own")
    apart = Apart(nc, nm)
    XS, YS = D_[f"xs{n}"], D_[f"ys{n}"]

    def route(dve):
        v = nc.vector
        dve.wait_ge(logits_done, 1)
        own.link(dve, v.tensor_copy(logits[0:S, :, :].rearrange("p b e -> p (b e)"), ps[0][0:S, 0:B * E]))
        for b in range(B):
            last = own.mark(v.max(top[0:S, b, :], logits[0:S, b, :]))
        dve.wait_ge(own.sem, last)
        for b in range(B):
            last = own.mark(v.max_index(idx[0:S, b, :], top[0:S, b, :], logits[0:S, b, :]))
        v.tensor_tensor(ex[0:S, :, :], top[0:S, :, :], top[0:S, :, 0:1].to_broadcast((S, B, E)),
                        ALU.subtract).then_inc(diff_ready, 1)
        dve.wait_ge(own.sem, last)
        own.link(dve, v.tensor_copy(chosen[0:S, :, :].rearrange("p k b -> p b k"), idx[0:S, :, 0:2]))
        dve.wait_ge(iotas, 3)
        shape = (S, 2, B, E)
        for k in range(2):
            ins = v.tensor_tensor(hot[0:S, k, :, :], T["experts"][0:S, :].unsqueeze(1).to_broadcast((S, B, E)),
                                  chosen[0:S, k, :].unsqueeze(2).to_broadcast((S, B, E)), ALU.is_equal)
            ins.then_inc(hot_ready, 1)
        dve.wait_ge(ex_ready, 1)
        own.link(dve, v.tensor_reduce(norm[0:S, :], ex[0:S, :, 0:(2 if n == 0 else E)], AX.X, ALU.add))
        own.link(dve, v.reciprocal(norm[0:S, :], norm[0:S, :]))
        own.link(dve, v.tensor_scalar(weight[0:S, 0, :], norm[0:S, :], T["gate"][0:S, 2 * n + 1:2 * n + 2], None, ALU.mult))
        own.link(dve, v.tensor_tensor(weight[0:S, 1, :], weight[0:S, 0, :], ex[0:S, :, 1], ALU.mult))
        dve.wait_ge(ranked, 1)
        flat = "p k b e -> p (k b e)"
        own.link(dve, v.tensor_copy(tot[0:S, :, :, :].rearrange(flat), ps[2][0:S, 0:2 * B * E]))
        own.link(dve, v.tensor_copy(run[0][0:S, :, :, :].rearrange(flat), ps[2][0:S, 0:2 * B * E]))
        a = 0
        for d in (1, 2, 4, 8):
            src, dst = run[a], run[1 - a]
            own.mark(v.tensor_copy(dst[0:S, :, 0:d, :], src[0:S, :, 0:d, :]))
            for k in range(2):
                last = own.mark(v.tensor_tensor(dst[0:S, k, d:B, :], src[0:S, k, d:B, :], src[0:S, k, 0:B - d, :], ALU.add))
            dve.wait_ge(own.sem, last)
            a = 1 - a
        run_t = run[a]
        own.link(dve, v.tensor_tensor(rank[0:S, :, :, :].rearrange(flat), ps[1][0:S, 0:2 * B * E],
                                      run_t[0:S, :, :, :].rearrange(flat), ALU.add))
        own.link(dve, v.tensor_tensor(rank[0:S, :, :, :].rearrange(flat), rank[0:S, :, :, :].rearrange(flat),
                                      tot[0:S, :, :, :].rearrange(flat), ALU.subtract))
        own.link(dve, v.tensor_tensor(rank[0:S, 1, :, :], rank[0:S, 1, :, :],
                                      run_t[0:S, 0, B - 1:B, :].to_broadcast((S, B, E)), ALU.add))
        if n == 1:
            own.link(dve, v.tensor_tensor(need[0:S, :], run_t[0:S, 0, B - 1, :], run_t[0:S, 1, B - 1, :], ALU.add))
            own.link(dve, v.tensor_scalar(need_i[0:S, :], need[0:S, :], float(P - 1), None, ALU.add))
            own.link(dve, v.tensor_scalar(need_i[0:S, :], need_i[0:S, :], 7, None, ALU.arith_shift_right))
            own.link(dve, v.tensor_copy(need[0:S, :], need_i[0:S, :]))
            own.link(dve, v.tensor_copy(ends[0][0:S, :], need_i[0:S, :]))
            a = 0
            for d in (1, 2, 4):
                own.mark(v.tensor_copy(ends[1 - a][0:S, 0:d], ends[a][0:S, 0:d]))
                own.link(dve, v.tensor_tensor(ends[1 - a][0:S, d:E], ends[a][0:S, d:E], ends[a][0:S, 0:E - d], ALU.add))
                a = 1 - a
            end = ends[a]
            own.link(dve, v.tensor_tensor(before[0:S, :, :], end[0:S, :].unsqueeze(1).to_broadcast((S, TILES, E)),
                                          step[0:S, :].unsqueeze(2).to_broadcast((S, TILES, E)), ALU.is_le))
            own.link(dve, v.tensor_reduce(owner_f[0:S, :], before[0:S, :, :], AX.X, ALU.add))
            own.link(dve, v.tensor_scalar(owner_i[0:S, :], owner_f[0:S, :], float(E - 1), None, ALU.min))
            own.link(dve, v.tensor_tensor(need[0:S, :], end[0:S, :], need[0:S, :], ALU.subtract))
            own.link(dve, v.tensor_scalar(need[0:S, :], need[0:S, :], float(P), None, ALU.mult))
            for k in range(2):
                last = own.mark(v.tensor_tensor(rank[0:S, k, :, :], rank[0:S, k, :, :],
                                                need[0:S, :].unsqueeze(1).to_broadcast((S, B, E)), ALU.add))
            dve.wait_ge(own.sem, last)
        own.link(dve, v.tensor_tensor(rank[0:S, :, :, :].rearrange(flat), rank[0:S, :, :, :].rearrange(flat),
                                      hot[0:S, :, :, :].rearrange(flat), ALU.mult))
        own.link(dve, v.tensor_reduce(picked[0:S, :, :], rank[0:S, :, :, :], AX.X, ALU.add))
        if n == 0:
            own.link(dve, v.tensor_scalar(valid[0:S, :, :], picked[0:S, :, :], float(CAP), None, ALU.is_lt))
            own.link(dve, v.scalar_tensor_tensor(slot[0:S, :, :], chosen[0:S, :, :], float(SLOTS), picked[0:S, :, :],
                                                 ALU.mult, ALU.add))
            own.link(dve, v.tensor_tensor(weight[0:S, :, :], weight[0:S, :, :], valid[0:S, :, :], ALU.mult))
            own.link(dve, v.tensor_tensor(row[0:S, :, :], slot[0:S, :, :], drop_row[0:S, :, :], ALU.subtract))
            own.link(dve, v.tensor_tensor(row[0:S, :, :], row[0:S, :, :], valid[0:S, :, :], ALU.mult))
            own.link(dve, v.tensor_tensor(scat[0:S, :, :], row[0:S, :, :], drop_row[0:S, :, :], ALU.add))
            own.link(dve, v.tensor_tensor(gath[0:S, :, :], slot[0:S, :, :], valid[0:S, :, :], ALU.mult))
        else:
            own.link(dve, v.tensor_copy(scat[0:S, :, :], picked[0:S, :, :]))
            own.link(dve, v.tensor_copy(gath[0:S, :, :], picked[0:S, :, :]))
        dve.sem_inc(rows_ready, 1)

    def pool_dispatch(pool):
        pool.iota(drop_row[0:S, :, :], pattern=[[B * S, 2], [S, B]], base=DROP0, channel_multiplier=1,
                  allow_small_or_imprecise_dtypes=True).then_inc(iotas, 1)
        pool.iota(step[0:S, :], pattern=[[1, TILES]], base=0, channel_multiplier=0,
                  allow_small_or_imprecise_dtypes=True).then_inc(iotas, 1)
        pool.iota(T["experts"][0:S, :], pattern=[[1, E]], base=0, channel_multiplier=0,
                  allow_small_or_imprecise_dtypes=True).then_inc(iotas, 1)
        pool.wait_ge(D_["cleared"], D_["cleared_value"])
        pool.wait_ge(rows_ready, 1)
        for k in range(2):
            for b in range(B):
                pool.indirect_dma_start(out=XS[:, :], out_offset=bass.IndirectOffsetOnAxis(ap=scat[0:S, k, b:b + 1], axis=0),
                                        in_=T["xn"][0:S, b * D:(b + 1) * D], in_offset=None).then_inc(dispatched, 16)

    def pool_gather(pool, stores):
        pool.wait_ge(stored, 16 * stores)
        for b in range(B):
            s = b % 2
            if b >= 2:
                pool.wait_ge(added, b - 1)
            for k in range(2):
                pool.indirect_dma_start(out=got[k][s][0:S, :], out_offset=None, in_=YS[:, :],
                                        in_offset=bass.IndirectOffsetOnAxis(ap=gath[0:S, k, b:b + 1], axis=0)).then_inc(gathered[s], 16)

    def combine(dve):
        for b in range(B):
            s = b % 2
            dve.wait_ge(gathered[s], 32 * (b // 2 + 1))
            x = T["x"][0:S, b * D:(b + 1) * D]
            own.link(dve, nc.vector.scalar_tensor_tensor(x, got[0][s][0:S, :], weight[0:S, 0, b:b + 1], x, ALU.mult, ALU.add))
            nc.vector.scalar_tensor_tensor(x, got[1][s][0:S, :], weight[0:S, 1, b:b + 1], x, ALU.mult,
                                           ALU.add).then_inc(added, 1)

    def logits_and_ranks(pe):
        for b in range(B):
            for k in range(DK):
                ins = nc.tensor.matmul(ps[0][0:S, b * E:(b + 1) * E], T["xn_t"][:, k, b * S:(b + 1) * S],
                                       T[f"wr{n}"][:, k, :], start=k == 0, stop=k == DK - 1)
        ins.then_inc(logits_done, 1)
        pe.wait_ge(hot_ready, 2)
        one_hots = hot[0:S, :, :, :].rearrange("p k b e -> p (k b e)")
        nc.tensor.matmul(ps[1][0:S, 0:2 * B * E], T["earlier"][0:S, 0:S], one_hots, start=True, stop=True)
        nc.tensor.matmul(ps[2][0:S, 0:2 * B * E], T["ones"][0:S, 0:S], one_hots, start=True, stop=True).then_inc(ranked, 1)

    def exps(act):
        act.wait_ge(diff_ready, 1)
        nc.scalar.activation(ex[0:S, :, :], ex[0:S, :, :], ACT.Exp).then_inc(ex_ready, 1)

    if n == 0:
        w1, w2 = T["w1_0"], T["w2_0"]
        xe = [sb(f"xe{s}", [P, 4, D]) for s in range(2)]
        xt = [sb(f"xt{s}", [P, DK, SLOTS]) for s in range(2)]
        ht = [sb(f"ht{s}", [P, F0 // P, SLOTS]) for s in range(2)]
        ye = [sb(f"ye{s}", [P, 4, D]) for s in range(2)]
        NF = F0 // P
        rows_in = [nc.alloc_semaphore(f"{nm}rows_in{s}") for s in range(2)]
        w_in = T["w_in"]
        x_turned = Counted(nc, nm + "x_turned", 2)
        xt_ready = Counted(nc, nm + "xt_ready", 2)
        up_done = Counted(nc, nm + "up_done", 2 * NF)
        gelu_done = Counted(nc, nm + "gelu_done", 2 * NF)
        down_done = Counted(nc, nm + "down_done", 8)
        y_ready = Counted(nc, nm + "y_ready", 8)
        y_out = [nc.alloc_semaphore(f"{nm}y_out{s}") for s in range(2)]
        X4 = XS[0:ROWS, :].rearrange("(e p j) d -> p e j d", e=E, j=4)
        Y4 = YS[0:ROWS, :].rearrange("(e p j) d -> p e j d", e=E, j=4)

        with nc.Block() as block:

            @block.sync
            def _(sp):
                def load_rows(e, s):
                    sp.dma_start(xe[s][:, :, :], X4[:, bass.ds(e, 1), :, :].rearrange("p e j d -> p (e j) d")).then_inc(rows_in[s], 16)

                sp.wait_ge(dispatched, 16 * 2 * B)
                load_rows(0, 0)
                load_rows(1, 1)
                with sp.Fori(0, E // 2) as i:
                    for s in range(2):
                        sp.wait_ge(y_ready.sem, y_ready.at(i, 4 * (s + 1)))
                        apart(sp)
                        sp.dma_start(Y4[:, bass.ds(2 * i + s, 1), :, :].rearrange("p e j d -> p (e j) d"), ye[s][:, :, :]).then_inc(y_out[s], 16)
                for s in range(2):
                    sp.wait_ge(y_out[s], 16 * (E // 2))
                sp.sem_inc(stored, 16)

            @block.gpsimd
            def _(pool):
                pool_dispatch(pool)
                pool_gather(pool, 1)

            @block.tensor
            def _(pe):
                for k in (x_turned, up_done, down_done):
                    k.credit(pe)
                logits_and_ranks(pe)

                def turn(i, s):
                    pe.wait_ge(rows_in[s], 16 * (i + 1))
                    pe.wait_ge(xt_ready.sem, xt_ready.at(i, s))
                    for k in range(DK):
                        for j in range(4):
                            ins = nc.tensor.transpose(ps[k][:, j * P:(j + 1) * P], xe[s][:, j, k * P:(k + 1) * P], T["ident"][:, :])
                    ins.then_inc(x_turned.sem, 1)

                def up(i, s):
                    pe.wait_ge(xt_ready.sem, xt_ready.at(i, s + 1))
                    pe.wait_ge(w_in[s], 32 * (i + 1))
                    for f in range(NF):
                        pe.wait_ge(gelu_done.sem, gelu_done.at(i, s * NF + f - 1))
                        for k in range(DK):
                            ins = nc.tensor.matmul(ps[2 + f % 2][:, :], w1[s][:, k, f * P:(f + 1) * P], xt[s][:, k, :],
                                                   start=k == 0, stop=k == DK - 1)
                        ins.then_inc(up_done.sem, 1)

                def down(i, s):
                    pe.wait_ge(gelu_done.sem, gelu_done.at(i, (s + 1) * NF))
                    for j in range(4):
                        pe.wait_ge(y_ready.sem, y_ready.at(i, s * 4 + j - 1))
                        for f in range(NF):
                            ins = nc.tensor.matmul(ps[4 + j % 2][:, 0:D], ht[s][:, f, j * P:(j + 1) * P], w2[s][:, f, :],
                                                   start=f == 0, stop=f == NF - 1)
                        ins.then_inc(down_done.sem, 1)

                with pe.Fori(0, E // 2) as i:
                    turn(i, 0)
                    up(i, 0)
                    turn(i, 1)
                    down(i, 0)
                    up(i, 1)
                    down(i, 1)

            @block.scalar
            def _(act):
                gelu_done.credit(act)
                exps(act)

                def load_expert(e, s):
                    act.dma_start(w1[s][:, :, :], D_["c_fc"][bass.ds(e, 1), :, :, :].rearrange("e p k f -> p (e k) f")).then_inc(w_in[s], 16)
                    act.dma_start(w2[s][:, :, :], D_["c_proj"][bass.ds(e, 1), :, :, :].rearrange("e p f d -> p (e f) d")).then_inc(w_in[s], 16)

                def gelus(i, s):
                    for f in range(NF):
                        act.wait_ge(up_done.sem, up_done.at(i, s * NF + f + 1))
                        if f == 0:
                            act.wait_ge(down_done.sem, down_done.at(i, s * 4 - 4))
                        nc.scalar.activation(ht[s][:, f, :], ps[2 + f % 2][:, :], ACT.Gelu).then_inc(gelu_done.sem, 1)

                def refill(i, s):
                    act.wait_ge(down_done.sem, down_done.at(i, s * 4 + 4))
                    load_expert(2 * i + 2 + s, s)
                    act.dma_start(xe[s][:, :, :], X4[:, bass.ds(2 * i + 2 + s, 1), :, :].rearrange("p e j d -> p (e j) d")).then_inc(rows_in[s], 16)

                with act.Fori(0, E // 2 - 1) as i:
                    gelus(i, 0)
                    gelus(i, 1)
                    refill(i, 0)
                    refill(i, 1)
                gelus(E // 2 - 1, 0)
                gelus(E // 2 - 1, 1)

            @block.vector
            def _(dve):
                xt_ready.credit(dve)
                y_ready.credit(dve)
                route(dve)

                def turned_rows(i, s):
                    dve.wait_ge(x_turned.sem, x_turned.at(i, s + 1))
                    dve.wait_ge(up_done.sem, up_done.at(i, (s - 1) * NF))
                    own_ready = None
                    nc.vector.tensor_copy(xt[s][:, 0, :], ps[0][:, :])
                    nc.vector.tensor_copy(xt[s][:, 1, :], ps[1][:, :]).then_inc(xt_ready.sem, 1)

                def rows_out(i, s):
                    for j in range(4):
                        dve.wait_ge(down_done.sem, down_done.at(i, s * 4 + j + 1))
                        if j == 0:
                            if isinstance(i, int):
                                if i > 0:
                                    dve.wait_ge(y_out[s], 16 * i)
                            else:
                                dve.wait_ge(y_out[s], 16 * i)
                        nc.vector.tensor_copy(ye[s][:, j, :], ps[4 + j % 2][:, 0:D]).then_inc(y_ready.sem, 1)

                def expert_pair(i):
                    turned_rows(i, 0)
                    turned_rows(i, 1)
                    rows_out(i, 0)
                    rows_out(i, 1)

                expert_pair(0)
                with dve.Fori(1, E // 2) as i:
                    expert_pair(i)
                combine(dve)
    else:
        w1, w2 = sb("w1", [P, E * DK * F1]), sb("w2", [P, E * (F1 // P) * D])
        b1, b2 = sb("b1", [P, E * F1]), sb("b2", [P, E * D])
        NF = F1 // P
        xe = [sb(f"xe{s}", [P, D]) for s in range(2)]
        xt = [sb(f"xt{s}", [P, DK, P]) for s in range(2)]
        hb = [sb(f"hb{s}", [P, F1]) for s in range(2)]
        hg = [sb(f"hg{s}", [P, F1]) for s in range(2)]
        ht = [sb(f"ht{s}", [P, NF, P]) for s in range(2)]
        ye = [sb(f"ye{s}", [P, D]) for s in range(2)]
        w_in = nc.alloc_semaphore(nm + "w_in")
        rows_in = [nc.alloc_semaphore(f"{nm}rows_in{s}") for s in range(2)]
        y_out = [nc.alloc_semaphore(f"{nm}y_out{s}") for s in range(2)]
        x_turned, xt_ready = Counted(nc, nm + "x_turned", 2), Counted(nc, nm + "xt_ready", 2)
        up_done, b1_added = Counted(nc, nm + "up_done", 2), Counted(nc, nm + "b1_added", 2)
        gelu_done, h_turned = Counted(nc, nm + "gelu_done", 2), Counted(nc, nm + "h_turned", 2)
        ht_ready, down_done = Counted(nc, nm + "ht_ready", 2), Counted(nc, nm + "down_done", 2)
        y_ready = Counted(nc, nm + "y_ready", 2)

        with nc.Block() as block:

            @block.sync
            def _(sp):
                sp.dma_start(w1[:, :], D_["W1"]).then_inc(w_in, 16)
                sp.dma_start(w2[:, :], D_["W2"]).then_inc(w_in, 16)
                sp.dma_start(b1[:, :], D_["b1"].to_broadcast((P, E * F1))).then_inc(w_in, 16)
                sp.dma_start(b2[:, :], D_["b2"].to_broadcast((P, E * D))).then_inc(w_in, 16)
                sp.wait_ge(dispatched, 16 * 2 * B)

                def load_rows(t, s):
                    sp.dma_start(xe[s][:, :], XS[bass.ds(t * P, P), :]).then_inc(rows_in[s], 16)

                load_rows(0, 0)
                load_rows(1, 1)

                def pair(i, more):
                    if more:
                        for s in range(2):
                            sp.wait_ge(x_turned.sem, x_turned.at(i, s + 1))
                            apart(sp)
                            load_rows(2 * i + 2 + s, s)
                    for s in range(2):
                        sp.wait_ge(y_ready.sem, y_ready.at(i, s + 1))
                        apart(sp)
                        sp.dma_start(YS[bass.ds((2 * i + s) * P, P), :], ye[s][:, :]).then_inc(y_out[s], 16)

                with sp.Fori(0, TILES // 2 - 1) as i:
                    pair(i, True)
                pair(TILES // 2 - 1, False)
                for s in range(2):
                    sp.wait_ge(y_out[s], 16 * (TILES // 2))
                sp.sem_inc(stored, 16)
                for h in range(2):
                    sp.wait_ge(added, B // 2 * (h + 1))
                    r = slice(h * B // 2, (h + 1) * B // 2)
                    sp.dma_start(out[r, :, :].rearrange("b s d -> s b d"),
                                 T["x"][0:S, :].rearrange("p (b d) -> p b d", b=B)[:, r, :]).then_inc(out_done, 16)
                sp.wait_ge(out_done, 32)

            @block.gpsimd
            def _(pool):
                pool_dispatch(pool)
                pool_gather(pool, 1)

            @block.tensor
            def _(pe):
                for k in (x_turned, up_done, h_turned, down_done):
                    k.credit(pe)
                logits_and_ranks(pe)
                pe.wait_ge(w_in, 64)
                pe.wait_ge(rows_ready, 1)

                with pe.Fori(0, TILES // 2) as i:
                    experts = []
                    for s in range(2):
                        expert = pe.value_load(owner_i[0:1, bass.ds(2 * i + s, 1)], min_val=0, max_val=E - 1)
                        experts.append(expert)
                        pe.wait_ge(rows_in[s], 16 * (i + 1))
                        pe.wait_ge(xt_ready.sem, xt_ready.at(i, s - 1))
                        for k in range(DK):
                            ins = nc.tensor.transpose(ps[s][:, k * P:(k + 1) * P], xe[s][:, k * P:(k + 1) * P], T["ident"][:, :])
                        ins.then_inc(x_turned.sem, 1)
                        pe.wait_ge(xt_ready.sem, xt_ready.at(i, s + 1))
                        pe.wait_ge(b1_added.sem, b1_added.at(i, s - 1))
                        for k in range(DK):
                            ins = nc.tensor.matmul(ps[2 + s][:, :], xt[s][:, k, :],
                                                   w1[:, bass.ds(expert * (DK * F1) + k * F1, F1)], start=k == 0, stop=k == DK - 1)
                        ins.then_inc(up_done.sem, 1)
                    for s in range(2):
                        pe.wait_ge(gelu_done.sem, gelu_done.at(i, s + 1))
                        pe.wait_ge(ht_ready.sem, ht_ready.at(i, s - 1))
                        for f in range(NF):
                            ins = nc.tensor.transpose(ps[4 + s][:, f * P:(f + 1) * P], hg[s][:, f * P:(f + 1) * P], T["ident"][:, :])
                        ins.then_inc(h_turned.sem, 1)
                        pe.wait_ge(ht_ready.sem, ht_ready.at(i, s + 1))
                        pe.wait_ge(y_ready.sem, y_ready.at(i, s - 1))
                        for f in range(NF):
                            ins = nc.tensor.matmul(ps[6 + s][:, 0:D], ht[s][:, f, :],
                                                   w2[:, bass.ds(experts[s] * (NF * D) + f * D, D)], start=f == 0, stop=f == NF - 1)
                        ins.then_inc(down_done.sem, 1)

            @block.scalar
            def _(act):
                for k in (xt_ready, gelu_done, ht_ready):
                    k.credit(act)
                exps(act)
                with act.Fori(0, TILES // 2) as i:
                    for s in range(2):
                        act.wait_ge(x_turned.sem, x_turned.at(i, s + 1))
                        act.wait_ge(up_done.sem, up_done.at(i, s - 1))
                        nc.scalar.copy(xt[s][:, :, :].rearrange("p k s -> p (k s)"), ps[s][:, 0:DK * P]).then_inc(xt_ready.sem, 1)
                    for s in range(2):
                        act.wait_ge(b1_added.sem, b1_added.at(i, s + 1))
                        act.wait_ge(h_turned.sem, h_turned.at(i, s - 1))
                        nc.scalar.activation(hg[s][:, :], hb[s][:, :], ACT.Gelu_apprx_tanh).then_inc(gelu_done.sem, 1)
                    for s in range(2):
                        act.wait_ge(h_turned.sem, h_turned.at(i, s + 1))
                        act.wait_ge(down_done.sem, down_done.at(i, s - 1))
                        nc.scalar.copy(ht[s][:, :, :].rearrange("p f s -> p (f s)"), ps[4 + s][:, :]).then_inc(ht_ready.sem, 1)

            @block.vector
            def _(dve):
                for k in (b1_added, y_ready):
                    k.credit(dve)
                route(dve)
                dve.wait_ge(w_in, 64)

                def pair(i, first):
                    experts = []
                    for s in range(2):
                        expert = dve.value_load(owner_i[0:1, bass.ds(2 * i + s, 1)], min_val=0, max_val=E - 1)
                        experts.append(expert)
                        dve.wait_ge(up_done.sem, up_done.at(i, s + 1))
                        dve.wait_ge(gelu_done.sem, gelu_done.at(i, s - 1))
                        nc.vector.tensor_tensor(hb[s][:, :], ps[2 + s][:, :], b1[:, bass.ds(expert * F1, F1)],
                                                ALU.add).then_inc(b1_added.sem, 1)
                    for s in range(2):
                        dve.wait_ge(down_done.sem, down_done.at(i, s + 1))
                        if not first:
                            dve.wait_ge(y_out[s], 16 * i)
                        nc.vector.tensor_tensor(ye[s][:, :], ps[6 + s][:, 0:D], b2[:, bass.ds(experts[s] * D, D)],
                                                ALU.add).then_inc(y_ready.sem, 1)

                pair(0, True)
                with dve.Fori(1, TILES // 2) as i:
                    pair(i, False)
                combine(dve)

    ctx.close()


def gated_two_layers(nc, a, out):
    ctx = ExitStack()

    def sb(name, shape, dt=F32):
        return ctx.enter_context(nc.sbuf_tensor(name, shape, dt))

    T, D_ = {}, dict(a)
    for n in (0, 1):
        D_[f"xs{n}"] = nc.dram_tensor(f"rows_in{n}", (DROP0 + 2 * B * S, D), F32, kind="Internal").ap()
        D_[f"ys{n}"] = nc.dram_tensor(f"rows_out{n}", (ROWS, D), F32, kind="Internal").ap()
    T["x"], T["xn"], T["xn_t"] = sb("x", [P, B * D]), sb("xn", [P, B * D]), sb("xn_t", [P, DK, B * S])
    T["ident"], T["ones"], T["earlier"] = sb("ident", [P, P]), sb("ones", [P, P]), sb("earlier", [P, P])
    T["experts"] = sb("experts", [P, E])
    T["wr0"], T["wr1"] = sb("wr0", [P, DK, E]), sb("wr1", [P, DK, E])
    T["bo0"], T["bo1"], T["gamma"], T["beta"] = (sb(k, [P, D]) for k in ("bo0", "bo1", "gamma", "beta"))
    T["bq_col"], T["bk_col"], T["bv_out"] = sb("bq_col", [P, 2]), sb("bk_col", [P, 2]), sb("bv_out", [P, 4])
    T["head_rows"], T["bq_head"] = sb("head_rows", [P, 8]), sb("bq_head", [P, H])
    gate_in, T["gate"] = sb("gate_in", [P, 4]), sb("gate", [P, 4])
    zero = T["zero"] = sb("zero", [P, 4 * D])
    T["x_in"], T["ident_ready"] = nc.alloc_semaphore("x_in"), nc.alloc_semaphore("ident_ready")
    T["weights_in"] = nc.alloc_semaphore("weights_in")
    T["w_in"] = [nc.alloc_semaphore(f"expert_in{s}") for s in range(2)]
    small_in, consts, built = (nc.alloc_semaphore(k) for k in ("small_in", "consts", "built"))
    zero_ready, padded = nc.alloc_semaphore("zero_ready"), nc.alloc_semaphore("padded")
    D_["cleared"], D_["cleared_value"] = nc.alloc_semaphore("cleared"), 16 * 2 * (ROWS // P // 4)
    w_first = [(f"w{k}0", f"w{k}0") for k in "qkv"]
    n0 = len(w_first) + 4
    T["weights_in_value"] = [16 * n0, 16 * (n0 + 4)]

    of_attention = ExitStack()
    for n, w, tiles in ((0, D, 4), (1, 1024, 8)):
        for k in "qkv":
            T[f"w{k}{n}"] = of_attention.enter_context(nc.sbuf_tensor(f"w{k}{n}", [P, DK, w], F32))
        T[f"wo{n}"] = of_attention.enter_context(nc.sbuf_tensor(f"wo{n}", [P, tiles, D], F32))
    early = ExitStack()
    T["w1_0"] = [early.enter_context(nc.sbuf_tensor(f"w1_0_{s}", [P, DK, F0], F32)) for s in range(2)]
    T["w2_0"] = [early.enter_context(nc.sbuf_tensor(f"w2_0_{s}", [P, F0 // P, D], F32)) for s in range(2)]

    with nc.Block() as block:

        @block.sync
        def _(sp):
            sp.dma_start(T["x"][0:S, :], D_["x"]).then_inc(T["x_in"], 16)
            for name, src in w_first:
                sp.dma_start(T[name][:, :, :], D_[src]).then_inc(T["weights_in"], 16)
            sp.wait_ge(zero_ready, 2)
            for j in range(4):
                r = 32 * j + 16 * (j % 2)
                sp.dma_start(T["wo0"][r:r + 16, :, :], D_["wo0"][:, j, :, :]).then_inc(T["weights_in"], 16)
            for k in ("wq1", "wk1", "wv1", "wo1"):
                sp.dma_start(T[k][:, :, :], D_[k]).then_inc(T["weights_in"], 16)
            sp.wait_ge(zero_ready, 3)
            for n in (0, 1):
                X = D_[f"xs{n}"][0:ROWS, :].rearrange("(g p j) d -> g p (j d)", p=P, j=4)
                for g in range(ROWS // P // 4):
                    sp.dma_start(X[g, :, :], zero[:, :]).then_inc(D_["cleared"], 16)
            for s in range(2):
                sp.dma_start(T["w1_0"][s][:, :, :], D_["c_fc"][s, :, :, :]).then_inc(T["w_in"][s], 16)
                sp.dma_start(T["w2_0"][s][:, :, :], D_["c_proj"][s, :, :, :]).then_inc(T["w_in"][s], 16)

        @block.scalar
        def _(act):
            small = [("bq_col", "bq"), ("bk_col", "bk"), ("wr0", "wr0"), ("wr1", "wr1")]
            for name, src in small:
                dst = T[name][:, :, :] if len(T[name].shape) == 3 else T[name][:, :]
                act.dma_start(dst, D_[src]).then_inc(small_in, 16)
            for name in ("bo0", "bo1", "gamma", "beta"):
                act.dma_start(T[name][:, :], D_[name].to_broadcast((P, D))).then_inc(small_in, 16)
            for k in range(4):
                act.dma_start(gate_in[:, k:k + 1], D_["gates"][k:k + 1, :].to_broadcast((P, 1))).then_inc(small_in, 16)
            act.wait_ge(zero_ready, 2)
            for j in range(4):
                r = 32 * j + 16 * (j % 2)
                act.dma_start(T["bv_out"][r:r + 16, :], D_["bv"][:, j, :]).then_inc(small_in, 16)
            act.wait_ge(small_in, 16 * 16)
            nc.scalar.activation(T["gate"][:, :], gate_in[:, :], ACT.Tanh).then_inc(built, 1)

        @block.gpsimd
        def _(pool):
            pool.memset(T["wo0"][:, :, :], 0.0).then_inc(zero_ready, 1)
            pool.memset(T["bv_out"][:, :], 0.0).then_inc(zero_ready, 1)
            pool.memset(zero[:, :], 0.0).then_inc(zero_ready, 1)
            pool.memset(T["ones"][:, :], 1.0).then_inc(consts, 1)
            pool.wait_ge(consts, 1)
            pool.affine_select(out=T["ident"][:, :], in_=T["ones"][:, :], compare_op=ALU.is_equal, fill=0.0, base=0,
                               pattern=[[1, P]], channel_multiplier=-1).then_inc(T["ident_ready"], 1)
            pool.affine_select(out=T["earlier"][:, :], in_=T["ones"][:, :], compare_op=ALU.is_gt, fill=0.0, base=0,
                               pattern=[[1, P]], channel_multiplier=-1).then_inc(consts, 1)
            pool.affine_select(out=T["head_rows"][:, :], in_=T["ones"][:, 0:8], compare_op=ALU.is_ge, fill=0.0, base=0,
                               pattern=[[-16, 8]], channel_multiplier=1).then_inc(consts, 1)
            pool.wait_ge(consts, 3)
            pool.affine_select(out=T["head_rows"][:, :], in_=T["head_rows"][:, :], compare_op=ALU.is_ge, fill=0.0, base=15,
                               pattern=[[16, 8]], channel_multiplier=-1).then_inc(consts, 1)

        @block.vector
        def _(dve):
            dve.wait_ge(small_in, 16 * 16)
            dve.wait_ge(consts, 4)
            for t in range(2):
                nc.vector.tensor_scalar(T["bq_head"][:, 8 * t:8 * t + 8], T["head_rows"][:, :], T["bq_col"][:, t:t + 1],
                                        None, ALU.mult).then_inc(built, 1)

    normalise(nc, T, "n0_", False)
    attention(nc, Layer(0, 16, 0.25), T, D_)
    normalise(nc, T, "n1_", False)
    feed_forward(nc, 0, T, D_, out)
    early.close()
    with ExitStack() as late:
        T["z"] = late.enter_context(nc.sbuf_tensor("z", [P, B * D], F32))
        normalise(nc, T, "n2_", False)
        attention(nc, Layer(1, 64, 1.0 / 16), T, D_)
        normalise(nc, T, "n3_", True)
    of_attention.close()
    feed_forward(nc, 1, T, D_, out)
    ctx.close()


def kernel(**inputs):
    import numpy as np
    import concourse.bacc as bacc
    from concourse import mybir as my
    from concourse.bass_utils import run_bass_kernel_spmd as run

    a = {k: np.asarray(v) for k, v in inputs.items()}

    def rows(w):
        return w.reshape(-1, 128, w.shape[-1]).transpose(1, 0, 2)

    def heads(w):
        return w.transpose(1, 0, 2).reshape(w.shape[1], -1)

    lay = {
        "x": a["x"].transpose(1, 0, 2).reshape(S, B * D),
        "ctx": rows(a["ctx_1024"].reshape(B * L, D).T),
        "mask0": a["mask_Bx1x1xS2_ik0"].reshape(B, L),
        "mask1": a["mask_BxSxS2_bf0"].transpose(1, 0, 2).reshape(S, B * L),
        "gates": np.stack([a["g_xattn"], a["g_ffn"]], 1).reshape(4, 1),
        "wq0": rows(a["L0_xattn_wq"].T), "wk0": rows(a["L0_xattn_wk"].T), "wv0": rows(a["L0_xattn_wv"].T),
        "wo0": a["L0_xattn_wo"].T.reshape(4, 4, 16, D).transpose(2, 1, 0, 3),
        "bq": a["L0_xattn_bq"].reshape(2, 128).T, "bk": a["L0_xattn_bk"].reshape(2, 128).T,
        "bv": a["L0_xattn_bv"].reshape(4, 4, 16).transpose(2, 1, 0),
        "bo0": a["L0_xattn_bo"].reshape(1, D), "bo1": a["L1_xattn_b_o"].reshape(1, D),
        "gamma": a["L1_xattn_gamma"].reshape(1, D), "beta": a["L1_xattn_beta"].reshape(1, D),
        "wr0": rows(a["L0_ffn_w_g"]), "wr1": rows(a["L1_ffn_routing_weights"]),
        "c_fc": a["L0_ffn_c_fc"].reshape(E, DK, 128, F0).transpose(0, 2, 1, 3),
        "c_proj": a["L0_ffn_c_proj"].reshape(E, F0 // 128, 128, D).transpose(0, 2, 1, 3),
        "wq1": rows(heads(a["L1_xattn_w_qs"])), "wk1": rows(heads(a["L1_xattn_w_ks"])),
        "wv1": rows(heads(a["L1_xattn_w_vs"])), "wo1": rows(a["L1_xattn_W_o"].T),
        "W1": a["L1_ffn_W1"].reshape(E, DK, 128, F1).transpose(2, 0, 1, 3).reshape(128, -1),
        "W2": a["L1_ffn_W2"].reshape(E, F1 // 128, 128, D).transpose(2, 0, 1, 3).reshape(128, -1),
        "b1": a["L1_ffn_b1"].reshape(1, E * F1), "b2": a["L1_ffn_b2"].reshape(1, E * D),
    }
    nc = bacc.Bacc("TRN2", target_bir_lowering=False, num_devices=1)
    arrays, dram = {}, {}
    for name, v in lay.items():
        v = np.ascontiguousarray(v)
        arrays[f"in_{name}"] = v
        dram[name] = nc.dram_tensor(f"in_{name}", v.shape, my.dt.from_np(v.dtype), kind="ExternalInput").ap()
    out = nc.dram_tensor("out", (B, S, D), my.dt.from_np(np.dtype("float32")), kind="ExternalOutput").ap()
    gated_two_layers(nc, dram, out)
    return run(nc, [arrays], core_ids=[0]).results[0]["out"]
```

```python
from contextlib import ExitStack

import concourse.bass as bass
from concourse import mybir

F32 = mybir.dt.float32
I32 = mybir.dt.int32
U32 = mybir.dt.uint32
U8 = mybir.dt.uint8
ALU = mybir.AluOpType
ACT = mybir.ActivationFunctionType
AX = mybir.AxisListType

P = 128
B, S, L, D = 16, 100, 361, 256
H = 16
E = 8
DK = D // P
PAIRS = B // 2
KTS = [(k, min(P, L - k)) for k in range(0, L, P)]
KT_N = len(KTS)
SLOTS = 512
CAP = 2 * 5 * B * S // (4 * E)
CAP += CAP % 2
TILES = 32
ROWS = TILES * P
DROP0 = ROWS
F0, F1 = 1024, 512
LN_EPS, Z_EPS = 1e-5, 1e-3
BIG = 3.0e38


class Counted:

    def __init__(self, nc, name, per, pre=0):
        self.sem, self.per, self.pre = nc.alloc_semaphore(name), per, pre

    def credit(self, eng):
        eng.sem_inc(self.sem, self.per)

    def before(self, k):
        return self.per + k

    def at(self, i, k):
        return self.per + self.pre + i * self.per + k


def wait(eng, counted, i, k):
    value = counted.at(i, k)
    if not isinstance(value, int) or value > counted.per:
        eng.wait_ge(counted.sem, value)


class Chain:

    def __init__(self, nc, name):
        self.sem, self.n = nc.alloc_semaphore(name), 0

    def mark(self, ins):
        self.n += 1
        ins.then_inc(self.sem, 1)
        return self.n

    def link(self, eng, ins):
        eng.wait_ge(self.sem, self.mark(ins))


class LoopChain:

    def __init__(self, nc, name, per):
        self.sem, self.per, self.n = nc.alloc_semaphore(name), per, 0

    def begin(self, i):
        self.i, self.n = i, 0

    def mark(self, ins):
        self.n += 1
        ins.then_inc(self.sem, 1)
        return self.i * self.per + self.n

    def link(self, eng, ins):
        eng.wait_ge(self.sem, self.mark(ins))

    def end(self):
        assert self.n == self.per, (self.n, self.per)


class Apart:

    def __init__(self, nc, name):
        self.sems = {eng.engine: nc.alloc_semaphore(f"{name}passed_{k}") for k, eng in
                     (("dve", nc.vector), ("pool", nc.gpsimd), ("sp", nc.sync))}

    def __call__(self, eng):
        eng.sem_inc(self.sems[eng.engine], 1)


class Layer:

    def __init__(self, n, dh, score_scale):
        self.n, self.dh, self.scale = n, dh, score_scale
        self.first = n == 0
        self.width = H * dh
        self.nt = self.width // P
        self.per_tile = P // dh
        self.v_cols = min(self.width, 512)
        self.v_parts = self.width // self.v_cols
        self.pv_rows = 32 if self.first else dh
        self.per_out = P // self.pv_rows
        self.out_tiles = H // self.per_out
        self.groups = self.out_tiles * S // 400


LT, LP = 3, 5
HEADS = 2 * H
N_SLOTS = HEADS + LP + 4
N_SB, N_PB, N_PT = 4, 4, 4


def schedule(layer, last):
    at = [[] for _ in range(N_SLOTS)]
    kv = [("K", t, 0) for t in range(layer.nt)]
    kv += [("V", t, p) for t in range(KT_N) for p in range(layer.v_parts)]
    first = [("Q", 0, t, 0) for t in range(layer.nt)]
    for n, (kind, t, p) in enumerate(kv):
        at[1 + n * (H - 2) // len(kv)].append((kind, 1, t, p))
    if not last:
        begin, end = H + LP + 1, HEADS + LP + 1
        for n, (kind, t, p) in enumerate(kv):
            at[begin + n * (end - begin) // len(kv)].append((kind, 0, t, p))
    for b in range(2):
        at[H * b + H - 1 + LP + 2].append(("W", b, 0, 0))
    units = first + [u for slot in at for u in slot]
    assert last or len(units) % 2 == 0
    owner, count = [], {"A": 0, "D": 0}
    for kind, b, t, p in units:
        if kind == "Q":
            eng = "AD"[t % 2]
        elif kind == "K":
            eng = "D" if layer.first or t % 2 else "A"
        elif kind == "V":
            eng = "AD"[(t + p) % 2] if layer.n else "A"
        else:
            eng = "D"
        count[eng] += 1
        owner.append((eng, count[eng]))
    index, slots = 0, []
    for slot in [first] + at:
        slots.append([(index + n, u) for n, u in enumerate(slot)])
        index += len(slot)
    return slots[0], slots[1:], owner, count, units


def attention(nc, layer, T, D_):
    n = layer.n
    nm = f"a{n}_"
    ctx = ExitStack()

    def sb(name, shape, dt=F32):
        return ctx.enter_context(nc.sbuf_tensor(nm + name, shape, dt))

    cx = [sb(f"context{s}", [P, DK, L]) for s in range(2)]
    kt = [sb(f"keys{s}", [P, layer.nt, L]) for s in range(2)]
    vt = [sb(f"values{s}", [P, KT_N, layer.width]) for s in range(2)]
    qm = sb("queries", [P, H, 2 * S])
    raw = [sb(f"mask_raw{s}", [P, L], I32 if n == 0 else U8) for s in range(2)]
    bias = [sb(f"mask_bias{s}", [P, L]) for s in range(2)]
    keep = [sb(f"mask_keep{s}", [P, L]) for s in range(2)] if n == 0 else None
    masked = sb("masked", [P, N_SB, L])
    low = sb("low", [P, N_SB])
    prob = sb("prob", [P, N_PB, L])
    total = sb("total", [P, N_PB])
    inv = sb("inv", [P, N_PB])
    pt = sb("prob_t", [P, N_PT, KT_N * S])
    ot = [sb(f"out_t{s}", [P, layer.out_tiles, S]) for s in range(2)]
    lin = sb("lin", [P, 2, D])
    ps_s = [ctx.enter_context(nc.psum_tensor(f"{nm}ps_s{k}", [P, 512], F32)) for k in range(2)]
    ps_t = [ctx.enter_context(nc.psum_tensor(f"{nm}ps_t{k}", [P, 512], F32)) for k in range(2)]
    ps_o = [ctx.enter_context(nc.psum_tensor(f"{nm}ps_o{k}", [P, 512], F32)) for k in range(2)]
    ps_p = [ctx.enter_context(nc.psum_tensor(f"{nm}ps_p{k}", [P, 512], F32)) for k in range(2)]

    full, lastly = schedule(layer, False), schedule(layer, True)
    n_units = len(full[4])
    pre_units = [("K", 0, t, 0) for t in range(layer.nt)]
    pre_units += [("V", 0, t, p) for t in range(KT_N) for p in range(layer.v_parts)]
    pre_owner, pre_count = [], {"A": 0, "D": 0}
    for kind, b, t, p in pre_units:
        eng = "D" if kind == "K" and n == 0 else "A"
        pre_count[eng] += 1
        pre_owner.append((eng, pre_count[eng]))

    groups = 2 * layer.groups
    scored = Counted(nc, nm + "scored", HEADS)
    maxed = Counted(nc, nm + "maxed", HEADS)
    exped = Counted(nc, nm + "exped", HEADS)
    inverted = Counted(nc, nm + "inverted", HEADS)
    normed = Counted(nc, nm + "normed", HEADS)
    turned = Counted(nc, nm + "turned", HEADS)
    pt_ready = Counted(nc, nm + "pt_ready", HEADS)
    valued = Counted(nc, nm + "valued", HEADS)
    out_ready = Counted(nc, nm + "out_ready", groups)
    unit_done = Counted(nc, nm + "unit_done", n_units, len(pre_units))
    taken = {"A": Counted(nc, nm + "taken_act", full[3]["A"], pre_count["A"]),
             "D": Counted(nc, nm + "taken_dve", full[3]["D"], pre_count["D"])}
    loaded = [nc.alloc_semaphore(f"{nm}loaded{s}") for s in range(2)]
    kept = [nc.alloc_semaphore(f"{nm}kept{s}") for s in range(2)]
    biased = [nc.alloc_semaphore(f"{nm}biased{s}") for s in range(2)]
    zeroed = nc.alloc_semaphore(nm + "zeroed")
    dve_own = LoopChain(nc, nm + "dve_own", 4)
    apart = Apart(nc, nm)
    LOADS = 2 * 16

    def body(sched):
        return sched[0], sched[1], sched[2]

    with nc.Block() as block:

        @block.sync
        def _(sp):
            def load(batch, s):
                apart(sp)
                if n == 0:
                    mask = D_["mask0"][bass.ds(batch, 1), :].to_broadcast((P, L))
                    dst = raw[s][:, :]
                else:
                    mask = D_["mask1"][:, bass.ds(batch * L, L)]
                    dst = raw[s][0:S, :]
                sp.dma_start(cx[s][:, :, :], D_["ctx"][:, :, bass.ds(batch * L, L)]).then_inc(loaded[s], 16)
                sp.dma_start(dst, mask).then_inc(loaded[s], 16)

            load(0, 0)
            load(1, 1)
            with sp.Fori(0, PAIRS - 1) as i:
                sp.wait_ge(unit_done.sem, unit_done.at(i, 0))
                apart(sp)
                sp.wait_ge(biased[0], i + 1)
                load(2 * i + 2, 0)
                last_kv1 = max(k for slot in full[1] for k, u in slot if u[0] in "KV" and u[1] == 1)
                sp.wait_ge(unit_done.sem, unit_done.at(i, last_kv1 + 1))
                apart(sp)
                sp.wait_ge(biased[1], i + 1)
                load(2 * i + 3, 1)

        @block.gpsimd
        def _(pool):
            if n == 1:
                nc.gpsimd.memset(qm[:, :, :], 0.0).then_inc(zeroed, 1)

            masked_value = -1.0e9 / layer.scale

            def convert(s, nth, before):
                pool.wait_ge(loaded[s], LOADS * nth)
                if before is not None:
                    pool.wait_ge(maxed.sem, before)
                apart(pool)
                if n == 0:
                    nc.gpsimd.tensor_scalar(bias[s][:, :], raw[s][:, :], 0.0, masked_value, ALU.is_equal,
                                            ALU.mult).then_inc(biased[s], 1)
                    pool.wait_ge(biased[s], nth)
                    apart(pool)
                    nc.gpsimd.tensor_scalar(keep[s][:, :], bias[s][:, :], 0.0, None, ALU.is_equal).then_inc(kept[s], 1)
                else:
                    nc.gpsimd.tensor_scalar(bias[s][0:S, :], raw[s][0:S, :], -BIG, 10.0, ALU.mult,
                                            ALU.mult).then_inc(biased[s], 1)

            convert(0, 1, None)
            convert(1, 1, None)
            with pool.Fori(0, PAIRS - 1) as i:
                convert(0, i + 2, maxed.at(i, H))
                convert(1, i + 2, maxed.at(i, HEADS))

        @block.tensor
        def _(pe):
            def project(u, unit, owner, i, pre):
                kind, s, t, p = unit
                bank = ps_p[u % 2]
                if pre:
                    if u >= 2:
                        eng, k = pre_owner[u - 2]
                        pe.wait_ge(taken[eng].sem, taken[eng].before(k))
                elif u >= 2:
                    eng, k = owner[u - 2]
                    pe.wait_ge(taken[eng].sem, taken[eng].at(i, k))
                else:
                    eng, k = full[2][n_units + u - 2]
                    pe.wait_ge(taken[eng].sem, taken[eng].at(i, k - taken[eng].per))
                if kind in "KV":
                    pe.wait_ge(loaded[s], LOADS if pre else (i + 2 - s) * LOADS)
                if kind == "Q":
                    for k in range(DK):
                        ins = nc.tensor.matmul(bank[:, 0:2 * S], T[f"wq{n}"][:, k, t * P:(t + 1) * P],
                                               T["xn_t"][:, k, bass.ds(i * 2 * S, 2 * S)],
                                               start=k == 0, stop=k == DK - 1)
                elif kind == "K":
                    for k in range(DK):
                        ins = nc.tensor.matmul(bank[:, 0:L], T[f"wk{n}"][:, k, t * P:(t + 1) * P],
                                               cx[s][:, k, :], start=k == 0, stop=k == DK - 1)
                elif kind == "V":
                    k0, kn = KTS[t]
                    w = layer.v_cols
                    for k in range(DK):
                        ins = nc.tensor.matmul(bank[0:kn, 0:w], cx[s][:, k, k0:k0 + kn],
                                               T[f"wv{n}"][:, k, p * w:(p + 1) * w],
                                               start=k == 0, stop=k == DK - 1)
                else:
                    pe.wait_ge(out_ready.sem, out_ready.at(i, layer.groups * (s + 1)))
                    for k in range(layer.out_tiles):
                        ins = nc.tensor.matmul(bank[0:S, 0:D], ot[s][:, k, :], T[f"wo{n}"][:, k, :],
                                               start=k == 0, stop=k == layer.out_tiles - 1)
                ins.then_inc(unit_done.sem, 1)

            def heads(i, sched):
                first, slots, owner = body(sched)
                for u, unit in first:
                    project(u, unit, owner, i, False)
                of_slot = {s: [x for slot in slots for x in slot if x[1][1] == s and x[1][0] in "KV"] for s in (0, 1)}
                for g in range(N_SLOTS):
                    if g < HEADS:
                        b, h = g // H, g % H
                        if g == 0:
                            for eng in "AD":
                                q = max([owner[u][1] for u, x in first if owner[u][0] == eng])
                                pe.wait_ge(taken[eng].sem, taken[eng].at(i, q))
                        if g == H:
                            for eng in "AD":
                                k1 = [owner[u][1] for u, x in of_slot[1] if owner[u][0] == eng]
                                if k1:
                                    pe.wait_ge(taken[eng].sem, taken[eng].at(i, max(k1)))
                        pe.wait_ge(maxed.sem, maxed.at(i, g - 1))
                        nc.tensor.matmul(ps_s[g % 2][0:S, 0:L], qm[:, h, b * S:(b + 1) * S],
                                         kt[b][:, h // layer.per_tile, :], start=True, stop=True).then_inc(scored.sem, 1)
                    for u, unit in slots[g]:
                        project(u, unit, owner, i, False)
                    t = g - LT
                    if 0 <= t < HEADS:
                        pe.wait_ge(normed.sem, normed.at(i, t + 1))
                        pe.wait_ge(pt_ready.sem, pt_ready.at(i, t - 1))
                        for c, (k0, kn) in enumerate(KTS):
                            ins = nc.tensor.transpose(ps_t[t % 2][0:kn, c * S:(c + 1) * S],
                                                      prob[0:S, t % N_PB, k0:k0 + kn], T["ident"][0:S, 0:S])
                        ins.then_inc(turned.sem, 1)
                    v = g - LP
                    if 0 <= v < HEADS:
                        b, h = v // H, v % H
                        per_group = H // layer.groups
                        group = v // per_group
                        pe.wait_ge(pt_ready.sem, pt_ready.at(i, v + 1))
                        if v % per_group == 0:
                            pe.wait_ge(out_ready.sem, out_ready.at(i, group - 1))
                        w = layer.pv_rows
                        row = h % layer.per_out * w
                        col = (h // layer.per_out * S) % 400
                        v0 = (h // 2 * 32) if n == 0 else h * w
                        for c, (k0, kn) in enumerate(KTS):
                            ins = nc.tensor.matmul(ps_o[group % 2][row:row + w, col:col + S],
                                                   vt[b][0:kn, c, v0:v0 + w], pt[0:kn, v % N_PT, c * S:(c + 1) * S],
                                                   start=c == 0, stop=c == KT_N - 1)
                        ins.then_inc(valued.sem, 1)

            for k in (scored, turned, valued, unit_done):
                k.credit(pe)
            pe.wait_ge(T["weights_in"], T["weights_in_value"][n])
            for u, unit in enumerate(pre_units):
                project(u, unit, pre_owner, 0, True)
            for eng in "AD":
                if pre_count[eng]:
                    pe.wait_ge(taken[eng].sem, taken[eng].before(pre_count[eng]))
            with pe.Fori(0, PAIRS - 1) as i:
                heads(i, full)
            heads(PAIRS - 1, lastly)

        def take(eng, nce, me, u, unit, i, pre):
            kind, s, t, p = unit
            bank = ps_p[u % 2]
            eng.wait_ge(unit_done.sem, unit_done.before(u + 1) if pre else unit_done.at(i, u + 1))
            act = me == "A"
            if kind == "Q":
                eng.wait_ge(scored.sem, scored.at(i, 0))
                if n == 0:
                    for j in range(layer.per_tile):
                        h = t * layer.per_tile + j
                        args = (qm[:, h, :], bank[:, 0:2 * S])
                        if act:
                            ins = nc.scalar.activation(*args, ACT.Identity, scale=T["head_rows"][:, j:j + 1],
                                                       bias=T["bq_head"][:, h:h + 1])
                        else:
                            ins = nc.vector.tensor_scalar(*args, T["head_rows"][:, j:j + 1],
                                                          T["bq_head"][:, h:h + 1], ALU.mult, ALU.add)
                else:
                    if not pre:
                        eng.wait_ge(zeroed, 1)
                    for j in range(2):
                        r = slice(64 * j, 64 * j + 64)
                        args = (qm[r, 2 * t + j, :], bank[r, 0:2 * S])
                        ins = nc.scalar.copy(*args) if act else nc.vector.tensor_copy(*args)
            elif kind == "K":
                if not pre:
                    eng.wait_ge(scored.sem, scored.at(i, 0 if s == 1 else H))
                if n == 0:
                    eng.wait_ge(kept[s], 1 if pre else i + 2 - s)
                    ins = nc.vector.scalar_tensor_tensor(kt[s][:, t, :], bank[:, 0:L], T["bk_col"][:, t:t + 1],
                                                         keep[s][:, :], ALU.add, ALU.mult)
                else:
                    args = (kt[s][:, t, :], bank[:, 0:L])
                    ins = nc.scalar.copy(*args) if act else nc.vector.tensor_copy(*args)
            elif kind == "V":
                if not pre:
                    eng.wait_ge(valued.sem, valued.at(i, 0 if s == 1 else H))
                kn, w = KTS[t][1], layer.v_cols
                args = (vt[s][0:kn, t, p * w:(p + 1) * w], bank[0:kn, 0:w])
                ins = nc.scalar.copy(*args) if act else nc.vector.tensor_copy(*args)
            else:
                x = T["x"][0:S, bass.ds((2 * i + s) * D, D)]
                dve_own.link(eng, nc.vector.tensor_tensor(lin[0:S, s, :], bank[0:S, 0:D], T[f"bo{n}"][0:S, :], ALU.add))
                if n == 0:
                    row = x
                    dve_own.link(eng, nc.vector.scalar_tensor_tensor(x, lin[0:S, s, :], T["gate"][0:S, 0:1], x,
                                                                     ALU.mult, ALU.add))
                else:
                    row = T["xn"][0:S, bass.ds((2 * i + s) * D, D)]
                    nc.vector.tensor_tensor(x, x, T["beta"][0:S, :], ALU.add)
                    dve_own.link(eng, nc.vector.tensor_tensor(row, lin[0:S, s, :], row, ALU.add))
                ins = nc.vector.bn_stats(T["stats"][0:S, bass.ds((2 * i + s) * 6, 6)], row)
            ins.then_inc(taken[me].sem, 1)

        def take_before(eng, nce, me):
            for u, unit in enumerate(pre_units):
                if pre_owner[u][0] == me:
                    take(eng, nce, me, u, unit, 0, True)

        @block.scalar
        def _(act):
            def heads(i, sched):
                first, slots, owner = body(sched)
                for u, unit in first:
                    if owner[u][0] == "A":
                        take(act, nc.scalar, "A", u, unit, i, False)
                for g in range(N_SLOTS):
                    t = g - LT
                    if 0 <= t < HEADS:
                        act.wait_ge(turned.sem, turned.at(i, t + 1))
                        act.wait_ge(valued.sem, valued.at(i, t + 1 - N_PT))
                        kl = KTS[-1][1]
                        nc.scalar.copy(pt[0:P, t % N_PT, 0:(KT_N - 1) * S], ps_t[t % 2][0:P, 0:(KT_N - 1) * S])
                        nc.scalar.copy(pt[0:kl, t % N_PT, (KT_N - 1) * S:KT_N * S],
                                       ps_t[t % 2][0:kl, (KT_N - 1) * S:KT_N * S]).then_inc(pt_ready.sem, 1)
                    if g < HEADS:
                        act.wait_ge(maxed.sem, maxed.at(i, g + 1))
                        act.wait_ge(turned.sem, turned.at(i, g + 1 - N_PB))
                        nc.scalar.activation(prob[0:S, g % N_PB, :], masked[0:S, g % N_SB, :], ACT.Exp,
                                             bias=low[0:S, g % N_SB:g % N_SB + 1], scale=-1.0,
                                             accum_out=total[0:S, g % N_PB:g % N_PB + 1]).then_inc(exped.sem, 1)
                    for u, unit in slots[g]:
                        if owner[u][0] == "A":
                            take(act, nc.scalar, "A", u, unit, i, False)

            for k in (exped, pt_ready, taken["A"]):
                k.credit(act)
            take_before(act, nc.scalar, "A")
            with act.Fori(0, PAIRS - 1) as i:
                heads(i, full)
            heads(PAIRS - 1, lastly)

        @block.vector
        def _(dve):
            def heads(i, sched):
                first, slots, owner = body(sched)
                dve_own.begin(i)
                for u, unit in first:
                    if owner[u][0] == "D":
                        take(dve, nc.vector, "D", u, unit, i, False)
                for g in range(N_SLOTS):
                    if g < HEADS:
                        s = g // H
                        if g % H == 0:
                            dve.wait_ge(biased[s], i + 1)
                        dve.wait_ge(scored.sem, scored.at(i, g + 1))
                        dve.wait_ge(exped.sem, exped.at(i, g + 1 - N_SB))
                        apart(dve)
                        nc.vector.tensor_tensor_reduce(out=masked[0:S, g % N_SB, :], in0=ps_s[g % 2][0:S, 0:L],
                                                       in1=bias[s][0:S, :], scale=-layer.scale, scalar=BIG,
                                                       op0=ALU.add, op1=ALU.min,
                                                       accum_out=low[0:S, g % N_SB:g % N_SB + 1]).then_inc(maxed.sem, 1)
                    for u, unit in slots[g]:
                        if owner[u][0] == "D":
                            take(dve, nc.vector, "D", u, unit, i, False)
                    r = g - 1
                    if 0 <= r < HEADS:
                        k = r % N_PB
                        dve.wait_ge(exped.sem, exped.at(i, r + 1))
                        nc.vector.reciprocal(inv[0:S, k:k + 1], total[0:S, k:k + 1]).then_inc(inverted.sem, 1)
                        dve.wait_ge(inverted.sem, inverted.at(i, r + 1))
                        nc.vector.tensor_scalar(prob[0:S, k, :], prob[0:S, k, :], inv[0:S, k:k + 1], None,
                                                ALU.mult).then_inc(normed.sem, 1)
                    v = g - LP - 1
                    per_group = H // layer.groups
                    if 0 <= v < HEADS and v % per_group == per_group - 1:
                        group = v // per_group
                        b, half = v // H, group % layer.groups
                        dve.wait_ge(valued.sem, valued.at(i, v + 1))
                        w_unit = [u for slot in full[1] for u, x in slot if x[0] == "W" and x[1] == b][0]
                        dve.wait_ge(unit_done.sem, unit_done.at(i, w_unit + 1 - n_units))
                        dst = ot[b][:, half * 4:half * 4 + 4, :]
                        src = ps_o[group % 2][:, 0:4 * S].rearrange("p (t s) -> p t s", t=4)
                        if n == 0:
                            bv = T["bv_out"][:, :].unsqueeze(2).to_broadcast((P, 4, S))
                            ins = nc.vector.tensor_tensor(dst, src, bv, ALU.add)
                        else:
                            ins = nc.vector.tensor_copy(dst, src)
                        ins.then_inc(out_ready.sem, 1)
                dve_own.end()

            for k in (maxed, inverted, normed, out_ready, taken["D"]):
                k.credit(dve)
            take_before(dve, nc.vector, "D")
            with dve.Fori(0, PAIRS - 1) as i:
                heads(i, full)
            heads(PAIRS - 1, lastly)

    ctx.close()


class Norm:

    GROUPS, PER = 4, 4

    def __init__(self, nc, T, nm, ctx, banks):
        self.nc, self.T, self.banks = nc, T, banks
        self.mv = ctx.enter_context(nc.sbuf_tensor(nm + "mv", [P, B, 2], F32))
        self.dev = ctx.enter_context(nc.sbuf_tensor(nm + "dev", [P, 2, B], F32))
        self.rs = ctx.enter_context(nc.sbuf_tensor(nm + "rs", [P, B], F32))
        self.shift = ctx.enter_context(nc.sbuf_tensor(nm + "shift", [P, B], F32))
        self.own = Chain(nc, nm + "norm_own")
        self.var_ready = nc.alloc_semaphore(nm + "var_ready")
        self.root_ready = nc.alloc_semaphore(nm + "root_ready")
        self.shift_ready = nc.alloc_semaphore(nm + "shift_ready")
        self.normed = nc.alloc_semaphore(nm + "normed")
        self.turned = nc.alloc_semaphore(nm + "turned")
        self.turns = 0

    def moments(self, dve, q, x=None):
        nc, T = self.nc, self.T
        r = range(q * self.PER, (q + 1) * self.PER)
        if x is not None:
            for b in r:
                last = self.own.mark(nc.vector.bn_stats(T["stats"][0:S, b * 6:b * 6 + 6], x[0:S, b * D:(b + 1) * D]))
            dve.wait_ge(self.own.sem, last)
        for b in r:
            last = self.own.mark(nc.vector.bn_aggr(self.mv[0:S, b, :], T["stats"][0:S, b * 6:b * 6 + 6]))
        dve.wait_ge(self.own.sem, last)

    def scales(self, dve, q, nth, factor, eps, eps_after):
        nc, g = self.nc, slice(q * self.PER, (q + 1) * self.PER)
        nc.vector.tensor_scalar(self.dev[0:S, 0, g], self.mv[0:S, g, 1], factor, eps, ALU.mult,
                                ALU.add).then_inc(self.var_ready, 1)
        dve.wait_ge(self.root_ready, nth + 1)
        self.own.link(dve, nc.vector.tensor_scalar(self.rs[0:S, g], self.dev[0:S, 1, g], eps_after, None, ALU.add))
        self.own.link(dve, nc.vector.reciprocal(self.rs[0:S, g], self.rs[0:S, g]))
        nc.vector.scalar_tensor_tensor(self.shift[0:S, g], self.mv[0:S, g, 0], -1.0, self.rs[0:S, g], ALU.mult,
                                       ALU.mult).then_inc(self.shift_ready, 1)

    def roots(self, act, q, nth):
        g = slice(q * self.PER, (q + 1) * self.PER)
        act.wait_ge(self.var_ready, nth + 1)
        self.nc.scalar.activation(self.dev[0:S, 1, g], self.dev[0:S, 0, g], ACT.Sqrt).then_inc(self.root_ready, 1)

    def apply(self, act, q, nth, src, dst):
        act.wait_ge(self.shift_ready, nth + 1)
        for b in range(q * self.PER, (q + 1) * self.PER):
            c = slice(b * D, (b + 1) * D)
            ins = self.nc.scalar.activation(dst[0:S, c], src[0:S, c], ACT.Identity, scale=self.rs[0:S, b:b + 1],
                                            bias=self.shift[0:S, b:b + 1])
        ins.then_inc(self.normed, 1)

    def turn(self, pe, q, nth):
        nc, T = self.nc, self.T
        pe.wait_ge(self.normed, nth)
        for k in range(DK):
            for j in range(self.PER):
                c = (q * self.PER + j) * D + k * P
                ins = nc.tensor.transpose(self.banks[q * DK + k][:, j * S:(j + 1) * S], T["xn"][0:S, c:c + P],
                                          T["ident"][0:S, 0:S])
            ins.then_inc(self.turned, 1)

    def keep(self, eng, copy, q, k):
        eng.wait_ge(self.turned, q * DK + k + 1)
        w = self.PER * S
        return copy(self.T["xn_t"][:, k, q * w:(q + 1) * w], self.banks[q * DK + k][:, 0:w])


def normalise(nc, T, nm, z_first, from_x):
    with ExitStack() as ctx:
        banks = [ctx.enter_context(nc.psum_tensor(f"{nm}bank{k}", [P, 512], F32)) for k in range(8)]
        norm = Norm(nc, T, nm, ctx, banks)
        q_all = range(Norm.GROUPS)
        n_z = Norm.GROUPS if z_first else 0

        with nc.Block() as block:

            @block.vector
            def _(dve):
                if from_x:
                    dve.wait_ge(T["x_in"], 16)
                if z_first:
                    for q in q_all:
                        norm.moments(dve, q)
                        norm.scales(dve, q, q, D / (D - 1.0), 0.0, Z_EPS)
                for q in q_all:
                    if z_first:
                        c = slice(q * 4 * D, (q + 1) * 4 * D)
                        z = T["xn"][0:S, c]
                        z3 = z.rearrange("p (b d) -> p b d", b=4)
                        dve.wait_ge(norm.normed, q + 1)
                        norm.own.link(dve, nc.vector.tensor_tensor(
                            z3, z3, T["gamma"][0:S, :].unsqueeze(1).to_broadcast((S, 4, D)), ALU.mult))
                        norm.own.link(dve, nc.vector.tensor_tensor(T["x"][0:S, c], T["x"][0:S, c], z, ALU.add))
                    norm.moments(dve, q, T["x"] if from_x or z_first else None)
                    norm.scales(dve, q, n_z + q, 1.0, LN_EPS, 0.0)
                for q in q_all:
                    norm.keep(dve, nc.vector.tensor_copy, q, 1)

            @block.scalar
            def _(act):
                if z_first:
                    for q in q_all:
                        norm.roots(act, q, q)
                        norm.apply(act, q, q, T["xn"], T["xn"])
                for q in q_all:
                    norm.roots(act, q, n_z + q)
                    norm.apply(act, q, n_z + q, T["x"], T["xn"])
                    if q:
                        norm.keep(act, nc.scalar.copy, q - 1, 0)
                norm.keep(act, nc.scalar.copy, Norm.GROUPS - 1, 0)

            @block.tensor
            def _(pe):
                pe.wait_ge(T["ident_ready"], 1)
                for q in q_all:
                    norm.turn(pe, q, n_z + q + 1)


def feed_forward(nc, n, T, D_, out):
    nm = f"f{n}_"
    ctx = ExitStack()

    def sb(name, shape, dt=F32):
        return ctx.enter_context(nc.sbuf_tensor(nm + name, shape, dt))

    logits, top, ex = sb("logits", [P, B, E]), sb("top", [P, B, E]), sb("ex", [P, B, E])
    idx, chosen = sb("idx", [P, B, E], U32), sb("chosen", [P, 2, B])
    weight = sb("weight", [P, 2, B])
    denom = sb("denom", [P, B])
    hot = sb("hot", [P, 2, B, E])
    tot = sb("tot", [P, 2, B, E])
    run = [sb(f"run{k}", [P, 2, B, E]) for k in range(2)]
    rank = sb("rank", [P, 2, B, E])
    picked = sb("picked", [P, 2, B])
    slot, row, valid = sb("slot", [P, 2, B]), sb("row", [P, 2, B]), sb("valid", [P, 2, B])
    scat, gath = sb("scat", [P, 2, B], U32), sb("gath", [P, 2, B], U32)
    drop_row = sb("drop_row", [P, 2, B])
    need, need_i, ends = sb("need", [P, E]), sb("need_i", [P, E], I32), [sb(f"ends{k}", [P, E]) for k in range(2)]
    step = sb("step", [P, TILES])
    before = sb("before", [P, TILES, E])
    owner_f, owner_i = sb("owner_f", [P, TILES]), sb("owner_i", [P, TILES], I32)
    NG = 4
    got = [[sb(f"got{k}_{s}", [P, D]) for s in range(NG)] for k in range(2)]
    ps = [ctx.enter_context(nc.psum_tensor(f"{nm}ps{k}", [P, 512], F32)) for k in range(8)]

    logits_done, hot_ready, ranked = (nc.alloc_semaphore(nm + k) for k in ("logits_done", "hot_ready", "ranked"))
    diff_ready, ex_ready = nc.alloc_semaphore(nm + "diff_ready"), nc.alloc_semaphore(nm + "ex_ready")
    rows_ready, dispatched = nc.alloc_semaphore(nm + "rows_ready"), nc.alloc_semaphore(nm + "dispatched")
    iotas = nc.alloc_semaphore(nm + "iotas")
    stored = nc.alloc_semaphore(nm + "stored")
    gathered = [nc.alloc_semaphore(f"{nm}gathered{s}") for s in range(NG)]
    added = nc.alloc_semaphore(nm + "added")
    out_done = nc.alloc_semaphore(nm + "out_done")
    own = Chain(nc, nm + "own")
    apart = Apart(nc, nm)
    XS, YS = D_[f"xs{n}"], D_[f"ys{n}"]

    def route(dve):
        v = nc.vector
        dve.wait_ge(logits_done, 1)
        own.link(dve, v.tensor_copy(logits[0:S, :, :].rearrange("p b e -> p (b e)"), ps[0][0:S, 0:B * E]))
        for b in range(B):
            last = own.mark(v.max(top[0:S, b, :], logits[0:S, b, :]))
        dve.wait_ge(own.sem, last)
        for b in range(B):
            last = own.mark(v.max_index(idx[0:S, b, :], top[0:S, b, :], logits[0:S, b, :]))
        v.tensor_tensor(ex[0:S, :, :], top[0:S, :, :], top[0:S, :, 0:1].to_broadcast((S, B, E)),
                        ALU.subtract).then_inc(diff_ready, 1)
        dve.wait_ge(own.sem, last)
        own.link(dve, v.tensor_copy(chosen[0:S, :, :].rearrange("p k b -> p b k"), idx[0:S, :, 0:2]))
        dve.wait_ge(iotas, 3)
        shape = (S, 2, B, E)
        for k in range(2):
            ins = v.tensor_tensor(hot[0:S, k, :, :], T["experts"][0:S, :].unsqueeze(1).to_broadcast((S, B, E)),
                                  chosen[0:S, k, :].unsqueeze(2).to_broadcast((S, B, E)), ALU.is_equal)
            ins.then_inc(hot_ready, 1)
        dve.wait_ge(ex_ready, 1)
        own.link(dve, v.tensor_reduce(denom[0:S, :], ex[0:S, :, 0:(2 if n == 0 else E)], AX.X, ALU.add))
        own.link(dve, v.reciprocal(denom[0:S, :], denom[0:S, :]))
        own.link(dve, v.tensor_scalar(weight[0:S, 0, :], denom[0:S, :], T["gate"][0:S, 2 * n + 1:2 * n + 2], None, ALU.mult))
        own.link(dve, v.tensor_tensor(weight[0:S, 1, :], weight[0:S, 0, :], ex[0:S, :, 1], ALU.mult))
        dve.wait_ge(ranked, 1)
        flat = "p k b e -> p (k b e)"
        own.link(dve, v.tensor_copy(tot[0:S, :, :, :].rearrange(flat), ps[2][0:S, 0:2 * B * E]))
        own.link(dve, v.tensor_copy(run[0][0:S, :, :, :].rearrange(flat), ps[2][0:S, 0:2 * B * E]))
        a = 0
        for d in (1, 2, 4, 8):
            src, dst = run[a], run[1 - a]
            own.mark(v.tensor_copy(dst[0:S, :, 0:d, :], src[0:S, :, 0:d, :]))
            for k in range(2):
                last = own.mark(v.tensor_tensor(dst[0:S, k, d:B, :], src[0:S, k, d:B, :], src[0:S, k, 0:B - d, :], ALU.add))
            dve.wait_ge(own.sem, last)
            a = 1 - a
        run_t = run[a]
        own.link(dve, v.tensor_tensor(rank[0:S, :, :, :].rearrange(flat), ps[1][0:S, 0:2 * B * E],
                                      run_t[0:S, :, :, :].rearrange(flat), ALU.add))
        own.link(dve, v.tensor_tensor(rank[0:S, :, :, :].rearrange(flat), rank[0:S, :, :, :].rearrange(flat),
                                      tot[0:S, :, :, :].rearrange(flat), ALU.subtract))
        own.link(dve, v.tensor_tensor(rank[0:S, 1, :, :], rank[0:S, 1, :, :],
                                      run_t[0:S, 0, B - 1:B, :].to_broadcast((S, B, E)), ALU.add))
        if n == 1:
            own.link(dve, v.tensor_tensor(need[0:S, :], run_t[0:S, 0, B - 1, :], run_t[0:S, 1, B - 1, :], ALU.add))
            own.link(dve, v.tensor_scalar(need_i[0:S, :], need[0:S, :], float(P - 1), None, ALU.add))
            own.link(dve, v.tensor_scalar(need_i[0:S, :], need_i[0:S, :], 7, None, ALU.arith_shift_right))
            own.link(dve, v.tensor_copy(need[0:S, :], need_i[0:S, :]))
            own.link(dve, v.tensor_copy(ends[0][0:S, :], need_i[0:S, :]))
            a = 0
            for d in (1, 2, 4):
                own.mark(v.tensor_copy(ends[1 - a][0:S, 0:d], ends[a][0:S, 0:d]))
                own.link(dve, v.tensor_tensor(ends[1 - a][0:S, d:E], ends[a][0:S, d:E], ends[a][0:S, 0:E - d], ALU.add))
                a = 1 - a
            end = ends[a]
            own.link(dve, v.tensor_tensor(before[0:S, :, :], end[0:S, :].unsqueeze(1).to_broadcast((S, TILES, E)),
                                          step[0:S, :].unsqueeze(2).to_broadcast((S, TILES, E)), ALU.is_le))
            own.link(dve, v.tensor_reduce(owner_f[0:S, :], before[0:S, :, :], AX.X, ALU.add))
            own.link(dve, v.tensor_scalar(owner_i[0:S, :], owner_f[0:S, :], float(E - 1), None, ALU.min))
            own.link(dve, v.tensor_tensor(need[0:S, :], end[0:S, :], need[0:S, :], ALU.subtract))
            own.link(dve, v.tensor_scalar(need[0:S, :], need[0:S, :], float(P), None, ALU.mult))
            for k in range(2):
                last = own.mark(v.tensor_tensor(rank[0:S, k, :, :], rank[0:S, k, :, :],
                                                need[0:S, :].unsqueeze(1).to_broadcast((S, B, E)), ALU.add))
            dve.wait_ge(own.sem, last)
        own.link(dve, v.tensor_tensor(rank[0:S, :, :, :].rearrange(flat), rank[0:S, :, :, :].rearrange(flat),
                                      hot[0:S, :, :, :].rearrange(flat), ALU.mult))
        own.link(dve, v.tensor_reduce(picked[0:S, :, :], rank[0:S, :, :, :], AX.X, ALU.add))
        if n == 0:
            own.link(dve, v.tensor_scalar(valid[0:S, :, :], picked[0:S, :, :], float(CAP), None, ALU.is_lt))
            own.link(dve, v.scalar_tensor_tensor(slot[0:S, :, :], chosen[0:S, :, :], float(SLOTS), picked[0:S, :, :],
                                                 ALU.mult, ALU.add))
            own.link(dve, v.tensor_tensor(weight[0:S, :, :], weight[0:S, :, :], valid[0:S, :, :], ALU.mult))
            own.link(dve, v.tensor_tensor(row[0:S, :, :], slot[0:S, :, :], drop_row[0:S, :, :], ALU.subtract))
            own.link(dve, v.tensor_tensor(row[0:S, :, :], row[0:S, :, :], valid[0:S, :, :], ALU.mult))
            own.link(dve, v.tensor_tensor(scat[0:S, :, :], row[0:S, :, :], drop_row[0:S, :, :], ALU.add))
            own.link(dve, v.tensor_tensor(gath[0:S, :, :], slot[0:S, :, :], valid[0:S, :, :], ALU.mult))
        else:
            own.link(dve, v.tensor_copy(scat[0:S, :, :], picked[0:S, :, :]))
            own.link(dve, v.tensor_copy(gath[0:S, :, :], picked[0:S, :, :]))
        dve.sem_inc(rows_ready, 1)

    def pool_dispatch(pool):
        pool.iota(drop_row[0:S, :, :], pattern=[[B * S, 2], [S, B]], base=DROP0, channel_multiplier=1,
                  allow_small_or_imprecise_dtypes=True).then_inc(iotas, 1)
        pool.iota(step[0:S, :], pattern=[[1, TILES]], base=0, channel_multiplier=0,
                  allow_small_or_imprecise_dtypes=True).then_inc(iotas, 1)
        pool.iota(T["experts"][0:S, :], pattern=[[1, E]], base=0, channel_multiplier=0,
                  allow_small_or_imprecise_dtypes=True).then_inc(iotas, 1)
        pool.wait_ge(D_["cleared"], D_["cleared_value"])
        pool.wait_ge(rows_ready, 1)
        for k in range(2):
            for b in range(B):
                pool.indirect_dma_start(out=XS[:, :], out_offset=bass.IndirectOffsetOnAxis(ap=scat[0:S, k, b:b + 1], axis=0),
                                        in_=T["xn"][0:S, b * D:(b + 1) * D], in_offset=None).then_inc(dispatched, 16)

    def pool_gather(pool, stores):
        pool.wait_ge(stored, 16 * stores)
        for b in range(B):
            s = b % NG
            if b >= NG:
                pool.wait_ge(added, b - NG + 1)
            for k in range(2):
                pool.indirect_dma_start(out=got[k][s][0:S, :], out_offset=None, in_=YS[:, :],
                                        in_offset=bass.IndirectOffsetOnAxis(ap=gath[0:S, k, b:b + 1], axis=0)).then_inc(gathered[s], 16)

    norm = Norm(nc, T, nm, ctx, ps) if n == 0 else None

    def combine(dve):
        for b in range(B):
            s = b % NG
            dve.wait_ge(gathered[s], 32 * (b // NG + 1))
            x = T["x"][0:S, b * D:(b + 1) * D]
            own.link(dve, nc.vector.scalar_tensor_tensor(x, got[0][s][0:S, :], weight[0:S, 0, b:b + 1], x, ALU.mult, ALU.add))
            nc.vector.scalar_tensor_tensor(x, got[1][s][0:S, :], weight[0:S, 1, b:b + 1], x, ALU.mult,
                                           ALU.add).then_inc(added, 1)
            if norm and b % 4 == 3:
                dve.wait_ge(added, b + 1)
                norm.moments(dve, b // 4, T["x"])
                norm.scales(dve, b // 4, b // 4, 1.0, LN_EPS, 0.0)

    def logits_and_ranks(pe):
        for b in range(B):
            for k in range(DK):
                ins = nc.tensor.matmul(ps[0][0:S, b * E:(b + 1) * E], T["xn_t"][:, k, b * S:(b + 1) * S],
                                       T[f"wr{n}"][:, k, :], start=k == 0, stop=k == DK - 1)
        ins.then_inc(logits_done, 1)
        pe.wait_ge(hot_ready, 2)
        one_hots = hot[0:S, :, :, :].rearrange("p k b e -> p (k b e)")
        nc.tensor.matmul(ps[1][0:S, 0:2 * B * E], T["earlier"][0:S, 0:S], one_hots, start=True, stop=True)
        nc.tensor.matmul(ps[2][0:S, 0:2 * B * E], T["ones"][0:S, 0:S], one_hots, start=True, stop=True).then_inc(ranked, 1)

    def exps(act):
        act.wait_ge(diff_ready, 1)
        nc.scalar.activation(ex[0:S, :, :], ex[0:S, :, :], ACT.Exp).then_inc(ex_ready, 1)

    if n == 0:
        w1, w2 = T["w1_0"], T["w2_0"]
        xe = [sb(f"xe{s}", [P, 4, D]) for s in range(2)]
        xt = [sb(f"xt{s}", [P, DK, SLOTS]) for s in range(2)]
        ht = [sb(f"ht{s}", [P, F0 // P, SLOTS]) for s in range(2)]
        ye = [sb(f"ye{s}", [P, 4, D]) for s in range(2)]
        NF = F0 // P
        rows_in = [nc.alloc_semaphore(f"{nm}rows_in{s}") for s in range(2)]
        w_in = T["w_in"]
        x_turned = Counted(nc, nm + "x_turned", 2)
        xt_ready = Counted(nc, nm + "xt_ready", 2)
        up_done = Counted(nc, nm + "up_done", 2 * NF)
        gelu_done = Counted(nc, nm + "gelu_done", 2 * NF)
        down_done = Counted(nc, nm + "down_done", 8)
        y_ready = Counted(nc, nm + "y_ready", 8)
        y_out = [nc.alloc_semaphore(f"{nm}y_out{s}") for s in range(2)]
        X4 = XS[0:ROWS, :].rearrange("(e p j) d -> p e j d", e=E, j=4)
        Y4 = YS[0:ROWS, :].rearrange("(e p j) d -> p e j d", e=E, j=4)

        with nc.Block() as block:

            @block.sync
            def _(sp):
                def load_rows(e, s):
                    sp.dma_start(xe[s][:, :, :], X4[:, bass.ds(e, 1), :, :].rearrange("p e j d -> p (e j) d")).then_inc(rows_in[s], 16)

                sp.wait_ge(dispatched, 16 * 2 * B)
                load_rows(0, 0)
                load_rows(1, 1)
                with sp.Fori(0, E // 2) as i:
                    for s in range(2):
                        sp.wait_ge(y_ready.sem, y_ready.at(i, 4 * (s + 1)))
                        apart(sp)
                        sp.dma_start(Y4[:, bass.ds(2 * i + s, 1), :, :].rearrange("p e j d -> p (e j) d"), ye[s][:, :, :]).then_inc(y_out[s], 16)
                for s in range(2):
                    sp.wait_ge(y_out[s], 16 * (E // 2))
                sp.sem_inc(stored, 16)

            @block.gpsimd
            def _(pool):
                pool_dispatch(pool)
                pool_gather(pool, 1)

            @block.tensor
            def _(pe):
                for k in (x_turned, up_done, down_done):
                    k.credit(pe)
                logits_and_ranks(pe)

                def turn(i, s):
                    pe.wait_ge(rows_in[s], 16 * (i + 1))
                    pe.wait_ge(xt_ready.sem, xt_ready.at(i, s))
                    for k in range(DK):
                        for j in range(4):
                            ins = nc.tensor.transpose(ps[k][:, j * P:(j + 1) * P], xe[s][:, j, k * P:(k + 1) * P], T["ident"][:, :])
                    ins.then_inc(x_turned.sem, 1)

                def up(i, s):
                    pe.wait_ge(xt_ready.sem, xt_ready.at(i, s + 1))
                    pe.wait_ge(w_in[s], 32 * (i + 1))
                    for f in range(NF):
                        pe.wait_ge(gelu_done.sem, gelu_done.at(i, s * NF + f - 1))
                        for k in range(DK):
                            ins = nc.tensor.matmul(ps[2 + f % 2][:, :], w1[s][:, k, f * P:(f + 1) * P], xt[s][:, k, :],
                                                   start=k == 0, stop=k == DK - 1)
                        ins.then_inc(up_done.sem, 1)

                def down(i, s):
                    pe.wait_ge(gelu_done.sem, gelu_done.at(i, (s + 1) * NF))
                    for j in range(4):
                        pe.wait_ge(y_ready.sem, y_ready.at(i, s * 4 + j - 1))
                        for f in range(NF):
                            ins = nc.tensor.matmul(ps[4 + j % 2][:, 0:D], ht[s][:, f, j * P:(j + 1) * P], w2[s][:, f, :],
                                                   start=f == 0, stop=f == NF - 1)
                        ins.then_inc(down_done.sem, 1)

                with pe.Fori(0, E // 2) as i:
                    turn(i, 0)
                    up(i, 0)
                    turn(i, 1)
                    down(i, 0)
                    up(i, 1)
                    down(i, 1)
                for q in range(Norm.GROUPS):
                    norm.turn(pe, q, q + 1)

            @block.scalar
            def _(act):
                gelu_done.credit(act)
                exps(act)

                def load_expert(e, s):
                    act.dma_start(w1[s][:, :, :], D_["c_fc"][bass.ds(e, 1), :, :, :].rearrange("e p k f -> p (e k) f")).then_inc(w_in[s], 16)
                    act.dma_start(w2[s][:, :, :], D_["c_proj"][bass.ds(e, 1), :, :, :].rearrange("e p f d -> p (e f) d")).then_inc(w_in[s], 16)

                def gelus(i, s):
                    for f in range(NF):
                        act.wait_ge(up_done.sem, up_done.at(i, s * NF + f + 1))
                        if f == 0:
                            act.wait_ge(down_done.sem, down_done.at(i, s * 4 - 4))
                        nc.scalar.activation(ht[s][:, f, :], ps[2 + f % 2][:, :], ACT.Gelu).then_inc(gelu_done.sem, 1)

                def refill(i, s):
                    act.wait_ge(down_done.sem, down_done.at(i, s * 4 + 4))
                    load_expert(2 * i + 2 + s, s)
                    act.dma_start(xe[s][:, :, :], X4[:, bass.ds(2 * i + 2 + s, 1), :, :].rearrange("p e j d -> p (e j) d")).then_inc(rows_in[s], 16)

                with act.Fori(0, E // 2 - 1) as i:
                    gelus(i, 0)
                    gelus(i, 1)
                    refill(i, 0)
                    refill(i, 1)
                gelus(E // 2 - 1, 0)
                gelus(E // 2 - 1, 1)
                for q in range(Norm.GROUPS):
                    norm.roots(act, q, q)
                    norm.apply(act, q, q, T["x"], T["xn"])
                    for k in range(DK * (q > 0)):
                        norm.keep(act, nc.scalar.copy, q - 1, k)
                for k in range(DK):
                    norm.keep(act, nc.scalar.copy, Norm.GROUPS - 1, k)

            @block.vector
            def _(dve):
                xt_ready.credit(dve)
                y_ready.credit(dve)
                route(dve)

                def turned_rows(i, s):
                    dve.wait_ge(x_turned.sem, x_turned.at(i, s + 1))
                    dve.wait_ge(up_done.sem, up_done.at(i, (s - 1) * NF))
                    own_ready = None
                    nc.vector.tensor_copy(xt[s][:, 0, :], ps[0][:, :])
                    nc.vector.tensor_copy(xt[s][:, 1, :], ps[1][:, :]).then_inc(xt_ready.sem, 1)

                def rows_out(i, s):
                    for j in range(4):
                        dve.wait_ge(down_done.sem, down_done.at(i, s * 4 + j + 1))
                        if j == 0:
                            if isinstance(i, int):
                                if i > 0:
                                    dve.wait_ge(y_out[s], 16 * i)
                            else:
                                dve.wait_ge(y_out[s], 16 * i)
                        nc.vector.tensor_copy(ye[s][:, j, :], ps[4 + j % 2][:, 0:D]).then_inc(y_ready.sem, 1)

                def expert_pair(i):
                    turned_rows(i, 0)
                    turned_rows(i, 1)
                    rows_out(i, 0)
                    rows_out(i, 1)

                expert_pair(0)
                with dve.Fori(1, E // 2) as i:
                    expert_pair(i)
                combine(dve)
    else:
        w1, w2 = sb("w1", [P, E * DK * F1]), sb("w2", [P, E * (F1 // P) * D])
        b1, b2 = sb("b1", [P, E * F1]), sb("b2", [P, E * D])
        NF = F1 // P
        xe = [sb(f"xe{s}", [P, D]) for s in range(2)]
        xt = [sb(f"xt{s}", [P, DK, P]) for s in range(2)]
        hb = [sb(f"hb{s}", [P, F1]) for s in range(2)]
        hg = [sb(f"hg{s}", [P, F1]) for s in range(2)]
        ht = [sb(f"ht{s}", [P, NF, P]) for s in range(2)]
        ye = [sb(f"ye{s}", [P, D]) for s in range(2)]
        w_in = nc.alloc_semaphore(nm + "w_in")
        rows_in = [nc.alloc_semaphore(f"{nm}rows_in{s}") for s in range(2)]
        y_out = [nc.alloc_semaphore(f"{nm}y_out{s}") for s in range(2)]
        x_turned, xt_ready = Counted(nc, nm + "x_turned", 2), Counted(nc, nm + "xt_ready", 2)
        up_done, b1_added = Counted(nc, nm + "up_done", 2), Counted(nc, nm + "b1_added", 2)
        gelu_done, h_turned = Counted(nc, nm + "gelu_done", 2), Counted(nc, nm + "h_turned", 2)
        ht_ready, down_done = Counted(nc, nm + "ht_ready", 2), Counted(nc, nm + "down_done", 2)
        y_ready = Counted(nc, nm + "y_ready", 2)

        with nc.Block() as block:

            @block.sync
            def _(sp):
                sp.dma_start(w1[:, :], D_["W1"]).then_inc(w_in, 16)
                sp.dma_start(w2[:, :], D_["W2"]).then_inc(w_in, 16)
                sp.dma_start(b1[:, :], D_["b1"].to_broadcast((P, E * F1))).then_inc(w_in, 16)
                sp.dma_start(b2[:, :], D_["b2"].to_broadcast((P, E * D))).then_inc(w_in, 16)
                sp.wait_ge(dispatched, 16 * 2 * B)

                def load_rows(t, s):
                    sp.dma_start(xe[s][:, :], XS[bass.ds(t * P, P), :]).then_inc(rows_in[s], 16)

                load_rows(0, 0)
                load_rows(1, 1)

                def tile(i, s, load, store):
                    if load:
                        wait(sp, x_turned, i, s + 1)
                        apart(sp)
                        load_rows(2 * i + s + 2, s)
                    if store:
                        wait(sp, y_ready, i, s - 1)
                        apart(sp)
                        sp.dma_start(YS[bass.ds((2 * i + s - 2) * P, P), :], ye[s][:, :]).then_inc(y_out[s], 16)

                for s in range(2):
                    sp.sem_inc(y_out[s], 16)
                    tile(0, s, True, False)
                with sp.Fori(1, TILES // 2 - 1) as i:
                    for s in range(2):
                        tile(i, s, True, True)
                for i in (TILES // 2 - 1, TILES // 2):
                    for s in range(2):
                        tile(i, s, False, True)
                for s in range(2):
                    sp.wait_ge(y_out[s], 16 * (TILES // 2 + 1))
                sp.sem_inc(stored, 16)
                for h in range(2):
                    sp.wait_ge(added, B // 2 * (h + 1))
                    r = slice(h * B // 2, (h + 1) * B // 2)
                    sp.dma_start(out[r, :, :].rearrange("b s d -> s b d"),
                                 T["x"][0:S, :].rearrange("p (b d) -> p b d", b=B)[:, r, :]).then_inc(out_done, 16)
                sp.wait_ge(out_done, 32)

            @block.gpsimd
            def _(pool):
                pool_dispatch(pool)
                pool_gather(pool, 1)

            @block.tensor
            def _(pe):
                for k in (x_turned, up_done, h_turned, down_done):
                    k.credit(pe)
                logits_and_ranks(pe)
                pe.wait_ge(w_in, 64)
                pe.wait_ge(rows_ready, 1)

                def turn(i, s):
                    pe.wait_ge(rows_in[s], 16 * (i + 1))
                    wait(pe, xt_ready, i, s - 1)
                    for k in range(DK):
                        ins = nc.tensor.transpose(ps[s][:, k * P:(k + 1) * P], xe[s][:, k * P:(k + 1) * P], T["ident"][:, :])
                    ins.then_inc(x_turned.sem, 1)

                def up(i, s):
                    expert = pe.value_load(owner_i[0:1, bass.ds(2 * i + s, 1)], min_val=0, max_val=E - 1)
                    wait(pe, xt_ready, i, s + 1)
                    wait(pe, b1_added, i, s - 1)
                    for k in range(DK):
                        ins = nc.tensor.matmul(ps[2 + s][:, :], xt[s][:, k, :],
                                               w1[:, bass.ds(expert * (DK * F1) + k * F1, F1)], start=k == 0, stop=k == DK - 1)
                    ins.then_inc(up_done.sem, 1)

                def turn_hidden(i, s):
                    wait(pe, gelu_done, i, s + 1)
                    wait(pe, ht_ready, i, s - 1)
                    for f in range(NF):
                        ins = nc.tensor.transpose(ps[4 + s][:, f * P:(f + 1) * P], hg[s][:, f * P:(f + 1) * P], T["ident"][:, :])
                    ins.then_inc(h_turned.sem, 1)

                def down(i, s):
                    expert = pe.value_load(owner_i[0:1, bass.ds(2 * i + s, 1)], min_val=0, max_val=E - 1)
                    wait(pe, ht_ready, i, s + 1)
                    wait(pe, y_ready, i, s - 1)
                    for f in range(NF):
                        ins = nc.tensor.matmul(ps[6 + s][:, 0:D], ht[s][:, f, :],
                                               w2[:, bass.ds(expert * (NF * D) + f * D, D)], start=f == 0, stop=f == NF - 1)
                    ins.then_inc(down_done.sem, 1)

                last = TILES // 2 - 1
                turn(0, 0)
                up(0, 0)
                turn(0, 1)
                up(0, 1)
                turn_hidden(0, 0)
                turn(1, 0)
                with pe.Fori(1, last) as i:
                    up(i, 0)
                    turn_hidden(i - 1, 1)
                    turn(i, 1)
                    down(i - 1, 0)
                    up(i, 1)
                    turn_hidden(i, 0)
                    turn(i + 1, 0)
                    down(i - 1, 1)
                up(last, 0)
                turn_hidden(last - 1, 1)
                turn(last, 1)
                down(last - 1, 0)
                up(last, 1)
                turn_hidden(last, 0)
                down(last - 1, 1)
                turn_hidden(last, 1)
                down(last, 0)
                down(last, 1)

            @block.scalar
            def _(act):
                for k in (xt_ready, gelu_done, ht_ready):
                    k.credit(act)
                exps(act)

                def keep_rows(i, s):
                    wait(act, x_turned, i, s + 1)
                    wait(act, up_done, i, s - 1)
                    nc.scalar.copy(xt[s][:, :, :].rearrange("p k s -> p (k s)"), ps[s][:, 0:DK * P]).then_inc(xt_ready.sem, 1)

                def gelu(i, s):
                    wait(act, b1_added, i, s + 1)
                    wait(act, h_turned, i, s - 1)
                    nc.scalar.activation(hg[s][:, :], hb[s][:, :], ACT.Gelu_apprx_tanh).then_inc(gelu_done.sem, 1)

                def keep_hidden(i, s):
                    wait(act, h_turned, i, s + 1)
                    wait(act, down_done, i, s - 1)
                    nc.scalar.copy(ht[s][:, :, :].rearrange("p f s -> p (f s)"), ps[4 + s][:, :]).then_inc(ht_ready.sem, 1)

                last = TILES // 2 - 1
                keep_rows(0, 0)
                gelu(0, 0)
                keep_rows(0, 1)
                keep_hidden(0, 0)
                gelu(0, 1)
                keep_rows(1, 0)
                with act.Fori(1, last) as i:
                    keep_hidden(i - 1, 1)
                    gelu(i, 0)
                    keep_rows(i, 1)
                    keep_hidden(i, 0)
                    gelu(i, 1)
                    keep_rows(i + 1, 0)
                keep_hidden(last - 1, 1)
                gelu(last, 0)
                keep_rows(last, 1)
                keep_hidden(last, 0)
                gelu(last, 1)
                keep_hidden(last, 1)

            @block.vector
            def _(dve):
                for k in (b1_added, y_ready):
                    k.credit(dve)
                route(dve)
                dve.wait_ge(w_in, 64)

                def add_b1(i, s):
                    expert = dve.value_load(owner_i[0:1, bass.ds(2 * i + s, 1)], min_val=0, max_val=E - 1)
                    wait(dve, up_done, i, s + 1)
                    wait(dve, gelu_done, i, s - 1)
                    nc.vector.tensor_tensor(hb[s][:, :], ps[2 + s][:, :], b1[:, bass.ds(expert * F1, F1)],
                                            ALU.add).then_inc(b1_added.sem, 1)

                def add_b2(i, s):
                    expert = dve.value_load(owner_i[0:1, bass.ds(2 * i + s, 1)], min_val=0, max_val=E - 1)
                    wait(dve, down_done, i, s + 1)
                    dve.wait_ge(y_out[s], 16 * (i + 1))
                    nc.vector.tensor_tensor(ye[s][:, :], ps[6 + s][:, 0:D], b2[:, bass.ds(expert * D, D)],
                                            ALU.add).then_inc(y_ready.sem, 1)

                for s in range(2):
                    add_b1(0, s)
                with dve.Fori(1, TILES // 2) as i:
                    for s in range(2):
                        add_b1(i, s)
                        add_b2(i - 1, s)
                for s in range(2):
                    add_b2(TILES // 2 - 1, s)
                combine(dve)

    ctx.close()


def gated_two_layers(nc, a, out):
    ctx = ExitStack()

    def sb(name, shape, dt=F32):
        return ctx.enter_context(nc.sbuf_tensor(name, shape, dt))

    T, D_ = {}, dict(a)
    for n in (0, 1):
        D_[f"xs{n}"] = nc.dram_tensor(f"rows_in{n}", (DROP0 + 2 * B * S, D), F32, kind="Internal").ap()
        D_[f"ys{n}"] = nc.dram_tensor(f"rows_out{n}", (ROWS, D), F32, kind="Internal").ap()
    T["x"], T["xn"], T["xn_t"] = sb("x", [P, B * D]), sb("xn", [P, B * D]), sb("xn_t", [P, DK, B * S])
    T["ident"], T["ones"], T["earlier"] = sb("ident", [P, P]), sb("ones", [P, P]), sb("earlier", [P, P])
    T["experts"] = sb("experts", [P, E])
    T["wr0"], T["wr1"] = sb("wr0", [P, DK, E]), sb("wr1", [P, DK, E])
    T["bo0"], T["bo1"], T["gamma"], T["beta"] = (sb(k, [P, D]) for k in ("bo0", "bo1", "gamma", "beta"))
    T["stats"] = sb("stats", [P, B * 6])
    T["bq_col"], T["bk_col"], T["bv_out"] = sb("bq_col", [P, 2]), sb("bk_col", [P, 2]), sb("bv_out", [P, 4])
    T["head_rows"], T["bq_head"] = sb("head_rows", [P, 8]), sb("bq_head", [P, H])
    gate_in, T["gate"] = sb("gate_in", [P, 4]), sb("gate", [P, 4])
    zero = T["zero"] = sb("zero", [P, 4 * D])
    T["x_in"], T["ident_ready"] = nc.alloc_semaphore("x_in"), nc.alloc_semaphore("ident_ready")
    T["weights_in"] = nc.alloc_semaphore("weights_in")
    T["w_in"] = [nc.alloc_semaphore(f"expert_in{s}") for s in range(2)]
    small_in, consts, built, built_gate = (nc.alloc_semaphore(k) for k in ("small_in", "consts", "built", "built_gate"))
    zero_ready, padded = nc.alloc_semaphore("zero_ready"), nc.alloc_semaphore("padded")
    D_["cleared"], D_["cleared_value"] = nc.alloc_semaphore("cleared"), 16 * 2 * (ROWS // P // 4)
    w_first = [(f"w{k}0", f"w{k}0") for k in "qkv"]
    n0 = len(w_first) + 4
    T["weights_in_value"] = [16 * n0, 16 * (n0 + 4)]

    of_attention = ExitStack()
    for n, w, tiles in ((0, D, 4), (1, 1024, 8)):
        for k in "qkv":
            T[f"w{k}{n}"] = of_attention.enter_context(nc.sbuf_tensor(f"w{k}{n}", [P, DK, w], F32))
        T[f"wo{n}"] = of_attention.enter_context(nc.sbuf_tensor(f"wo{n}", [P, tiles, D], F32))
    early = ExitStack()
    T["w1_0"] = [early.enter_context(nc.sbuf_tensor(f"w1_0_{s}", [P, DK, F0], F32)) for s in range(2)]
    T["w2_0"] = [early.enter_context(nc.sbuf_tensor(f"w2_0_{s}", [P, F0 // P, D], F32)) for s in range(2)]

    with nc.Block() as block:

        @block.sync
        def _(sp):
            sp.dma_start(T["x"][0:S, :], D_["x"]).then_inc(T["x_in"], 16)
            for name, src in w_first:
                sp.dma_start(T[name][:, :, :], D_[src]).then_inc(T["weights_in"], 16)
            sp.wait_ge(zero_ready, 2)
            for j in range(4):
                r = 32 * j + 16 * (j % 2)
                sp.dma_start(T["wo0"][r:r + 16, :, :], D_["wo0"][:, j, :, :]).then_inc(T["weights_in"], 16)
            for k in ("wq1", "wk1", "wv1", "wo1"):
                sp.dma_start(T[k][:, :, :], D_[k]).then_inc(T["weights_in"], 16)
            sp.wait_ge(zero_ready, 3)
            for n in (0, 1):
                X = D_[f"xs{n}"][0:ROWS, :].rearrange("(g p j) d -> g p (j d)", p=P, j=4)
                for g in range(ROWS // P // 4):
                    sp.dma_start(X[g, :, :], zero[:, :]).then_inc(D_["cleared"], 16)
            for s in range(2):
                sp.dma_start(T["w1_0"][s][:, :, :], D_["c_fc"][s, :, :, :]).then_inc(T["w_in"][s], 16)
                sp.dma_start(T["w2_0"][s][:, :, :], D_["c_proj"][s, :, :, :]).then_inc(T["w_in"][s], 16)

        @block.scalar
        def _(act):
            small = [("bq_col", "bq"), ("bk_col", "bk"), ("wr0", "wr0"), ("wr1", "wr1")]
            for name, src in small:
                dst = T[name][:, :, :] if len(T[name].shape) == 3 else T[name][:, :]
                act.dma_start(dst, D_[src]).then_inc(small_in, 16)
            for name in ("bo0", "bo1", "gamma", "beta"):
                act.dma_start(T[name][:, :], D_[name].to_broadcast((P, D))).then_inc(small_in, 16)
            for k in range(4):
                act.dma_start(gate_in[:, k:k + 1], D_["gates"][k:k + 1, :].to_broadcast((P, 1))).then_inc(small_in, 16)
            act.wait_ge(zero_ready, 2)
            for j in range(4):
                r = 32 * j + 16 * (j % 2)
                act.dma_start(T["bv_out"][r:r + 16, :], D_["bv"][:, j, :]).then_inc(small_in, 16)
            act.wait_ge(small_in, 16 * 16)
            nc.scalar.activation(T["gate"][:, :], gate_in[:, :], ACT.Tanh).then_inc(built_gate, 1)

        @block.gpsimd
        def _(pool):
            pool.memset(T["wo0"][:, :, :], 0.0).then_inc(zero_ready, 1)
            pool.memset(T["bv_out"][:, :], 0.0).then_inc(zero_ready, 1)
            pool.memset(zero[:, :], 0.0).then_inc(zero_ready, 1)
            pool.memset(T["ones"][:, :], 1.0).then_inc(consts, 1)
            pool.wait_ge(consts, 1)
            pool.affine_select(out=T["ident"][:, :], in_=T["ones"][:, :], compare_op=ALU.is_equal, fill=0.0, base=0,
                               pattern=[[1, P]], channel_multiplier=-1).then_inc(T["ident_ready"], 1)
            pool.affine_select(out=T["earlier"][:, :], in_=T["ones"][:, :], compare_op=ALU.is_gt, fill=0.0, base=0,
                               pattern=[[1, P]], channel_multiplier=-1).then_inc(consts, 1)
            pool.affine_select(out=T["head_rows"][:, :], in_=T["ones"][:, 0:8], compare_op=ALU.is_ge, fill=0.0, base=0,
                               pattern=[[-16, 8]], channel_multiplier=1).then_inc(consts, 1)
            pool.wait_ge(consts, 3)
            pool.affine_select(out=T["head_rows"][:, :], in_=T["head_rows"][:, :], compare_op=ALU.is_ge, fill=0.0, base=15,
                               pattern=[[16, 8]], channel_multiplier=-1).then_inc(consts, 1)

        @block.vector
        def _(dve):
            dve.wait_ge(small_in, 16 * 16)
            dve.wait_ge(consts, 4)
            dve.wait_ge(built_gate, 1)
            for k in ("gamma", "beta"):
                nc.vector.tensor_scalar(T[k][:, :], T[k][:, :], T["gate"][:, 2:3], None, ALU.mult).then_inc(built, 1)
            for t in range(2):
                nc.vector.tensor_scalar(T["bq_head"][:, 8 * t:8 * t + 8], T["head_rows"][:, :], T["bq_col"][:, t:t + 1],
                                        None, ALU.mult).then_inc(built, 1)

    normalise(nc, T, "n0_", False, True)
    attention(nc, Layer(0, 16, 0.25), T, D_)
    normalise(nc, T, "n1_", False, False)
    feed_forward(nc, 0, T, D_, out)
    early.close()
    attention(nc, Layer(1, 64, 1.0 / 16), T, D_)
    normalise(nc, T, "n3_", True, False)
    of_attention.close()
    feed_forward(nc, 1, T, D_, out)
    ctx.close()


def kernel(**inputs):
    import numpy as np
    import concourse.bacc as bacc
    from concourse import mybir as my
    from concourse.bass_utils import run_bass_kernel_spmd as run

    a = {k: np.asarray(v) for k, v in inputs.items()}

    def rows(w):
        return w.reshape(-1, 128, w.shape[-1]).transpose(1, 0, 2)

    def heads(w):
        return w.transpose(1, 0, 2).reshape(w.shape[1], -1)

    lay = {
        "x": a["x"].transpose(1, 0, 2).reshape(S, B * D),
        "ctx": rows(a["ctx_1024"].reshape(B * L, D).T),
        "mask0": a["mask_Bx1x1xS2_ik0"].reshape(B, L),
        "mask1": a["mask_BxSxS2_bf0"].transpose(1, 0, 2).reshape(S, B * L),
        "gates": np.stack([a["g_xattn"], a["g_ffn"]], 1).reshape(4, 1),
        "wq0": rows(a["L0_xattn_wq"].T), "wk0": rows(a["L0_xattn_wk"].T), "wv0": rows(a["L0_xattn_wv"].T),
        "wo0": a["L0_xattn_wo"].T.reshape(4, 4, 16, D).transpose(2, 1, 0, 3),
        "bq": a["L0_xattn_bq"].reshape(2, 128).T, "bk": a["L0_xattn_bk"].reshape(2, 128).T,
        "bv": a["L0_xattn_bv"].reshape(4, 4, 16).transpose(2, 1, 0),
        "bo0": a["L0_xattn_bo"].reshape(1, D), "bo1": a["L1_xattn_b_o"].reshape(1, D),
        "gamma": a["L1_xattn_gamma"].reshape(1, D), "beta": a["L1_xattn_beta"].reshape(1, D),
        "wr0": rows(a["L0_ffn_w_g"]), "wr1": rows(a["L1_ffn_routing_weights"]),
        "c_fc": a["L0_ffn_c_fc"].reshape(E, DK, 128, F0).transpose(0, 2, 1, 3),
        "c_proj": a["L0_ffn_c_proj"].reshape(E, F0 // 128, 128, D).transpose(0, 2, 1, 3),
        "wq1": rows(heads(a["L1_xattn_w_qs"])), "wk1": rows(heads(a["L1_xattn_w_ks"])),
        "wv1": rows(heads(a["L1_xattn_w_vs"])), "wo1": rows(a["L1_xattn_W_o"].T),
        "W1": a["L1_ffn_W1"].reshape(E, DK, 128, F1).transpose(2, 0, 1, 3).reshape(128, -1),
        "W2": a["L1_ffn_W2"].reshape(E, F1 // 128, 128, D).transpose(2, 0, 1, 3).reshape(128, -1),
        "b1": a["L1_ffn_b1"].reshape(1, E * F1), "b2": a["L1_ffn_b2"].reshape(1, E * D),
    }
    nc = bacc.Bacc("TRN2", target_bir_lowering=False, num_devices=1)
    arrays, dram = {}, {}
    for name, v in lay.items():
        v = np.ascontiguousarray(v)
        arrays[f"in_{name}"] = v
        dram[name] = nc.dram_tensor(f"in_{name}", v.shape, my.dt.from_np(v.dtype), kind="ExternalInput").ap()
    out = nc.dram_tensor("out", (B, S, D), my.dt.from_np(np.dtype("float32")), kind="ExternalOutput").ap()
    gated_two_layers(nc, dram, out)
    return run(nc, [arrays], core_ids=[0]).results[0]["out"]
```

```python
from contextlib import ExitStack

import concourse.bass as bass
from concourse import mybir

F32 = mybir.dt.float32
F32R = mybir.dt.float32r
I32 = mybir.dt.int32
U32 = mybir.dt.uint32
U8 = mybir.dt.uint8
ALU = mybir.AluOpType
ACT = mybir.ActivationFunctionType
AX = mybir.AxisListType

P = 128
B, S, L, D = 16, 100, 361, 256
H = 16
E = 8
DK = D // P
PAIRS = B // 2
KTS = [(k, min(P, L - k)) for k in range(0, L, P)]
KT_N = len(KTS)
SLOTS = 512
CAP = 2 * 5 * B * S // (4 * E)
CAP += CAP % 2
TILES = 32
ROWS = TILES * P
DROP0 = ROWS
F0, F1 = 1024, 512
LN_EPS, Z_EPS = 1e-5, 1e-3
BIG = 3.0e38


class Counted:

    def __init__(self, nc, name, per, pre=0):
        self.sem, self.per, self.pre = nc.alloc_semaphore(name), per, pre

    def credit(self, eng):
        eng.sem_inc(self.sem, self.per)

    def before(self, k):
        return self.per + k

    def at(self, i, k):
        return self.per + self.pre + i * self.per + k


def wait(eng, counted, i, k):
    value = counted.at(i, k)
    if not isinstance(value, int) or value > counted.per:
        eng.wait_ge(counted.sem, value)


class Chain:

    def __init__(self, nc, name):
        self.sem, self.n = nc.alloc_semaphore(name), 0

    def mark(self, ins):
        self.n += 1
        ins.then_inc(self.sem, 1)
        return self.n

    def link(self, eng, ins):
        eng.wait_ge(self.sem, self.mark(ins))


class LoopChain:

    def __init__(self, nc, name, per):
        self.sem, self.per, self.n = nc.alloc_semaphore(name), per, 0

    def begin(self, i):
        self.i, self.n = i, 0

    def mark(self, ins):
        self.n += 1
        ins.then_inc(self.sem, 1)
        return self.i * self.per + self.n

    def link(self, eng, ins):
        eng.wait_ge(self.sem, self.mark(ins))

    def skip(self, eng, k):
        self.n += k
        eng.sem_inc(self.sem, k)


class Apart:

    def __init__(self, nc):
        self.sems = {eng.engine: nc.alloc_semaphore(f"passed_{k}") for k, eng in
                     (("dve", nc.vector), ("pool", nc.gpsimd), ("sp", nc.sync))}

    def __call__(self, eng):
        eng.sem_inc(self.sems[eng.engine], 1)


class Layer:

    def __init__(self, n, dh, score_scale):
        self.n, self.dh, self.scale = n, dh, score_scale
        self.first = n == 0
        self.width = H * dh
        self.nt = self.width // P
        self.per_tile = P // dh
        self.q_heads = 64 // dh if self.first else 2
        self.q_tiles = H // self.q_heads
        self.v_cols = min(self.width, 512)
        self.v_parts = self.width // self.v_cols
        self.pv_rows = 32 if self.first else dh
        self.per_out = P // self.pv_rows
        self.out_tiles = H // self.per_out
        self.groups = self.out_tiles * S // 400
        self.lags = (1, 7, 8) if self.first else (1, 5, 6)


HEADS = 2 * H
N_PB, N_PT = 8, 2
PASSES = ((0, 0), (1, 0), (0, 1))
BANKS = 3
LN2 = L + 1


def schedule(layer, last):
    LP = layer.lags[2]
    at = [[] for _ in range(HEADS + LP + 3)]

    def put(g, unit):
        while len(at[g]) == 2:
            g += 1
        at[g].append(unit)

    for half in range(1 if last else 2):
        s, base = 1 - half, H * half
        if half:
            for t in range(layer.q_tiles):
                put(base + (t + 1) * layer.q_heads - 1, ("Q", 0, t, 0))
        for t in range(layer.nt):
            late = half if layer.per_tile < 8 else 0
            put(min(base + (t + 1) * layer.per_tile - 1 + late, base + H - 1), ("K", s, t, 0))
    put(LP + 2, ("W", 1, 0, -1))
    put(H + LP + 1, ("W", 0, 0, 0))
    parts = [(t, p) for t in range(KT_N) for p in range(layer.v_parts)]
    for half in range(1 if last else 2):
        begin, end = (LP + 1, H + LP - 1) if half == 0 else (H + LP, HEADS)
        for m, (t, p) in enumerate(parts):
            put(begin + m * (end - begin) // len(parts), ("V", 1 - half, t, p))
    if last:
        put(HEADS + LP + 2, ("W", 1, 0, 0))
    else:
        at = at[:HEADS]
        for k in range(-sum(len(slot) for slot in at) % BANKS):
            put(4 * k, ("none", 0, k, 0))
    units = [u for slot in at for u in slot]
    assert last or len(units) == (2 * (layer.nt + KT_N * layer.v_parts + 1) + layer.q_tiles + 2) // 3 * 3
    return Units(layer, units, at)


class Units:

    def __init__(self, layer, units, at=None):
        self.units, self.owner, self.split = units, [], []
        self.count, self.splits = {"A": 0, "D": 0}, 0
        for kind, b, t, p in units:
            eng = "A" if kind == "V" and layer.n and (t + p) % 2 else "D"
            self.count[eng] += 1
            self.splits += kind in ("Q", "K")
            self.owner.append((eng, self.count[eng]))
            self.split.append(self.splits)
        self.slots, index = [], 0
        for slot in at or []:
            self.slots.append([(index + m, u) for m, u in enumerate(slot)])
            index += len(slot)

    def find(self, kind, b, t=None):
        return [u for u, x in enumerate(self.units) if x[0] == kind and x[1] == b and t in (None, x[2])]


def attention(nc, layer, T, D_):
    n = layer.n
    nm = f"a{n}_"
    LE, LT, LP = layer.lags
    ctx = ExitStack()

    def sb(name, shape, dt=F32):
        return ctx.enter_context(nc.sbuf_tensor(nm + name, shape, dt))

    if n == 0:
        cx = [sb(f"context{s}", [P, DK, L]) for s in range(2)]
    if n == 1:
        cx = [sb("context", [P, DK, L])] * 2
        cx_parts = [[sb(f"context_part{k}_{s}", [P, DK, LN2], F32R) for k in range(2)] for s in range(2)]
        w_parts = {k: [sb(f"w{k}_part{m}", [P, DK, layer.width], F32R) for m in range(2)] for k in "kv"}
    kt = sb("keys", [P, 2 * layer.nt, LN2], F32R)
    vt = [sb(f"values{s}", [P, KT_N, layer.width]) for s in range(2)]
    q_hi, q_lo = sb("queries_hi", [P, H, 2 * S], F32R), sb("queries_lo", [P, H, 2 * S], F32R)
    whole = {"Q": sb("whole_queries", [P, 2 * S]), "K": sb("whole_keys", [P, L])} if n == 0 else None
    parts = [sb(f"query_part{k}", [P, 2 * S], F32R) for k in range(2)] if n == 0 else None
    raw = [sb(f"mask_raw{s}", [P, L], I32 if n == 0 else U8) for s in range(2)]
    bias = [sb(f"mask_bias{s}", [P, L]) for s in range(2)]
    keep = [sb(f"mask_keep{s}", [P, L]) for s in range(2)] if n == 0 else None
    prob = sb("prob", [P, N_PB, L])
    low = sb("low", [P, N_PB])
    total = sb("total", [P, N_PB])
    inv = sb("inv", [P, N_PB])
    pt = sb("prob_t", [P, N_PT, KT_N * S])
    ot = [sb(f"out_t{s}", [P, layer.out_tiles, S]) for s in range(2)]
    lin = sb("lin", [P, D]) if n == 0 else None
    ps_s = [ctx.enter_context(nc.psum_tensor(f"{nm}ps_s{k}", [P, 512], F32)) for k in range(2)]
    ps_t = ctx.enter_context(nc.psum_tensor(f"{nm}ps_t", [P, 512], F32))
    ps_o = [ctx.enter_context(nc.psum_tensor(f"{nm}ps_o{k}", [P, 512], F32)) for k in range(2)]
    ps_p = [ctx.enter_context(nc.psum_tensor(f"{nm}ps_p{k}", [P, 512], F32)) for k in range(BANKS)]

    full, final = schedule(layer, False), schedule(layer, True)
    pre = Units(layer, [("Q", 0, t, 0) for t in range(layer.q_tiles)] + [("K", 0, t, 0) for t in range(layer.nt)]
                + [("V", 0, t, p) for t in range(KT_N) for p in range(layer.v_parts)])
    n_units, n_pre = len(full.units), len(pre.units)

    groups = 2 * layer.groups
    per_group = H // layer.groups
    scored = Counted(nc, nm + "scored", HEADS)
    maxed = Counted(nc, nm + "maxed", HEADS)
    exped = Counted(nc, nm + "exped", HEADS)
    inverted = Counted(nc, nm + "inverted", HEADS)
    normed = Counted(nc, nm + "normed", HEADS)
    turned = Counted(nc, nm + "turned", HEADS)
    pt_ready = Counted(nc, nm + "pt_ready", HEADS)
    valued = Counted(nc, nm + "valued", HEADS)
    out_ready = Counted(nc, nm + "out_ready", groups)
    unit_done = Counted(nc, nm + "unit_done", n_units, n_pre)
    taken = {"A": Counted(nc, nm + "taken_act", full.count["A"], pre.count["A"]),
             "D": Counted(nc, nm + "taken_dve", full.count["D"], pre.count["D"])}
    hi_ready = Counted(nc, nm + "hi_ready", full.splits, pre.splits)
    if n == 0:
        lo_ready = Counted(nc, nm + "lo_ready", full.splits, pre.splits)
        half_lower = Counted(nc, nm + "half_lower", full.splits, pre.splits)
        whole_ready = Counted(nc, nm + "whole_ready", full.splits, pre.splits)
        kept = [nc.alloc_semaphore(f"{nm}kept{s}") for s in range(2)]
    else:
        cx_hi = [nc.alloc_semaphore(f"{nm}context_hi{s}") for s in range(2)]
        cx_ready = [nc.alloc_semaphore(f"{nm}context_ready{s}") for s in range(2)]
        w_in = [nc.alloc_semaphore(f"{nm}w{w}_in") for w in "kv"]
        w_hi, w_ready = nc.alloc_semaphore(nm + "weights_hi"), nc.alloc_semaphore(nm + "weights_ready")
    loaded = [nc.alloc_semaphore(f"{nm}loaded{s}") for s in range(2)]
    biased = [nc.alloc_semaphore(f"{nm}biased{s}") for s in range(2)]
    zeroed = nc.alloc_semaphore(nm + "zeroed")
    dve_own = LoopChain(nc, nm + "dve_own", 4)
    apart = T["apart"]
    LOADS = 2 * 16

    def lagging(g, by, i):
        k = g - by
        if k >= HEADS or (k < 0 and isinstance(i, int) and i == 0):
            return None
        return (i - 1, k + HEADS) if k < 0 else (i, k)

    def iterations(eng, heads):
        heads(0, full)
        with eng.Fori(1, PAIRS - 1) as i:
            heads(i, full)
        heads(PAIRS - 1, final)

    def halves(half):
        low_half, high_half = slice(0, 64), slice(64, 128)
        return (high_half, low_half) if half else (low_half, high_half)

    def no_outputs(i, part):
        return part == -1 and isinstance(i, int) and i == 0

    def bank_of(u, before):
        return ps_p[(u - n_pre if before else u) % BANKS]

    def units_of(i, g, sched):
        if g >= 0:
            return [(u, unit, sched, i) for u, unit in sched.slots[g]]
        if isinstance(i, int) and i == 0:
            return []
        return [(u, unit, full, i - 1) for u, unit in full.slots[g]]

    def queries_free(i, t):
        return scored.at(i, H + (t + 1) * layer.q_heads)

    def keys_free(i, s, t):
        return scored.at(i, (H if s == 0 else 0) + (t + 1) * layer.per_tile)

    with nc.Block() as block:

        @block.sync
        def _(sp):
            def load(batch, s):
                apart(sp)
                if n == 0:
                    mask = D_["mask0"][bass.ds(batch, 1), :].to_broadcast((P, L))
                    dst = raw[s][:, :]
                else:
                    mask = D_["mask1"][:, bass.ds(batch * L, L)]
                    dst = raw[s][0:S, :]
                sp.dma_start(cx[s][:, :, :], D_["ctx"][:, :, bass.ds(batch * L, L)]).then_inc(loaded[s], 16)
                sp.dma_start(dst, mask).then_inc(loaded[s], 16)

            load(0, 0)
            if n == 1:
                for s, w in enumerate("kv"):
                    sp.dma_start(vt[s][:, 0:DK, :], D_[f"w{w}1"]).then_inc(w_in[s], 16)
                sp.wait_ge(cx_ready[0], 1)
            load(1, 1)
            if n == 0:
                T["load_later"](sp)
            with sp.Fori(0, PAIRS - 1) as i:
                for s in range(2):
                    if n == 1:
                        sp.wait_ge(cx_ready[1 - s], i + 1 + s)
                    else:
                        last = max(full.find("K", 1) + full.find("V", 1)) + 1
                        sp.wait_ge(unit_done.sem, unit_done.at(i, last if s else 0))
                    apart(sp)
                    sp.wait_ge(biased[s], i + 1)
                    load(2 * i + 2 + s, s)

        @block.gpsimd
        def _(pool):
            pool.memset(kt[:, :, L:LN2].bitcast(F32), 0.0).then_inc(zeroed, 1)
            masked_value = -1.0e9 / layer.scale

            def convert(s, nth, before):
                pool.wait_ge(loaded[s], LOADS * nth)
                if before is not None:
                    pool.wait_ge(maxed.sem, before)
                apart(pool)
                if n == 0:
                    nc.gpsimd.tensor_scalar(bias[s][:, :], raw[s][:, :], 0.0, masked_value, ALU.is_equal,
                                            ALU.mult).then_inc(biased[s], 1)
                    pool.wait_ge(biased[s], nth)
                    apart(pool)
                    nc.gpsimd.tensor_scalar(keep[s][:, :], bias[s][:, :], 0.0, None, ALU.is_equal).then_inc(kept[s], 1)
                    pool.wait_ge(kept[s], nth)
                    apart(pool)
                else:
                    nc.gpsimd.tensor_scalar(bias[s][0:S, :], raw[s][0:S, :], -BIG, 10.0, ALU.mult,
                                            ALU.mult).then_inc(biased[s], 1)

            def split_context(s, nth, before):
                pool.wait_ge(loaded[s], LOADS * nth)
                if before is not None:
                    pool.wait_ge(unit_done.sem, before)
                apart(pool)
                hi, lo = (x[:, :, 0:L] for x in cx_parts[s])
                nc.gpsimd.tensor_copy(hi, cx[s][:, :, :]).then_inc(cx_hi[s], 1)
                pool.wait_ge(cx_hi[s], nth)
                apart(pool)
                nc.gpsimd.tensor_tensor(lo, cx[s][:, :, :], hi, ALU.subtract).then_inc(cx_ready[s], 1)

            def lower(unit, split, i, before):
                kind, s, t, p = unit
                pool.wait_ge(hi_ready.sem, hi_ready.before(split) if before else hi_ready.at(i, split))
                apart(pool)
                def behind(ins, done):
                    ins.then_inc(done.sem, 1)
                    pool.wait_ge(done.sem, done.before(split) if before else done.at(i, split))
                    apart(pool)

                if kind == "Q":
                    if not before:
                        pool.wait_ge(scored.sem, queries_free(i, t))
                        apart(pool)
                    behind(nc.gpsimd.tensor_tensor(parts[1][:, :], whole["Q"][:, :], parts[0][:, :], ALU.subtract), half_lower)
                    for part, q in zip(parts, (q_hi, q_lo)):
                        shape = (P, layer.q_heads, 2 * S)
                        ins = nc.gpsimd.tensor_tensor(q[:, t * layer.q_heads:(t + 1) * layer.q_heads, :],
                                                      part[:, :].unsqueeze(1).to_broadcast(shape),
                                                      T["head_rows"][:, :].unsqueeze(2).to_broadcast(shape), ALU.mult)
                    behind(ins, lo_ready)
                else:
                    for half in range(2):
                        r, o = halves(half)
                        ins = nc.gpsimd.tensor_tensor(kt[o, 2 * t + half, 0:L], whole["K"][r, :], kt[r, 2 * t + half, 0:L],
                                                      ALU.subtract)
                        behind(ins, lo_ready if half else half_lower)

            def heads(i, sched):
                for g in range(HEADS):
                    for u, unit, of, j in units_of(i, g - 2, sched):
                        if n == 0 and unit[0] in ("Q", "K"):
                            lower(unit, of.split[u], j, False)
                    if n == 1 and sched is full and g == 1:
                        split_context(0, i + 2, unit_done.at(i, 0))
                    if sched is full and g == H + 1:
                        convert(0, i + 2, maxed.at(i, H))
                    if sched is full and g == HEADS - 1:
                        if n == 1:
                            split_context(1, i + 2, unit_done.at(i, max(full.find("K", 1) + full.find("V", 1)) + 1))
                        convert(1, i + 2, maxed.at(i, HEADS))

            if n == 0:
                lo_ready.credit(pool)
                half_lower.credit(pool)
                pool.wait_ge(zeroed, 1)
            if n == 1:
                for part in cx_parts[0] + cx_parts[1]:
                    pool.memset(part[:, :, L:LN2].bitcast(F32), 0.0).then_inc(zeroed, 1)
                for s in range(2):
                    split_context(s, 1, None)
            convert(0, 1, None)
            if n == 1:
                convert(1, 1, None)
            else:
                for u, unit in enumerate(pre.units):
                    if unit[0] in ("Q", "K"):
                        lower(unit, pre.split[u], 0, True)
                convert(1, 1, None)
            iterations(pool, heads)

        @block.tensor
        def _(pe):
            def project(u, unit, sched, i):
                kind, s, t, p = unit
                before = sched is pre
                bank = bank_of(u, before)
                back = u - BANKS
                if before:
                    if back >= 0:
                        eng, k = pre.owner[back]
                        pe.wait_ge(taken[eng].sem, taken[eng].before(k))
                elif back >= 0:
                    eng, k = sched.owner[back]
                    pe.wait_ge(taken[eng].sem, taken[eng].at(i, k))
                elif isinstance(i, int) and i == 0:
                    eng, k = pre.owner[n_pre + back]
                    pe.wait_ge(taken[eng].sem, taken[eng].before(k))
                else:
                    eng, k = full.owner[n_units + back]
                    pe.wait_ge(taken[eng].sem, taken[eng].at(i, k - taken[eng].per))
                if before and n == 1 and kind in ("K", "V"):
                    pe.wait_ge(w_ready, DK if kind == "K" else 2 * DK)
                if kind in ("K", "V"):
                    there, per = (loaded[s], LOADS) if n == 0 else (cx_ready[s], 1)
                    pe.wait_ge(there, per if before else (i + 2 - s) * per)
                if kind == "Q":
                    first = 0 if before else (i + 1) * 2 * S
                    for k in range(DK):
                        ins = nc.tensor.matmul(bank[:, 0:2 * S], T[f"wq{n}"][:, k, t * P:(t + 1) * P],
                                               T["xn_t"][:, k, bass.ds(first, 2 * S)],
                                               start=k == 0, stop=k == DK - 1)
                elif kind == "K" and n == 1:
                    for m, (k, (a, b)) in enumerate((k, ab) for k in range(DK) for ab in PASSES):
                        ins = nc.tensor.matmul(bank[:, 0:LN2], w_parts["k"][a][:, k, t * P:(t + 1) * P],
                                               cx_parts[s][b][:, k, :], start=m == 0, stop=m == DK * len(PASSES) - 1)
                elif kind == "V" and n == 1:
                    k0, w = KTS[t][0], layer.v_cols
                    kn = min(P, LN2 - k0)
                    for m, (k, (a, b)) in enumerate((k, ab) for k in range(DK) for ab in PASSES):
                        ins = nc.tensor.matmul(bank[0:kn, 0:w], cx_parts[s][b][:, k, k0:k0 + kn],
                                               w_parts["v"][a][:, k, p * w:(p + 1) * w],
                                               start=m == 0, stop=m == DK * len(PASSES) - 1)
                elif kind == "K":
                    for k in range(DK):
                        ins = nc.tensor.matmul(bank[:, 0:L], T[f"wk{n}"][:, k, t * P:(t + 1) * P],
                                               cx[s][:, k, :], start=k == 0, stop=k == DK - 1)
                elif kind == "V":
                    k0, kn = KTS[t]
                    w = layer.v_cols
                    for k in range(DK):
                        ins = nc.tensor.matmul(bank[0:kn, 0:w], cx[s][:, k, k0:k0 + kn],
                                               T[f"wv{n}"][:, k, p * w:(p + 1) * w],
                                               start=k == 0, stop=k == DK - 1)
                elif kind == "none" or no_outputs(i, p):
                    pe.wait_ge(unit_done.sem, unit_done.at(i, u))
                    pe.sem_inc(unit_done.sem, 1)
                    return
                else:
                    pe.wait_ge(out_ready.sem, out_ready.at(i + p, layer.groups * (s + 1)))
                    for k in range(layer.out_tiles):
                        ins = nc.tensor.matmul(bank[0:S, 0:D], ot[s][:, k, :], T[f"wo{n}"][:, k, :],
                                               start=k == 0, stop=k == layer.out_tiles - 1)
                ins.then_inc(unit_done.sem, 1)

            def heads(i, sched):
                first_one = isinstance(i, int) and i == 0
                for g in range(len(sched.slots)):
                    if g < HEADS:
                        b, h = g // H, g % H
                        made_in = sched if b else full

                        def in_sbuf(kind, t):
                            u = made_in.find(kind, b, t)[0]
                            count, k = (lo_ready, made_in.split[u]) if n == 0 else (taken["D"], made_in.owner[u][1])
                            pe.wait_ge(count.sem, count.at(i, k if b else k - count.per))

                        if b == 0 and not first_one and h % layer.q_heads == 0:
                            in_sbuf("Q", h // layer.q_heads)
                        if (b or not first_one) and h % layer.per_tile == 0:
                            in_sbuf("K", h // layer.per_tile)
                        pe.wait_ge(maxed.sem, maxed.at(i, g - 1))
                        keys = kt[:, h * layer.dh // 64, :]
                        nc.tensor.matmul(ps_s[g % 2][0:S, 0:LN2], q_hi[:, h, b * S:(b + 1) * S], keys,
                                         start=True, stop=False)
                        nc.tensor.matmul(ps_s[g % 2][0:S, 0:LN2], q_lo[:, h, b * S:(b + 1) * S], keys,
                                         start=False, stop=True).then_inc(scored.sem, 1)
                    lag = lagging(g, LT, i)
                    if lag:
                        j, t = lag
                        pe.wait_ge(normed.sem, normed.at(j, t + 1))
                        pe.wait_ge(pt_ready.sem, pt_ready.at(j, t))
                        for c, (k0, kn) in enumerate(KTS):
                            ins = nc.tensor.transpose(ps_t[0:kn, c * S:(c + 1) * S],
                                                      prob[0:S, t % N_PB, k0:k0 + kn], T["ident"][0:S, 0:S])
                        ins.then_inc(turned.sem, 1)
                    lag = lagging(g, LP, i)
                    if lag:
                        j, v = lag
                        b, h = v // H, v % H
                        group = v // per_group
                        if h == 0:
                            made_in = sched if b else full
                            for eng in "AD":
                                k = [made_in.owner[u][1] for u in made_in.find("V", b) if made_in.owner[u][0] == eng]
                                if k and (b or not first_one):
                                    pe.wait_ge(taken[eng].sem, taken[eng].at(j, max(k) - (0 if b else taken[eng].per)))
                        pe.wait_ge(pt_ready.sem, pt_ready.at(j, v + 1))
                        if v % per_group == 0:
                            pe.wait_ge(out_ready.sem, out_ready.at(j, group - 1))
                        w = layer.pv_rows
                        row = h % layer.per_out * w
                        col = (h // layer.per_out * S) % 400
                        v0 = (h // 2 * 32) if n == 0 else h * w
                        for c, (k0, kn) in enumerate(KTS):
                            ins = nc.tensor.matmul(ps_o[group % 2][row:row + w, col:col + S],
                                                   vt[b][0:kn, c, v0:v0 + w], pt[0:kn, v % N_PT, c * S:(c + 1) * S],
                                                   start=c == 0, stop=c == KT_N - 1)
                        ins.then_inc(valued.sem, 1)
                    for u, unit in sched.slots[g]:
                        project(u, unit, sched, i)

            for k in (scored, turned, valued, unit_done):
                k.credit(pe)
            pe.wait_ge(T["weights_in"][n], T["weights_in_value"][n])
            if n == 1:
                pe.wait_ge(zeroed, 5)
            for u, unit in enumerate(pre.units):
                project(u, unit, pre, 0)
            if n == 0:
                pe.wait_ge(zeroed, 1)
            for k in [taken["A"], taken["D"]] + ([lo_ready] if n == 0 else []):
                if k.pre:
                    pe.wait_ge(k.sem, k.before(k.pre))
            iterations(pe, heads)

        def take_values(eng, copy, me, u, unit, sched, i):
            kind, s, t, p = unit
            before = sched is pre
            eng.wait_ge(unit_done.sem, unit_done.before(u + 1) if before else unit_done.at(i, u + 1))
            if not before:
                eng.wait_ge(valued.sem, valued.at(i, 0 if s == 1 else H))
            kn, w = KTS[t][1], layer.v_cols
            copy(vt[s][0:kn, t, p * w:(p + 1) * w], bank_of(u, before)[0:kn, 0:w]).then_inc(taken[me].sem, 1)

        @block.scalar
        def _(act):
            def upper(u, unit, sched, i):
                kind, s, t, p = unit
                before = sched is pre
                source = whole_ready if n == 0 else unit_done
                k = sched.split[u] if n == 0 else u + 1
                act.wait_ge(source.sem, source.before(k) if before else source.at(i, k))
                if not before:
                    act.wait_ge(scored.sem, queries_free(i, t) if kind == "Q" else keys_free(i, s, t))
                src = whole[kind] if n == 0 else bank_of(u, before)
                if kind == "Q" and n == 0:
                    ins = nc.scalar.copy(parts[0][:, :], src[:, :])
                elif kind == "Q":
                    for half in range(2):
                        r, o = halves(half)
                        for to in (r, o):
                            ins = nc.scalar.copy(q_hi[to, 2 * t + half, :], src[r, 0:2 * S])
                else:
                    for half in range(2):
                        r, o = halves(half)
                        ins = nc.scalar.copy(kt[r, 2 * t + half, 0:L], src[r, 0:L])
                ins.then_inc(hi_ready.sem, 1)

            def take(u, unit, sched, i):
                if unit[0] in ("Q", "K"):
                    upper(u, unit, sched, i)
                elif sched.owner[u][0] == "A":
                    take_values(act, nc.scalar.copy, "A", u, unit, sched, i)

            def heads(i, sched):
                for g in range(len(sched.slots)):
                    lag = lagging(g, LT, i)
                    if lag:
                        j, t = lag
                        act.wait_ge(turned.sem, turned.at(j, t + 1))
                        act.wait_ge(valued.sem, valued.at(j, t + 1 - N_PT))
                        kl = KTS[-1][1]
                        nc.scalar.copy(pt[0:P, t % N_PT, 0:(KT_N - 1) * S], ps_t[0:P, 0:(KT_N - 1) * S])
                        nc.scalar.copy(pt[0:kl, t % N_PT, (KT_N - 1) * S:KT_N * S],
                                       ps_t[0:kl, (KT_N - 1) * S:KT_N * S]).then_inc(pt_ready.sem, 1)
                    lag = lagging(g, LE, i)
                    if lag:
                        j, r = lag
                        k = r % N_PB
                        act.wait_ge(maxed.sem, maxed.at(j, r + 1))
                        nc.scalar.activation(prob[0:S, k, :], prob[0:S, k, :], ACT.Exp, bias=low[0:S, k:k + 1], scale=-1.0,
                                             accum_out=total[0:S, k:k + 1]).then_inc(exped.sem, 1)
                    for args in units_of(i, g - 2 if n == 0 else g, sched):
                        take(*args)

            for k in [exped, pt_ready, hi_ready] + [taken["A"]] * (taken["A"].per > 0):
                k.credit(act)
            if n == 1:
                for s, w in enumerate("kv"):
                    act.wait_ge(w_in[s], 16)
                    for k in range(DK):
                        nc.scalar.copy(w_parts[w][0][:, k, :], vt[s][:, k, :]).then_inc(w_hi, 1)
            for u, unit in enumerate(pre.units):
                take(u, unit, pre, 0)
            iterations(act, heads)

        @block.vector
        def _(dve):
            def lower(u, unit, sched, i):
                kind, s, t, p = unit
                before = sched is pre
                dve.wait_ge(hi_ready.sem, hi_ready.before(sched.split[u]) if before else hi_ready.at(i, sched.split[u]))
                bank = bank_of(u, before)
                for half in range(2):
                    r, o = halves(half)
                    c = 2 * t + half
                    if kind == "Q":
                        for to in (r, o):
                            ins = nc.vector.tensor_tensor(q_lo[to, c, :], bank[r, 0:2 * S], q_hi[r, c, :], ALU.subtract)
                    else:
                        ins = nc.vector.tensor_tensor(kt[o, c, 0:L], bank[r, 0:L], kt[r, c, 0:L], ALU.subtract)
                ins.then_inc(taken["D"].sem, 1)

            def count_taken(sched, u, i):
                k, units = sched.owner[u][1] - 1, taken["D"]
                dve.wait_ge(units.sem, units.before(k) if sched is pre else units.at(i, k))
                dve.sem_inc(units.sem, 1)

            def make_whole(u, unit, sched, i):
                kind, s, t, p = unit
                before = sched is pre
                bank = bank_of(u, before)
                dve.wait_ge(unit_done.sem, unit_done.before(u + 1) if before else unit_done.at(i, u + 1))
                k = sched.split[u] - 1
                same = [sched.split[w] for w in range(u) if sched.units[w][0] == kind]
                if not same and not before:
                    same = [full.split[w] - full.splits for w in range(n_units) if full.units[w][0] == kind]
                if same:
                    dve.wait_ge(lo_ready.sem, lo_ready.before(same[-1]) if before else lo_ready.at(i, same[-1]))
                if kind == "Q":
                    ins = nc.vector.tensor_scalar(whole["Q"][:, :], bank[:, 0:2 * S], T["bq_col"][:, t:t + 1], None, ALU.add)
                else:
                    dve.wait_ge(kept[s], 1 if before else i + 2 - s)
                    ins = nc.vector.scalar_tensor_tensor(whole["K"][:, :], bank[:, 0:L], T["bk_col"][:, t:t + 1],
                                                         keep[s][:, :], ALU.add, ALU.mult)
                ins.then_inc(whole_ready.sem, 1)
                dve.wait_ge(whole_ready.sem, whole_ready.before(k + 1) if before else whole_ready.at(i, k + 1))
                count_taken(sched, u, i)

            def take_outputs(u, unit, sched, i):
                kind, s, t, p = unit
                if no_outputs(i, p):
                    dve_own.skip(dve, 2)
                    count_taken(sched, u, i)
                    return
                bank = bank_of(u, False)
                b = 2 * (i + p) + s
                dve.wait_ge(unit_done.sem, unit_done.at(i, u + 1))
                x = T["x"][0:S, bass.ds(b * D, D)]
                bias_row = T[f"bo{n}"][0:S, :]
                if n == 0:
                    row = x
                    dve_own.link(dve, nc.vector.tensor_tensor(lin[0:S, :], bank[0:S, 0:D], bias_row, ALU.add))
                    dve_own.link(dve, nc.vector.scalar_tensor_tensor(x, lin[0:S, :], T["gate"][0:S, 0:1], x,
                                                                     ALU.mult, ALU.add))
                else:
                    row = T["xn"][0:S, bass.ds(b * D, D)]
                    dve_own.link(dve, nc.vector.tensor_tensor(row, bank[0:S, 0:D], row, ALU.add))
                    nc.vector.tensor_tensor(x, x, T["beta"][0:S, :], ALU.add)
                    dve_own.link(dve, nc.vector.tensor_tensor(row, row, bias_row, ALU.add))
                nc.vector.bn_stats(T["stats"][0:S, bass.ds(b * 6, 6)], row).then_inc(taken["D"].sem, 1)

            def take(u, unit, sched, i):
                if unit[0] in ("Q", "K"):
                    (make_whole if n == 0 else lower)(u, unit, sched, i)
                elif unit[0] == "W":
                    take_outputs(u, unit, sched, i)
                elif unit[0] == "none":
                    count_taken(sched, u, i)
                elif sched.owner[u][0] == "D":
                    take_values(dve, nc.vector.tensor_copy, "D", u, unit, sched, i)

            def heads(i, sched):
                dve_own.begin(i)
                for g in range(len(sched.slots)):
                    if g < HEADS:
                        s = g // H
                        if g % H == 0:
                            dve.wait_ge(biased[s], i + 1)
                        dve.wait_ge(scored.sem, scored.at(i, g + 1))
                        dve.wait_ge(turned.sem, turned.at(i, g + 1 - N_PB))
                        apart(dve)
                        nc.vector.tensor_tensor_reduce(out=prob[0:S, g % N_PB, :], in0=ps_s[g % 2][0:S, 0:L],
                                                       in1=bias[s][0:S, :], scale=-layer.scale, scalar=BIG,
                                                       op0=ALU.add, op1=ALU.min,
                                                       accum_out=low[0:S, g % N_PB:g % N_PB + 1]).then_inc(maxed.sem, 1)
                    lag = lagging(g, LE + 1, i)
                    if lag:
                        j, r = lag
                        k = r % N_PB
                        dve.wait_ge(exped.sem, exped.at(j, r + 1))
                        nc.vector.reciprocal(inv[0:S, k:k + 1], total[0:S, k:k + 1]).then_inc(inverted.sem, 1)
                    lag = lagging(g, LE + 2, i)
                    if lag:
                        j, r = lag
                        k = r % N_PB
                        dve.wait_ge(inverted.sem, inverted.at(j, r + 1))
                        nc.vector.tensor_scalar(prob[0:S, k, :], prob[0:S, k, :], inv[0:S, k:k + 1], None,
                                                ALU.mult).then_inc(normed.sem, 1)
                    lag = lagging(g, LP + 1, i)
                    if lag and lag[1] % per_group == per_group - 1:
                        j, v = lag
                        group = v // per_group
                        b, part = v // H, group % layer.groups
                        dve.wait_ge(valued.sem, valued.at(j, v + 1))
                        if b == 0:
                            dve.wait_ge(unit_done.sem, unit_done.at(j - 1, full.units.index(("W", 0, 0, 0)) + 1))
                        else:
                            dve.wait_ge(unit_done.sem, unit_done.at(j, full.units.index(("W", 1, 0, -1)) + 1))
                        dst = ot[b][:, part * 4:part * 4 + 4, :]
                        src = ps_o[group % 2][:, 0:4 * S].rearrange("p (t s) -> p t s", t=4)
                        if n == 0:
                            bv = T["bv_out"][:, :].unsqueeze(2).to_broadcast((P, 4, S))
                            ins = nc.vector.tensor_tensor(dst, src, bv, ALU.add)
                        else:
                            ins = nc.vector.tensor_copy(dst, src)
                        ins.then_inc(out_ready.sem, 1)
                    for args in units_of(i, g - 1, sched):
                        take(*args)
                if sched is final:
                    for args in units_of(i, g, sched):
                        take(*args)

            for k in [maxed, inverted, normed, out_ready, taken["D"]] + ([whole_ready] if n == 0 else []):
                k.credit(dve)
            if n == 1:
                for m, w in enumerate("kv"):
                    for k in range(DK):
                        dve.wait_ge(w_hi, m * DK + k + 1)
                        nc.vector.tensor_tensor(w_parts[w][1][:, k, :], vt[m][:, k, :], w_parts[w][0][:, k, :],
                                                ALU.subtract).then_inc(w_ready, 1)
            for u, unit in enumerate(pre.units):
                take(u, unit, pre, 0)
            iterations(dve, heads)

    ctx.close()


class Norm:

    GROUPS, PER = 4, 4

    def __init__(self, nc, T, nm, ctx, banks):
        self.nc, self.T, self.banks = nc, T, banks
        self.mv = ctx.enter_context(nc.sbuf_tensor(nm + "mv", [P, B, 2], F32))
        self.dev = ctx.enter_context(nc.sbuf_tensor(nm + "dev", [P, 2, B], F32))
        self.rs = ctx.enter_context(nc.sbuf_tensor(nm + "rs", [P, B], F32))
        self.shift = ctx.enter_context(nc.sbuf_tensor(nm + "shift", [P, B], F32))
        self.own = Chain(nc, nm + "norm_own")
        self.var_ready = nc.alloc_semaphore(nm + "var_ready")
        self.root_ready = nc.alloc_semaphore(nm + "root_ready")
        self.shift_ready = nc.alloc_semaphore(nm + "shift_ready")
        self.normed = nc.alloc_semaphore(nm + "normed")
        self.turned = nc.alloc_semaphore(nm + "turned")
        self.turns = 0

    def moments(self, dve, q, x=None):
        nc, T = self.nc, self.T
        r = range(q * self.PER, (q + 1) * self.PER)
        if x is not None:
            for b in r:
                last = self.own.mark(nc.vector.bn_stats(T["stats"][0:S, b * 6:b * 6 + 6], x[0:S, b * D:(b + 1) * D]))
            dve.wait_ge(self.own.sem, last)
        for b in r:
            last = self.own.mark(nc.vector.bn_aggr(self.mv[0:S, b, :], T["stats"][0:S, b * 6:b * 6 + 6]))
        dve.wait_ge(self.own.sem, last)

    def scales(self, dve, q, nth, factor, eps, eps_after):
        nc, g = self.nc, slice(q * self.PER, (q + 1) * self.PER)
        nc.vector.tensor_scalar(self.dev[0:S, 0, g], self.mv[0:S, g, 1], factor, eps, ALU.mult,
                                ALU.add).then_inc(self.var_ready, 1)
        dve.wait_ge(self.root_ready, nth + 1)
        self.own.link(dve, nc.vector.tensor_scalar(self.rs[0:S, g], self.dev[0:S, 1, g], eps_after, None, ALU.add))
        self.own.link(dve, nc.vector.reciprocal(self.rs[0:S, g], self.rs[0:S, g]))
        nc.vector.scalar_tensor_tensor(self.shift[0:S, g], self.mv[0:S, g, 0], -1.0, self.rs[0:S, g], ALU.mult,
                                       ALU.mult).then_inc(self.shift_ready, 1)

    def roots(self, act, q, nth):
        g = slice(q * self.PER, (q + 1) * self.PER)
        act.wait_ge(self.var_ready, nth + 1)
        self.nc.scalar.activation(self.dev[0:S, 1, g], self.dev[0:S, 0, g], ACT.Sqrt).then_inc(self.root_ready, 1)

    def apply(self, act, q, nth, src, dst):
        act.wait_ge(self.shift_ready, nth + 1)
        for b in range(q * self.PER, (q + 1) * self.PER):
            c = slice(b * D, (b + 1) * D)
            ins = self.nc.scalar.activation(dst[0:S, c], src[0:S, c], ACT.Identity, scale=self.rs[0:S, b:b + 1],
                                            bias=self.shift[0:S, b:b + 1])
        ins.then_inc(self.normed, 1)

    def turn(self, pe, q, nth):
        nc, T = self.nc, self.T
        pe.wait_ge(self.normed, nth)
        for k in range(DK):
            for j in range(self.PER):
                c = (q * self.PER + j) * D + k * P
                ins = nc.tensor.transpose(self.banks[q * DK + k][:, j * S:(j + 1) * S], T["xn"][0:S, c:c + P],
                                          T["ident"][0:S, 0:S])
            ins.then_inc(self.turned, 1)

    def keep(self, eng, copy, q, k):
        eng.wait_ge(self.turned, q * DK + k + 1)
        w = self.PER * S
        return copy(self.T["xn_t"][:, k, q * w:(q + 1) * w], self.banks[q * DK + k][:, 0:w])


def normalise(nc, T, nm, z_first, from_x):
    with ExitStack() as ctx:
        banks = [ctx.enter_context(nc.psum_tensor(f"{nm}bank{k}", [P, 512], F32)) for k in range(8)]
        norm = Norm(nc, T, nm, ctx, banks)
        q_all = range(Norm.GROUPS)
        n_z = Norm.GROUPS if z_first else 0

        with nc.Block() as block:

            @block.vector
            def _(dve):
                if z_first:
                    for q in q_all:
                        norm.moments(dve, q)
                        norm.scales(dve, q, q, D / (D - 1.0), 0.0, Z_EPS)
                for q in q_all:
                    if z_first:
                        c = slice(q * 4 * D, (q + 1) * 4 * D)
                        z = T["xn"][0:S, c]
                        z3 = z.rearrange("p (b d) -> p b d", b=4)
                        dve.wait_ge(norm.normed, q + 1)
                        norm.own.link(dve, nc.vector.tensor_tensor(
                            z3, z3, T["gamma"][0:S, :].unsqueeze(1).to_broadcast((S, 4, D)), ALU.mult))
                        norm.own.link(dve, nc.vector.tensor_tensor(T["x"][0:S, c], T["x"][0:S, c], z, ALU.add))
                    if from_x:
                        dve.wait_ge(T["x_in"][q], 16)
                    norm.moments(dve, q, T["x"] if from_x or z_first else None)
                    norm.scales(dve, q, n_z + q, 1.0, LN_EPS, 0.0)
                for q in q_all:
                    norm.keep(dve, nc.vector.tensor_copy, q, 1)

            @block.scalar
            def _(act):
                if z_first:
                    for q in q_all:
                        norm.roots(act, q, q)
                        norm.apply(act, q, q, T["xn"], T["xn"])
                for q in q_all:
                    norm.roots(act, q, n_z + q)
                    norm.apply(act, q, n_z + q, T["x"], T["xn"])
                    if q:
                        norm.keep(act, nc.scalar.copy, q - 1, 0)
                norm.keep(act, nc.scalar.copy, Norm.GROUPS - 1, 0)

            @block.tensor
            def _(pe):
                pe.wait_ge(T["ident_ready"], 1)
                for q in q_all:
                    norm.turn(pe, q, n_z + q + 1)


def feed_forward(nc, n, T, D_, out):
    nm = f"f{n}_"
    ctx = ExitStack()

    def sb(name, shape, dt=F32):
        return ctx.enter_context(nc.sbuf_tensor(nm + name, shape, dt))

    logits, top, ex = sb("logits", [P, B, E]), sb("top", [P, B, E]), sb("ex", [P, B, E])
    idx, chosen = sb("idx", [P, B, E], U32), sb("chosen", [P, 2, B])
    weight = sb("weight", [P, 2, B])
    denom = sb("denom", [P, B])
    hot = sb("hot", [P, 2, B, E])
    tot = sb("tot", [P, 2, B, E])
    run = [sb(f"run{k}", [P, 2, B, E]) for k in range(2)]
    rank = sb("rank", [P, 2, B, E])
    picked = sb("picked", [P, 2, B])
    slot, row, valid = sb("slot", [P, 2, B]), sb("row", [P, 2, B]), sb("valid", [P, 2, B])
    scat, gath = sb("scat", [P, 2, B], U32), sb("gath", [P, 2, B], U32)
    drop_row = sb("drop_row", [P, 2, B])
    need, need_i, ends = sb("need", [P, E]), sb("need_i", [P, E], I32), [sb(f"ends{k}", [P, E]) for k in range(2)]
    step = sb("step", [P, TILES])
    before = sb("before", [P, TILES, E])
    owner_f, owner_i = sb("owner_f", [P, TILES]), sb("owner_i", [P, TILES], I32)
    NG = 4
    got = [[sb(f"got{k}_{s}", [P, D]) for s in range(NG)] for k in range(2)]
    ps = [ctx.enter_context(nc.psum_tensor(f"{nm}ps{k}", [P, 512], F32)) for k in range(8)]

    logits_done, hot_ready, ranked = (nc.alloc_semaphore(nm + k) for k in ("logits_done", "hot_ready", "ranked"))
    diff_ready, ex_ready = nc.alloc_semaphore(nm + "diff_ready"), nc.alloc_semaphore(nm + "ex_ready")
    rows_ready, dispatched = nc.alloc_semaphore(nm + "rows_ready"), nc.alloc_semaphore(nm + "dispatched")
    iotas = nc.alloc_semaphore(nm + "iotas")
    stored = nc.alloc_semaphore(nm + "stored")
    gathered = [nc.alloc_semaphore(f"{nm}gathered{s}") for s in range(NG)]
    added = nc.alloc_semaphore(nm + "added")
    out_done = nc.alloc_semaphore(nm + "out_done")
    own = Chain(nc, nm + "own")
    apart = T["apart"]
    XS, YS = D_[f"xs{n}"], D_[f"ys{n}"]

    def route(dve):
        v = nc.vector
        dve.wait_ge(logits_done, 1)
        own.link(dve, v.tensor_copy(logits[0:S, :, :].rearrange("p b e -> p (b e)"), ps[0][0:S, 0:B * E]))
        for b in range(B):
            last = own.mark(v.max(top[0:S, b, :], logits[0:S, b, :]))
        dve.wait_ge(own.sem, last)
        for b in range(B):
            last = own.mark(v.max_index(idx[0:S, b, :], top[0:S, b, :], logits[0:S, b, :]))
        v.tensor_tensor(ex[0:S, :, :], top[0:S, :, :], top[0:S, :, 0:1].to_broadcast((S, B, E)),
                        ALU.subtract).then_inc(diff_ready, 1)
        dve.wait_ge(own.sem, last)
        own.link(dve, v.tensor_copy(chosen[0:S, :, :].rearrange("p k b -> p b k"), idx[0:S, :, 0:2]))
        dve.wait_ge(iotas, 3)
        shape = (S, 2, B, E)
        for k in range(2):
            ins = v.tensor_tensor(hot[0:S, k, :, :], T["experts"][0:S, :].unsqueeze(1).to_broadcast((S, B, E)),
                                  chosen[0:S, k, :].unsqueeze(2).to_broadcast((S, B, E)), ALU.is_equal)
            ins.then_inc(hot_ready, 1)
        dve.wait_ge(ex_ready, 1)
        own.link(dve, v.tensor_reduce(denom[0:S, :], ex[0:S, :, 0:(2 if n == 0 else E)], AX.X, ALU.add))
        own.link(dve, v.reciprocal(denom[0:S, :], denom[0:S, :]))
        own.link(dve, v.tensor_scalar(weight[0:S, 0, :], denom[0:S, :], T["gate"][0:S, 2 * n + 1:2 * n + 2], None, ALU.mult))
        own.link(dve, v.tensor_tensor(weight[0:S, 1, :], weight[0:S, 0, :], ex[0:S, :, 1], ALU.mult))
        dve.wait_ge(ranked, 1)
        flat = "p k b e -> p (k b e)"
        own.link(dve, v.tensor_copy(tot[0:S, :, :, :].rearrange(flat), ps[2][0:S, 0:2 * B * E]))
        own.link(dve, v.tensor_copy(run[0][0:S, :, :, :].rearrange(flat), ps[2][0:S, 0:2 * B * E]))
        a = 0
        for d in (1, 2, 4, 8):
            src, dst = run[a], run[1 - a]
            own.mark(v.tensor_copy(dst[0:S, :, 0:d, :], src[0:S, :, 0:d, :]))
            for k in range(2):
                last = own.mark(v.tensor_tensor(dst[0:S, k, d:B, :], src[0:S, k, d:B, :], src[0:S, k, 0:B - d, :], ALU.add))
            dve.wait_ge(own.sem, last)
            a = 1 - a
        run_t = run[a]
        own.link(dve, v.tensor_tensor(rank[0:S, :, :, :].rearrange(flat), ps[1][0:S, 0:2 * B * E],
                                      run_t[0:S, :, :, :].rearrange(flat), ALU.add))
        own.link(dve, v.tensor_tensor(rank[0:S, :, :, :].rearrange(flat), rank[0:S, :, :, :].rearrange(flat),
                                      tot[0:S, :, :, :].rearrange(flat), ALU.subtract))
        own.link(dve, v.tensor_tensor(rank[0:S, 1, :, :], rank[0:S, 1, :, :],
                                      run_t[0:S, 0, B - 1:B, :].to_broadcast((S, B, E)), ALU.add))
        if n == 1:
            own.link(dve, v.tensor_tensor(need[0:S, :], run_t[0:S, 0, B - 1, :], run_t[0:S, 1, B - 1, :], ALU.add))
            own.link(dve, v.tensor_scalar(need_i[0:S, :], need[0:S, :], float(P - 1), None, ALU.add))
            own.link(dve, v.tensor_scalar(need_i[0:S, :], need_i[0:S, :], 7, None, ALU.arith_shift_right))
            own.link(dve, v.tensor_copy(need[0:S, :], need_i[0:S, :]))
            own.link(dve, v.tensor_copy(ends[0][0:S, :], need_i[0:S, :]))
            a = 0
            for d in (1, 2, 4):
                own.mark(v.tensor_copy(ends[1 - a][0:S, 0:d], ends[a][0:S, 0:d]))
                own.link(dve, v.tensor_tensor(ends[1 - a][0:S, d:E], ends[a][0:S, d:E], ends[a][0:S, 0:E - d], ALU.add))
                a = 1 - a
            end = ends[a]
            own.link(dve, v.tensor_tensor(before[0:S, :, :], end[0:S, :].unsqueeze(1).to_broadcast((S, TILES, E)),
                                          step[0:S, :].unsqueeze(2).to_broadcast((S, TILES, E)), ALU.is_le))
            own.link(dve, v.tensor_reduce(owner_f[0:S, :], before[0:S, :, :], AX.X, ALU.add))
            own.link(dve, v.tensor_scalar(owner_i[0:S, :], owner_f[0:S, :], float(E - 1), None, ALU.min))
            own.link(dve, v.tensor_tensor(need[0:S, :], end[0:S, :], need[0:S, :], ALU.subtract))
            own.link(dve, v.tensor_scalar(need[0:S, :], need[0:S, :], float(P), None, ALU.mult))
            for k in range(2):
                last = own.mark(v.tensor_tensor(rank[0:S, k, :, :], rank[0:S, k, :, :],
                                                need[0:S, :].unsqueeze(1).to_broadcast((S, B, E)), ALU.add))
            dve.wait_ge(own.sem, last)
        own.link(dve, v.tensor_tensor(rank[0:S, :, :, :].rearrange(flat), rank[0:S, :, :, :].rearrange(flat),
                                      hot[0:S, :, :, :].rearrange(flat), ALU.mult))
        own.link(dve, v.tensor_reduce(picked[0:S, :, :], rank[0:S, :, :, :], AX.X, ALU.add))
        if n == 0:
            own.link(dve, v.tensor_scalar(valid[0:S, :, :], picked[0:S, :, :], float(CAP), None, ALU.is_lt))
            own.link(dve, v.scalar_tensor_tensor(slot[0:S, :, :], chosen[0:S, :, :], float(SLOTS), picked[0:S, :, :],
                                                 ALU.mult, ALU.add))
            own.link(dve, v.tensor_tensor(weight[0:S, :, :], weight[0:S, :, :], valid[0:S, :, :], ALU.mult))
            own.link(dve, v.tensor_tensor(row[0:S, :, :], slot[0:S, :, :], drop_row[0:S, :, :], ALU.subtract))
            own.link(dve, v.tensor_tensor(row[0:S, :, :], row[0:S, :, :], valid[0:S, :, :], ALU.mult))
            own.link(dve, v.tensor_tensor(scat[0:S, :, :], row[0:S, :, :], drop_row[0:S, :, :], ALU.add))
            own.link(dve, v.tensor_tensor(gath[0:S, :, :], slot[0:S, :, :], valid[0:S, :, :], ALU.mult))
        else:
            own.link(dve, v.tensor_copy(scat[0:S, :, :], picked[0:S, :, :]))
            own.link(dve, v.tensor_copy(gath[0:S, :, :], picked[0:S, :, :]))
        dve.sem_inc(rows_ready, 1)

    def pool_dispatch(pool):
        pool.iota(drop_row[0:S, :, :], pattern=[[B * S, 2], [S, B]], base=DROP0, channel_multiplier=1,
                  allow_small_or_imprecise_dtypes=True).then_inc(iotas, 1)
        pool.iota(step[0:S, :], pattern=[[1, TILES]], base=0, channel_multiplier=0,
                  allow_small_or_imprecise_dtypes=True).then_inc(iotas, 1)
        pool.iota(T["experts"][0:S, :], pattern=[[1, E]], base=0, channel_multiplier=0,
                  allow_small_or_imprecise_dtypes=True).then_inc(iotas, 1)
        pool.wait_ge(D_["cleared"], D_["cleared_value"])
        pool.wait_ge(rows_ready, 1)
        for k in range(2):
            for b in range(B):
                pool.indirect_dma_start(out=XS[:, :], out_offset=bass.IndirectOffsetOnAxis(ap=scat[0:S, k, b:b + 1], axis=0),
                                        in_=T["xn"][0:S, b * D:(b + 1) * D], in_offset=None).then_inc(dispatched, 16)

    def pool_gather(pool, stores):
        pool.wait_ge(stored, 16 * stores)
        for b in range(B):
            s = b % NG
            if b >= NG:
                pool.wait_ge(added, b - NG + 1)
            for k in range(2):
                pool.indirect_dma_start(out=got[k][s][0:S, :], out_offset=None, in_=YS[:, :],
                                        in_offset=bass.IndirectOffsetOnAxis(ap=gath[0:S, k, b:b + 1], axis=0)).then_inc(gathered[s], 16)

    norm = Norm(nc, T, nm, ctx, ps) if n == 0 else None

    def combine(dve):
        for b in range(B):
            s = b % NG
            dve.wait_ge(gathered[s], 32 * (b // NG + 1))
            x = T["x"][0:S, b * D:(b + 1) * D]
            own.link(dve, nc.vector.scalar_tensor_tensor(x, got[0][s][0:S, :], weight[0:S, 0, b:b + 1], x, ALU.mult, ALU.add))
            nc.vector.scalar_tensor_tensor(x, got[1][s][0:S, :], weight[0:S, 1, b:b + 1], x, ALU.mult,
                                           ALU.add).then_inc(added, 1)
            if norm and b % 4 == 3:
                dve.wait_ge(added, b + 1)
                norm.moments(dve, b // 4, T["x"])
                norm.scales(dve, b // 4, b // 4, 1.0, LN_EPS, 0.0)

    def logits_and_ranks(pe):
        for b in range(B):
            for k in range(DK):
                ins = nc.tensor.matmul(ps[0][0:S, b * E:(b + 1) * E], T["xn_t"][:, k, b * S:(b + 1) * S],
                                       T[f"wr{n}"][:, k, :], start=k == 0, stop=k == DK - 1)
        ins.then_inc(logits_done, 1)
        pe.wait_ge(hot_ready, 2)
        one_hots = hot[0:S, :, :, :].rearrange("p k b e -> p (k b e)")
        nc.tensor.matmul(ps[1][0:S, 0:2 * B * E], T["earlier"][0:S, 0:S], one_hots, start=True, stop=True)
        nc.tensor.matmul(ps[2][0:S, 0:2 * B * E], T["ones"][0:S, 0:S], one_hots, start=True, stop=True).then_inc(ranked, 1)

    def exps(act):
        act.wait_ge(diff_ready, 1)
        nc.scalar.activation(ex[0:S, :, :], ex[0:S, :, :], ACT.Exp).then_inc(ex_ready, 1)

    if n == 0:
        w1, w2 = T["w1_0"], T["w2_0"]
        NF = F0 // P
        xe = [sb(f"xe{s}", [P, 4, D]) for s in range(2)]
        xt = [sb(f"xt{k}", [P, DK, SLOTS], F32R) for k in range(2)]
        w1_parts = [sb(f"w1_part{k}", [P, DK, F0], F32R) for k in range(2)]
        w2_parts = [sb(f"w2_part{k}", [P, NF, D], F32R) for k in range(2)]
        NH = 4
        hidden = [sb(f"hidden{k}", [P, SLOTS]) for k in range(NH)]
        ht = [sb(f"ht{k}", [P, NF, SLOTS], F32R) for k in range(2)]
        ye = sb("ye", [P, 4, D])
        rows_in = [nc.alloc_semaphore(f"{nm}rows_in{s}") for s in range(2)]
        w_in = T["w_in"]
        x_turned = Counted(nc, nm + "x_turned", 2, 1)
        xt_hi = Counted(nc, nm + "xt_hi", 2, 1)
        xt_ready = Counted(nc, nm + "xt_ready", 2, 1)
        w1_hi = Counted(nc, nm + "w1_hi", 2 * DK, DK)
        w1_ready = Counted(nc, nm + "w1_ready", 2 * DK, DK)
        w2_hi = Counted(nc, nm + "w2_hi", 4)
        w2_ready = Counted(nc, nm + "w2_ready", 4)
        up_done = Counted(nc, nm + "up_done", 2 * NF)
        gelu_done = Counted(nc, nm + "gelu_done", 2 * NF)
        h_hi = Counted(nc, nm + "h_hi", 2 * NF)
        h_ready = Counted(nc, nm + "h_ready", 2 * NF)
        down_done = Counted(nc, nm + "down_done", 8)
        y_ready = Counted(nc, nm + "y_ready", 8)
        y_out = [nc.alloc_semaphore(f"{nm}y_out{s}") for s in range(2)]
        X4 = XS[0:ROWS, :].rearrange("(e p j) d -> p e j d", e=E, j=4)
        Y4 = YS[0:ROWS, :].rearrange("(e p j) d -> p e j d", e=E, j=4)

        def experts(eng, step):
            with eng.Fori(0, E // 2 - 1) as i:
                step(i, 0, True, True)
                step(i, 1, True, True)
            step(E // 2 - 1, 0, True, False)
            step(E // 2 - 1, 1, False, False)

        with nc.Block() as block:

            @block.sync
            def _(sp):
                def load_rows(e, s):
                    sp.dma_start(xe[s][:, :, :], X4[:, bass.ds(e, 1), :, :].rearrange("p e j d -> p (e j) d")).then_inc(rows_in[s], 16)

                def step(i, s, more, two):
                    if two:
                        wait(sp, x_turned, i, s)
                        apart(sp)
                        load_rows(2 * i + s + 2, s)
                        sp.wait_ge(w1_ready.sem, w1_ready.at(i, DK * s))
                        apart(sp)
                        sp.dma_start(w1[s][:, :, :], D_["c_fc"][bass.ds(2 * i + s + 2, 1), :, :, :].rearrange(
                            "e p k f -> p (e k) f")).then_inc(w_in[s], 16)
                        sp.wait_ge(w2_ready.sem, w2_ready.at(i, 2 * (s + 1)))
                        apart(sp)
                        sp.dma_start(w2[s][:, :, :], D_["c_proj"][bass.ds(2 * i + s + 2, 1), :, :, :].rearrange(
                            "e p f d -> p (e f) d")).then_inc(w_in[s], 16)
                    sp.wait_ge(y_ready.sem, y_ready.at(i, 4 * (s + 1)))
                    apart(sp)
                    sp.dma_start(Y4[:, bass.ds(2 * i + s, 1), :, :].rearrange("p e j d -> p (e j) d"), ye[:, :, :]).then_inc(y_out[s], 16)

                sp.wait_ge(dispatched, 16 * 2 * B)
                load_rows(0, 0)
                load_rows(1, 1)
                for s in range(2):
                    sp.sem_inc(y_out[s], 16)
                experts(sp, step)
                for s in range(2):
                    sp.wait_ge(y_out[s], 16 * (E // 2 + 1))
                sp.sem_inc(stored, 16)

            @block.gpsimd
            def _(pool):
                w2_hi.credit(pool)
                pool_dispatch(pool)

                def step(i, s, more, two):
                    pool.wait_ge(w_in[s], 32 * (i + 1))
                    pool.wait_ge(down_done.sem, down_done.at(i, 4 * s))
                    apart(pool)
                    for c in range(2):
                        f = slice(c * NF // 2, (c + 1) * NF // 2)
                        nc.gpsimd.tensor_copy(w2_parts[0][:, f, :], w2[s][:, f, :]).then_inc(w2_hi.sem, 1)

                experts(pool, step)
                pool_gather(pool, 1)

            @block.tensor
            def _(pe):
                for k in (x_turned, up_done, down_done):
                    k.credit(pe)
                logits_and_ranks(pe)

                def turn(rows, s, taken_before):
                    pe.wait_ge(rows_in[s], 16 * rows)
                    pe.wait_ge(xt_ready.sem, taken_before)
                    for k in range(DK):
                        for j in range(4):
                            ins = nc.tensor.transpose(ps[k][:, j * P:(j + 1) * P], xe[s][:, j, k * P:(k + 1) * P], T["ident"][:, :])
                    ins.then_inc(x_turned.sem, 1)

                def step(i, s, more, two):
                    pe.wait_ge(xt_ready.sem, xt_ready.at(i, s))
                    pe.wait_ge(w1_ready.sem, w1_ready.at(i, DK * s))
                    for f in range(NF):
                        pe.wait_ge(gelu_done.sem, gelu_done.at(i, s * NF + f - 1))
                        for m, (k, (a, b)) in enumerate((k, ab) for k in range(DK) for ab in PASSES):
                            ins = nc.tensor.matmul(ps[2 + f % 2][:, :], w1_parts[a][:, k, f * P:(f + 1) * P], xt[b][:, k, :],
                                                   start=m == 0, stop=m == DK * len(PASSES) - 1)
                        ins.then_inc(up_done.sem, 1)
                    if more:
                        turn(i + 1 + s, 1 - s, xt_ready.at(i, s))
                    for j in range(4):
                        pe.wait_ge(y_ready.sem, y_ready.at(i, s * 4 + j - 1))
                        for m, (f, (a, b)) in enumerate((f, ab) for f in range(NF) for ab in PASSES):
                            if j == 0 and m % len(PASSES) == 0:
                                pe.wait_ge(h_ready.sem, h_ready.at(i, s * NF + f + 1))
                                if f % (NF // 2) == 0:
                                    pe.wait_ge(w2_ready.sem, w2_ready.at(i, 2 * s + f // (NF // 2) + 1))
                            ins = nc.tensor.matmul(ps[4 + j % 2][:, 0:D], ht[a][:, f, j * P:(j + 1) * P], w2_parts[b][:, f, :],
                                                   start=m == 0, stop=m == NF * len(PASSES) - 1)
                        ins.then_inc(down_done.sem, 1)

                pe.wait_ge(ranked, 1)
                turn(1, 0, xt_ready.before(0))
                experts(pe, step)
                for q in range(Norm.GROUPS):
                    norm.turn(pe, q, q + 1)

            @block.scalar
            def _(act):
                for k in (gelu_done, xt_hi, w1_hi, h_hi):
                    k.credit(act)

                def next_rows(i, s):
                    act.wait_ge(x_turned.sem, x_turned.at(i, s + 1) if i is not None else x_turned.before(1))
                    if i is not None:
                        act.wait_ge(up_done.sem, up_done.at(i, (s + 1) * NF))
                    for k in range(DK):
                        ins = nc.scalar.copy(xt[0][:, k, :], ps[k][:, :])
                    ins.then_inc(xt_hi.sem, 1)

                def next_weights(i, s):
                    if i is None:
                        act.wait_ge(w_in[0], 32)
                    else:
                        act.wait_ge(w_in[1 - s], 32 * (i + 1 + s))
                        act.wait_ge(up_done.sem, up_done.at(i, (s + 1) * NF))
                    for k in range(DK):
                        nc.scalar.copy(w1_parts[0][:, k, :], w1[1 - s][:, k, :]).then_inc(w1_hi.sem, 1)

                def step(i, s, more, two):
                    def upper(f):
                        act.wait_ge(down_done.sem, down_done.at(i, s * 4))
                        act.wait_ge(gelu_done.sem, gelu_done.at(i, s * NF + f + 1))
                        nc.scalar.copy(ht[0][:, f, :], hidden[f % NH][:, :]).then_inc(h_hi.sem, 1)

                    for f in range(NF):
                        act.wait_ge(up_done.sem, up_done.at(i, s * NF + f + 1))
                        act.wait_ge(h_ready.sem, h_ready.at(i, s * NF + f + 1 - NH))
                        nc.scalar.activation(hidden[f % NH][:, :], ps[2 + f % 2][:, :], ACT.Gelu).then_inc(gelu_done.sem, 1)
                        if f:
                            upper(f - 1)
                    upper(NF - 1)
                    if more:
                        next_rows(i, s)
                        next_weights(i, s)

                next_weights(None, 1)
                exps(act)
                next_rows(None, 1)
                experts(act, step)
                for q in range(Norm.GROUPS):
                    norm.roots(act, q, q)
                    norm.apply(act, q, q, T["x"], T["xn"])
                    for k in range(DK * (q > 0)):
                        norm.keep(act, nc.scalar.copy, q - 1, k)
                for k in range(DK):
                    norm.keep(act, nc.scalar.copy, Norm.GROUPS - 1, k)

            @block.vector
            def _(dve):
                for k in (xt_ready, w1_ready, w2_ready, h_ready, y_ready):
                    k.credit(dve)

                def next_rows(i, s):
                    dve.wait_ge(xt_hi.sem, xt_hi.at(i, s + 1) if i is not None else xt_hi.before(1))
                    for k in range(DK):
                        ins = nc.vector.tensor_tensor(xt[1][:, k, :], ps[k][:, :], xt[0][:, k, :], ALU.subtract)
                    ins.then_inc(xt_ready.sem, 1)

                def next_weights(i, s, k):
                    dve.wait_ge(w1_hi.sem, w1_hi.at(i, DK * s + k + 1) if i is not None else w1_hi.before(k + 1))
                    nc.vector.tensor_tensor(w1_parts[1][:, k, :], w1[1 - s][:, k, :], w1_parts[0][:, k, :],
                                            ALU.subtract).then_inc(w1_ready.sem, 1)

                def step(i, s, more, two):
                    for f in range(NF):
                        dve.wait_ge(h_hi.sem, h_hi.at(i, s * NF + f + 1))
                        nc.vector.tensor_tensor(ht[1][:, f, :], hidden[f % NH][:, :], ht[0][:, f, :],
                                                ALU.subtract).then_inc(h_ready.sem, 1)
                        if f in (NF // 2 - 1, NF - 2):
                            c = int(f >= NF // 2)
                            g = slice(c * NF // 2, (c + 1) * NF // 2)
                            dve.wait_ge(w2_hi.sem, w2_hi.at(i, 2 * s + c + 1))
                            nc.vector.tensor_tensor(w2_parts[1][:, g, :], w2[s][:, g, :], w2_parts[0][:, g, :],
                                                    ALU.subtract).then_inc(w2_ready.sem, 1)
                    if more:
                        next_rows(i, s)
                        next_weights(i, s, 0)
                    for j in range(4):
                        dve.wait_ge(down_done.sem, down_done.at(i, s * 4 + j + 1))
                        if j == 0:
                            dve.wait_ge(y_out[1 - s], 16 * (i + 1 + s))
                        nc.vector.tensor_copy(ye[:, j, :], ps[4 + j % 2][:, 0:D]).then_inc(y_ready.sem, 1)
                        if j == 0 and more:
                            next_weights(i, s, 1)

                for k in range(DK):
                    next_weights(None, 1, k)
                route(dve)
                next_rows(None, 1)
                experts(dve, step)
                combine(dve)
    else:
        w1, w2 = sb("w1", [P, E * DK * F1]), sb("w2", [P, E * (F1 // P) * D])
        b1, b2 = sb("b1", [P, E * F1]), sb("b2", [P, E * D])
        NF = F1 // P
        xe = [sb(f"xe{s}", [P, D]) for s in range(2)]
        xt = [sb(f"xt{s}", [P, DK, P]) for s in range(2)]
        hb = [sb(f"hb{s}", [P, F1]) for s in range(2)]
        hg = [sb(f"hg{s}", [P, F1]) for s in range(2)]
        ht = [sb(f"ht{s}", [P, NF, P]) for s in range(2)]
        ye = [sb(f"ye{s}", [P, D]) for s in range(2)]
        w_in = nc.alloc_semaphore(nm + "w_in")
        rows_in = [nc.alloc_semaphore(f"{nm}rows_in{s}") for s in range(2)]
        y_out = [nc.alloc_semaphore(f"{nm}y_out{s}") for s in range(2)]
        x_turned, xt_ready = Counted(nc, nm + "x_turned", 2), Counted(nc, nm + "xt_ready", 2)
        up_done, b1_added = Counted(nc, nm + "up_done", 2), Counted(nc, nm + "b1_added", 2)
        gelu_done, h_turned = Counted(nc, nm + "gelu_done", 2), Counted(nc, nm + "h_turned", 2)
        ht_ready, down_done = Counted(nc, nm + "ht_ready", 2), Counted(nc, nm + "down_done", 2)
        y_ready = Counted(nc, nm + "y_ready", 2)

        with nc.Block() as block:

            @block.sync
            def _(sp):
                sp.dma_start(w1[:, :], D_["W1"]).then_inc(w_in, 16)
                sp.dma_start(w2[:, :], D_["W2"]).then_inc(w_in, 16)
                sp.dma_start(b1[:, :], D_["b1"].to_broadcast((P, E * F1))).then_inc(w_in, 16)
                sp.dma_start(b2[:, :], D_["b2"].to_broadcast((P, E * D))).then_inc(w_in, 16)
                sp.wait_ge(dispatched, 16 * 2 * B)

                def load_rows(t, s):
                    sp.dma_start(xe[s][:, :], XS[bass.ds(t * P, P), :]).then_inc(rows_in[s], 16)

                load_rows(0, 0)
                load_rows(1, 1)

                def tile(i, s, load, store):
                    if load:
                        wait(sp, x_turned, i, s + 1)
                        apart(sp)
                        load_rows(2 * i + s + 2, s)
                    if store:
                        wait(sp, y_ready, i, s - 1)
                        apart(sp)
                        sp.dma_start(YS[bass.ds((2 * i + s - 2) * P, P), :], ye[s][:, :]).then_inc(y_out[s], 16)

                for s in range(2):
                    sp.sem_inc(y_out[s], 16)
                    tile(0, s, True, False)
                with sp.Fori(1, TILES // 2 - 1) as i:
                    for s in range(2):
                        tile(i, s, True, True)
                for i in (TILES // 2 - 1, TILES // 2):
                    for s in range(2):
                        tile(i, s, False, True)
                for s in range(2):
                    sp.wait_ge(y_out[s], 16 * (TILES // 2 + 1))
                sp.sem_inc(stored, 16)
                for h in range(2):
                    sp.wait_ge(added, B // 2 * (h + 1))
                    r = slice(h * B // 2, (h + 1) * B // 2)
                    sp.dma_start(out[r, :, :].rearrange("b s d -> s b d"),
                                 T["x"][0:S, :].rearrange("p (b d) -> p b d", b=B)[:, r, :]).then_inc(out_done, 16)
                sp.wait_ge(out_done, 32)

            @block.gpsimd
            def _(pool):
                pool_dispatch(pool)
                pool_gather(pool, 1)

            @block.tensor
            def _(pe):
                for k in (x_turned, up_done, h_turned, down_done):
                    k.credit(pe)
                logits_and_ranks(pe)
                pe.wait_ge(w_in, 64)
                pe.wait_ge(rows_ready, 1)

                def turn(i, s):
                    pe.wait_ge(rows_in[s], 16 * (i + 1))
                    wait(pe, xt_ready, i, s - 1)
                    for k in range(DK):
                        ins = nc.tensor.transpose(ps[s][:, k * P:(k + 1) * P], xe[s][:, k * P:(k + 1) * P], T["ident"][:, :])
                    ins.then_inc(x_turned.sem, 1)

                def up(i, s):
                    expert = pe.value_load(owner_i[0:1, bass.ds(2 * i + s, 1)], min_val=0, max_val=E - 1)
                    wait(pe, xt_ready, i, s + 1)
                    wait(pe, b1_added, i, s - 1)
                    for k in range(DK):
                        ins = nc.tensor.matmul(ps[2 + s][:, :], xt[s][:, k, :],
                                               w1[:, bass.ds(expert * (DK * F1) + k * F1, F1)], start=k == 0, stop=k == DK - 1)
                    ins.then_inc(up_done.sem, 1)

                def turn_hidden(i, s):
                    wait(pe, gelu_done, i, s + 1)
                    wait(pe, ht_ready, i, s - 1)
                    for f in range(NF):
                        ins = nc.tensor.transpose(ps[4 + s][:, f * P:(f + 1) * P], hg[s][:, f * P:(f + 1) * P], T["ident"][:, :])
                    ins.then_inc(h_turned.sem, 1)

                def down(i, s):
                    expert = pe.value_load(owner_i[0:1, bass.ds(2 * i + s, 1)], min_val=0, max_val=E - 1)
                    wait(pe, ht_ready, i, s + 1)
                    wait(pe, y_ready, i, s - 1)
                    for f in range(NF):
                        ins = nc.tensor.matmul(ps[6 + s][:, 0:D], ht[s][:, f, :],
                                               w2[:, bass.ds(expert * (NF * D) + f * D, D)], start=f == 0, stop=f == NF - 1)
                    ins.then_inc(down_done.sem, 1)

                last = TILES // 2 - 1
                turn(0, 0)
                up(0, 0)
                turn(0, 1)
                up(0, 1)
                turn_hidden(0, 0)
                turn(1, 0)
                with pe.Fori(1, last) as i:
                    up(i, 0)
                    turn_hidden(i - 1, 1)
                    turn(i, 1)
                    down(i - 1, 0)
                    up(i, 1)
                    turn_hidden(i, 0)
                    turn(i + 1, 0)
                    down(i - 1, 1)
                up(last, 0)
                turn_hidden(last - 1, 1)
                turn(last, 1)
                down(last - 1, 0)
                up(last, 1)
                turn_hidden(last, 0)
                down(last - 1, 1)
                turn_hidden(last, 1)
                down(last, 0)
                down(last, 1)

            @block.scalar
            def _(act):
                for k in (xt_ready, gelu_done, ht_ready):
                    k.credit(act)
                exps(act)

                def keep_rows(i, s):
                    wait(act, x_turned, i, s + 1)
                    wait(act, up_done, i, s - 1)
                    nc.scalar.copy(xt[s][:, :, :].rearrange("p k s -> p (k s)"), ps[s][:, 0:DK * P]).then_inc(xt_ready.sem, 1)

                def gelu(i, s):
                    wait(act, b1_added, i, s + 1)
                    wait(act, h_turned, i, s - 1)
                    nc.scalar.activation(hg[s][:, :], hb[s][:, :], ACT.Gelu_apprx_tanh).then_inc(gelu_done.sem, 1)

                def keep_hidden(i, s):
                    wait(act, h_turned, i, s + 1)
                    wait(act, down_done, i, s - 1)
                    nc.scalar.copy(ht[s][:, :, :].rearrange("p f s -> p (f s)"), ps[4 + s][:, :]).then_inc(ht_ready.sem, 1)

                last = TILES // 2 - 1
                keep_rows(0, 0)
                gelu(0, 0)
                keep_rows(0, 1)
                keep_hidden(0, 0)
                gelu(0, 1)
                keep_rows(1, 0)
                with act.Fori(1, last) as i:
                    keep_hidden(i - 1, 1)
                    gelu(i, 0)
                    keep_rows(i, 1)
                    keep_hidden(i, 0)
                    gelu(i, 1)
                    keep_rows(i + 1, 0)
                keep_hidden(last - 1, 1)
                gelu(last, 0)
                keep_rows(last, 1)
                keep_hidden(last, 0)
                gelu(last, 1)
                keep_hidden(last, 1)

            @block.vector
            def _(dve):
                for k in (b1_added, y_ready):
                    k.credit(dve)
                route(dve)
                dve.wait_ge(w_in, 64)

                def add_b1(i, s):
                    expert = dve.value_load(owner_i[0:1, bass.ds(2 * i + s, 1)], min_val=0, max_val=E - 1)
                    wait(dve, up_done, i, s + 1)
                    wait(dve, gelu_done, i, s - 1)
                    nc.vector.tensor_tensor(hb[s][:, :], ps[2 + s][:, :], b1[:, bass.ds(expert * F1, F1)],
                                            ALU.add).then_inc(b1_added.sem, 1)

                def add_b2(i, s):
                    expert = dve.value_load(owner_i[0:1, bass.ds(2 * i + s, 1)], min_val=0, max_val=E - 1)
                    wait(dve, down_done, i, s + 1)
                    dve.wait_ge(y_out[s], 16 * (i + 1))
                    nc.vector.tensor_tensor(ye[s][:, :], ps[6 + s][:, 0:D], b2[:, bass.ds(expert * D, D)],
                                            ALU.add).then_inc(y_ready.sem, 1)

                for s in range(2):
                    add_b1(0, s)
                with dve.Fori(1, TILES // 2) as i:
                    for s in range(2):
                        add_b1(i, s)
                        add_b2(i - 1, s)
                for s in range(2):
                    add_b2(TILES // 2 - 1, s)
                combine(dve)

    ctx.close()


def gated_two_layers(nc, a, out):
    ctx = ExitStack()

    def sb(name, shape, dt=F32):
        return ctx.enter_context(nc.sbuf_tensor(name, shape, dt))

    T, D_ = {"apart": Apart(nc)}, dict(a)
    for n in (0, 1):
        D_[f"xs{n}"] = nc.dram_tensor(f"rows_in{n}", (DROP0 + 2 * B * S, D), F32, kind="Internal").ap()
        D_[f"ys{n}"] = nc.dram_tensor(f"rows_out{n}", (ROWS, D), F32, kind="Internal").ap()
    T["x"], T["xn"], T["xn_t"] = sb("x", [P, B * D]), sb("xn", [P, B * D]), sb("xn_t", [P, DK, B * S])
    T["ident"], T["ones"], T["earlier"] = sb("ident", [P, P]), sb("ones", [P, P]), sb("earlier", [P, P])
    T["experts"] = sb("experts", [P, E])
    T["wr0"], T["wr1"] = sb("wr0", [P, DK, E]), sb("wr1", [P, DK, E])
    T["bo1"], T["gamma"], T["beta"] = (sb(k, [P, D]) for k in ("bo1", "gamma", "beta"))
    T["stats"] = sb("stats", [P, B * 6])
    T["bq_col"], T["bk_col"], T["bv_out"] = sb("bq_col", [P, 4]), sb("bk_col", [P, 2]), sb("bv_out", [P, 4])
    T["head_rows"] = sb("head_rows", [P, 4])
    gate_in, T["gate"] = sb("gate_in", [P, 4]), sb("gate", [P, 4])
    T["x_in"] = [nc.alloc_semaphore(f"x_in{q}") for q in range(Norm.GROUPS)]
    T["ident_ready"] = nc.alloc_semaphore("ident_ready")
    T["weights_in"] = [nc.alloc_semaphore(f"weights_in{n}") for n in (0, 1)]
    T["w_in"] = [nc.alloc_semaphore(f"expert_in{s}") for s in range(2)]
    small_in, consts, built, built_gate = (nc.alloc_semaphore(k) for k in ("small_in", "consts", "built", "built_gate"))
    zero_ready, padded = nc.alloc_semaphore("zero_ready"), nc.alloc_semaphore("padded")
    D_["cleared"], D_["cleared_value"] = nc.alloc_semaphore("cleared"), 16 * 2 * (ROWS // P // 4)
    w_first = [(f"w{k}0", f"w{k}0") for k in "qkv"]
    n0 = len(w_first) + 4
    T["weights_in_value"] = [16 * n0, 16 * 2]

    def group(*tiles):
        stack = ExitStack()
        for name, shape, dt in tiles:
            T[name] = stack.enter_context(nc.sbuf_tensor(name, shape, dt))
        return stack

    of_second = group(("wq1", [P, DK, 1024], F32), ("wo1", [P, 8, D], F32))
    early = ExitStack()
    T["w1_0"] = [early.enter_context(nc.sbuf_tensor(f"w1_0_{s}", [P, DK, F0], F32)) for s in range(2)]
    T["w2_0"] = [early.enter_context(nc.sbuf_tensor(f"w2_0_{s}", [P, F0 // P, D], F32)) for s in range(2)]
    of_first = group(("wq0", [P, DK, 2 * D], F32), ("wk0", [P, DK, D], F32), ("wv0", [P, DK, D], F32),
                     ("wo0", [P, 4, D], F32), ("bo0", [P, D], F32), ("zero", [P, 4 * D], F32))
    zero = T["zero"]

    def load_later(sp):
        for k in ("wq1", "wo1"):
            sp.dma_start(T[k][:, :, :], D_[k]).then_inc(T["weights_in"][1], 16)
        sp.wait_ge(zero_ready, 3)
        for n in (0, 1):
            X = D_[f"xs{n}"][0:ROWS, :].rearrange("(g p j) d -> g p (j d)", p=P, j=4)
            for g in range(ROWS // P // 4):
                sp.dma_start(X[g, :, :], zero[:, :]).then_inc(D_["cleared"], 16)
        for s in range(2):
            sp.dma_start(T["w1_0"][s][:, :, :], D_["c_fc"][s, :, :, :]).then_inc(T["w_in"][s], 16)
            sp.dma_start(T["w2_0"][s][:, :, :], D_["c_proj"][s, :, :, :]).then_inc(T["w_in"][s], 16)

    T["load_later"] = load_later

    with nc.Block() as block:

        @block.sync
        def _(sp):
            for q in range(Norm.GROUPS):
                c = slice(q * Norm.PER * D, (q + 1) * Norm.PER * D)
                sp.dma_start(T["x"][0:S, c], D_["x"][:, c]).then_inc(T["x_in"][q], 16)
            for name, src in w_first:
                sp.dma_start(T[name][:, :, :], D_[src]).then_inc(T["weights_in"][0], 16)
            sp.wait_ge(zero_ready, 2)
            for j in range(4):
                r = 32 * j + 16 * (j % 2)
                sp.dma_start(T["wo0"][r:r + 16, :, :], D_["wo0"][:, j, :, :]).then_inc(T["weights_in"][0], 16)

        @block.scalar
        def _(act):
            small = [("bq_col", "bq"), ("bk_col", "bk"), ("wr0", "wr0"), ("wr1", "wr1")]
            for name, src in small:
                dst = T[name][:, :, :] if len(T[name].shape) == 3 else T[name][:, :]
                act.dma_start(dst, D_[src]).then_inc(small_in, 16)
            for name in ("bo0", "bo1", "gamma", "beta"):
                act.dma_start(T[name][:, :], D_[name].to_broadcast((P, D))).then_inc(small_in, 16)
            for k in range(4):
                act.dma_start(gate_in[:, k:k + 1], D_["gates"][k:k + 1, :].to_broadcast((P, 1))).then_inc(small_in, 16)
            act.wait_ge(zero_ready, 2)
            for j in range(4):
                r = 32 * j + 16 * (j % 2)
                act.dma_start(T["bv_out"][r:r + 16, :], D_["bv"][:, j, :]).then_inc(small_in, 16)
            act.wait_ge(small_in, 16 * 16)
            nc.scalar.activation(T["gate"][:, :], gate_in[:, :], ACT.Tanh).then_inc(built_gate, 1)

        @block.gpsimd
        def _(pool):
            pool.memset(T["wo0"][:, :, :], 0.0).then_inc(zero_ready, 1)
            pool.memset(T["bv_out"][:, :], 0.0).then_inc(zero_ready, 1)
            pool.memset(zero[:, :], 0.0).then_inc(zero_ready, 1)
            pool.memset(T["ones"][:, :], 1.0).then_inc(consts, 1)
            pool.wait_ge(consts, 1)
            pool.affine_select(out=T["ident"][:, :], in_=T["ones"][:, :], compare_op=ALU.is_equal, fill=0.0, base=0,
                               pattern=[[1, P]], channel_multiplier=-1).then_inc(T["ident_ready"], 1)
            pool.affine_select(out=T["earlier"][:, :], in_=T["ones"][:, :], compare_op=ALU.is_gt, fill=0.0, base=0,
                               pattern=[[1, P]], channel_multiplier=-1).then_inc(consts, 1)
            for k, r in enumerate((slice(0, 64), slice(64, P))):
                pool.affine_select(out=T["head_rows"][r, :], in_=T["ones"][r, 0:4], compare_op=ALU.is_ge, fill=0.0,
                                   base=0, pattern=[[-16, 4]], channel_multiplier=1).then_inc(consts, 1)
                pool.wait_ge(consts, 3 + 2 * k)
                pool.affine_select(out=T["head_rows"][r, :], in_=T["head_rows"][r, :], compare_op=ALU.is_ge, fill=0.0,
                                   base=15, pattern=[[16, 4]], channel_multiplier=-1).then_inc(consts, 1)

        @block.vector
        def _(dve):
            dve.wait_ge(small_in, 16 * 16)
            dve.wait_ge(consts, 6)
            dve.wait_ge(built_gate, 1)
            for k in ("gamma", "beta"):
                nc.vector.tensor_scalar(T[k][:, :], T[k][:, :], T["gate"][:, 2:3], None, ALU.mult).then_inc(built, 1)

    normalise(nc, T, "n0_", False, True)
    attention(nc, Layer(0, 16, 0.25), T, D_)
    of_first.close()
    normalise(nc, T, "n1_", False, False)
    feed_forward(nc, 0, T, D_, out)
    early.close()
    attention(nc, Layer(1, 64, 1.0 / 16), T, D_)
    normalise(nc, T, "n3_", True, False)
    of_second.close()
    feed_forward(nc, 1, T, D_, out)
    ctx.close()


def kernel(**inputs):
    import numpy as np
    import concourse.bacc as bacc
    from concourse import mybir as my
    from concourse.bass_utils import run_bass_kernel_spmd as run

    a = {k: np.asarray(v) for k, v in inputs.items()}

    def rows(w):
        return w.reshape(-1, 128, w.shape[-1]).transpose(1, 0, 2)

    def heads(w):
        return w.transpose(1, 0, 2).reshape(w.shape[1], -1)

    def twice(w):
        return np.repeat(w.reshape(-1, D // 64, 1, 64), 2, axis=2).reshape(-1, 2 * D)

    lay = {
        "x": a["x"].transpose(1, 0, 2).reshape(S, B * D),
        "ctx": rows(a["ctx_1024"].reshape(B * L, D).T),
        "mask0": a["mask_Bx1x1xS2_ik0"].reshape(B, L),
        "mask1": a["mask_BxSxS2_bf0"].transpose(1, 0, 2).reshape(S, B * L),
        "gates": np.stack([a["g_xattn"], a["g_ffn"]], 1).reshape(4, 1),
        "wq0": rows(twice(a["L0_xattn_wq"].T)), "wk0": rows(a["L0_xattn_wk"].T), "wv0": rows(a["L0_xattn_wv"].T),
        "wo0": a["L0_xattn_wo"].T.reshape(4, 4, 16, D).transpose(2, 1, 0, 3),
        "bq": twice(a["L0_xattn_bq"].reshape(1, D)).reshape(4, P).T, "bk": a["L0_xattn_bk"].reshape(2, 128).T,
        "bv": a["L0_xattn_bv"].reshape(4, 4, 16).transpose(2, 1, 0),
        "bo0": a["L0_xattn_bo"].reshape(1, D), "bo1": a["L1_xattn_b_o"].reshape(1, D),
        "gamma": a["L1_xattn_gamma"].reshape(1, D), "beta": a["L1_xattn_beta"].reshape(1, D),
        "wr0": rows(a["L0_ffn_w_g"]), "wr1": rows(a["L1_ffn_routing_weights"]),
        "c_fc": a["L0_ffn_c_fc"].reshape(E, DK, 128, F0).transpose(0, 2, 1, 3),
        "c_proj": a["L0_ffn_c_proj"].reshape(E, F0 // 128, 128, D).transpose(0, 2, 1, 3),
        "wq1": rows(heads(a["L1_xattn_w_qs"])), "wk1": rows(heads(a["L1_xattn_w_ks"])),
        "wv1": rows(heads(a["L1_xattn_w_vs"])), "wo1": rows(a["L1_xattn_W_o"].T),
        "W1": a["L1_ffn_W1"].reshape(E, DK, 128, F1).transpose(2, 0, 1, 3).reshape(128, -1),
        "W2": a["L1_ffn_W2"].reshape(E, F1 // 128, 128, D).transpose(2, 0, 1, 3).reshape(128, -1),
        "b1": a["L1_ffn_b1"].reshape(1, E * F1), "b2": a["L1_ffn_b2"].reshape(1, E * D),
    }
    nc = bacc.Bacc("TRN2", target_bir_lowering=False, num_devices=1)
    arrays, dram = {}, {}
    for name, v in lay.items():
        v = np.ascontiguousarray(v)
        arrays[f"in_{name}"] = v
        dram[name] = nc.dram_tensor(f"in_{name}", v.shape, my.dt.from_np(v.dtype), kind="ExternalInput").ap()
    out = nc.dram_tensor("out", (B, S, D), my.dt.from_np(np.dtype("float32")), kind="ExternalOutput").ap()
    gated_two_layers(nc, dram, out)
    return run(nc, [arrays], core_ids=[0]).results[0]["out"]
```
